# Optimizing a Trainium2 kernel written in Bass

```python
import numpy as np
import jax
import jax.numpy as jnp

def _softmax(x, axis=-1):
    return jax.nn.softmax(x, axis=axis)

def _gelu(x):
    return jax.nn.gelu(x, approximate=True)

def _silu(x):
    return jax.nn.silu(x)

def _sigmoid(x):
    return jax.nn.sigmoid(x)

def _layernorm(x, axis=-1, eps=1e-05):
    m = jnp.mean(x, axis=axis, keepdims=True)
    v = jnp.var(x, axis=axis, keepdims=True)
    return (x - m) / jnp.sqrt(v + eps)

def _scatter_add(tgt, idx, src, axis=0):
    return tgt.at[idx].add(src)

def _segment_sum(src, seg, n):
    return jax.ops.segment_sum(src, seg, n)
kernel_name = 'mk_xattn_ffn_d2_seqx_r8_260b86'

def setup_inputs(seed: int=0):
    np.random.seed(seed)
    _w = jnp.asarray

    def _rec_inputs():
        import jax
        import jax.numpy as jnp
        _rk = jax.random.key(seed)
        x = 4.136e-05 + 0.9999 * jax.random.normal(jax.random.fold_in(_rk, 1), (4, 256, 256), jnp.float32)
        _lenS = 256 - jax.random.randint(jax.random.fold_in(_rk, 7), (4,), 0, max(1, 256 // 4) + 1, jnp.int32)
        _lenS2 = 256 - jax.random.randint(jax.random.fold_in(_rk, 8), (4,), 0, max(1, 256 // 4) + 1, jnp.int32)
        _ctx_1024P = jax.random.normal(jax.random.fold_in(_rk, 11), (4, 16, 128), jnp.float32)
        _ctx_1024c = jax.random.dirichlet(jax.random.fold_in(_rk, 511), 0.3 * jnp.ones((16,), jnp.float32), (4, 256))
        _ctx_1024t = jnp.einsum('bsk,bkd->bsd', _ctx_1024c, _ctx_1024P)
        _ctx_1024t = _ctx_1024t * jax.lax.rsqrt(jnp.mean(jnp.square(_ctx_1024t)) + 1e-12) * 0.953939
        ctx_1024 = -0.000292821 + 1.00034 * (_ctx_1024t + 0.3 * jax.random.normal(jax.random.fold_in(_rk, 611), (4, 256, 128), jnp.float32))
        return (x, ctx_1024)
    x, ctx_1024 = _rec_inputs()

    def _L0_xattn_setup():
        import jax, jax.numpy as jnp
        import numpy as np
        import math
        B, L, DM = (2, 256, 128)
        DS, DC, EXP = (16, 4, 2)
        DI = EXP * DM
        DR = math.ceil(DM / 16)
        DT_MIN, DT_MAX, DT_FLOOR = (0.001, 0.1, 0.0001)

        def _ssm_forward(hidden_states, z, in_proj_w, conv_w, conv_b, x_proj_w, dt_proj_w, dt_proj_b, A_log, D):
            b = hidden_states.shape[0]
            x = jnp.einsum('ed,bld->bel', in_proj_w, hidden_states)
            xp = jnp.pad(x, ((0, 0), (0, 0), (DC - 1, 0)))
            xc = jax.lax.conv_general_dilated(xp, conv_w[:, None, :], window_strides=(1,), padding='VALID', dimension_numbers=('NCH', 'OIH', 'NCH'), feature_group_count=DI)
            u = jax.nn.silu(xc + conv_b[None, :, None])
            x_dbl = jnp.einsum('ke,bel->bkl', x_proj_w, u)
            dt_lo = x_dbl[:, :DR]
            Bm = x_dbl[:, DR:DR + DS]
            Cm = x_dbl[:, DR + DS:]
            delta = jax.nn.softplus(jnp.einsum('er,brl->bel', dt_proj_w, dt_lo) + dt_proj_b[None, :, None])
            A = -jnp.exp(A_log)

            def step(state, xs):
                d_t, B_t, C_t, u_t = xs
                dA = jnp.exp(d_t[..., None] * A)
                state = state * dA + (d_t * u_t)[..., None] * B_t[:, None, :]
                y_t = jnp.einsum('ben,bn->be', state, C_t)
                return (state, y_t)
            xs = (jnp.moveaxis(delta, -1, 0), jnp.moveaxis(Bm, -1, 0), jnp.moveaxis(Cm, -1, 0), jnp.moveaxis(u, -1, 0))
            state0 = jnp.zeros((b, DI, DS), delta.dtype)
            _, ys = jax.lax.scan(step, state0, xs)
            y = jnp.moveaxis(ys, 0, -1)
            y = y + D[None, :, None] * u
            y = y * jax.nn.silu(z)
            return jnp.swapaxes(y, 1, 2)
        key = jax.random.key(seed)
        ks = jax.random.split(key, 8)
        hidden_states = jax.random.normal(ks[0], (B, L, DM), jnp.float32)
        z = jax.random.normal(ks[1], (B, DI, L), jnp.float32)
        in_proj_w = jax.random.normal(ks[2], (DI, DM), jnp.float32) * DM ** (-0.5)
        conv_w = jax.random.normal(ks[3], (DI, DC), jnp.float32) * DC ** (-0.5)
        conv_b = jnp.zeros((DI,), jnp.float32)
        x_proj_w = jax.random.normal(ks[4], (DR + 2 * DS, DI), jnp.float32) * DI ** (-0.5)
        dt_std = DR ** (-0.5)
        dt_proj_w = jax.random.uniform(ks[5], (DI, DR), jnp.float32, -dt_std, dt_std)
        dt = jnp.exp(jax.random.uniform(ks[6], (DI,), jnp.float32) * (math.log(DT_MAX) - math.log(DT_MIN)) + math.log(DT_MIN))
        dt = jnp.clip(dt, DT_FLOOR)
        dt_proj_b = dt + jnp.log(-jnp.expm1(-dt))
        A_log = jnp.log(jnp.broadcast_to(jnp.arange(1, DS + 1, dtype=jnp.float32), (DI, DS)))
        D = jnp.ones((DI,), jnp.float32)
        return dict(hidden_states=hidden_states, z=z, in_proj_w=in_proj_w, conv_w=conv_w, conv_b=conv_b, x_proj_w=x_proj_w, dt_proj_w=dt_proj_w, dt_proj_b=dt_proj_b, A_log=A_log, D=D)
    _L0_xattn_all = _L0_xattn_setup()
    _L0_xattn_in = {k: v for k, v in _L0_xattn_all.items() if k in ('in_proj_w', 'conv_w', 'conv_b', 'x_proj_w', 'dt_proj_w', 'dt_proj_b', 'A_log', 'D')}
    del _L0_xattn_all

    def _L0_ffn_setup():
        import jax, jax.numpy as jnp
        import numpy as np
        B, S, H = (2, 128, 256)
        E, K = (8, 2)
        F = 176
        FS = 704
        NORM_TOPK = False

        def _swiglu(x, wg, wu, wd):
            return jax.nn.silu(x @ wg) * (x @ wu) @ wd
        key = jax.random.key(seed)
        ks = jax.random.split(key, 9)
        s = 0.02
        return {'hidden_states': jax.random.normal(ks[0], (B, S, H), dtype=jnp.float32), 'Wr': jax.random.normal(ks[1], (H, E), dtype=jnp.float32) * s, 'Wg': jax.random.normal(ks[2], (E, H, F), dtype=jnp.float32) * s, 'Wu': jax.random.normal(ks[3], (E, H, F), dtype=jnp.float32) * s, 'Wd': jax.random.normal(ks[4], (E, F, H), dtype=jnp.float32) * s, 'Sg': jax.random.normal(ks[5], (H, FS), dtype=jnp.float32) * s, 'Su': jax.random.normal(ks[6], (H, FS), dtype=jnp.float32) * s, 'Sd': jax.random.normal(ks[7], (FS, H), dtype=jnp.float32) * s, 'Wsg': jax.random.normal(ks[8], (H, 1), dtype=jnp.float32) * s}
    _L0_ffn_all = _L0_ffn_setup()
    _L0_ffn_in = {k: v for k, v in _L0_ffn_all.items() if k in ('Wr', 'Wg', 'Wu', 'Wd', 'Sg', 'Su', 'Sd', 'Wsg')}
    del _L0_ffn_all

    def _L1_xattn_setup():
        import jax, jax.numpy as jnp
        import numpy as np
        EPS = 1e-05

        def rmsnorm(x, g, eps=EPS):
            var = jnp.mean(jnp.square(x), axis=-1, keepdims=True)
            return x * jax.lax.rsqrt(var + eps) * g
        key = jax.random.key(seed)
        ks = jax.random.split(key, 8)
        B, Sq, Skv = (2, 512, 64)
        dim, cdim, H, D = (256, 128, 16, 128)
        inner = H * D
        s = lambda f: 1.0 / np.sqrt(f)
        return {'hidden_states': jax.random.normal(ks[0], (B, Sq, dim), jnp.float32), 'encoder_hidden_states': jax.random.normal(ks[1], (B, Skv, cdim), jnp.float32), 'Wq': jax.random.normal(ks[2], (dim, inner), jnp.float32) * s(dim), 'Wk': jax.random.normal(ks[3], (cdim, inner), jnp.float32) * s(cdim), 'Wv': jax.random.normal(ks[4], (cdim, inner), jnp.float32) * s(cdim), 'Wo': jax.random.normal(ks[5], (inner, dim), jnp.float32) * s(inner), 'gq': jnp.ones((D,), jnp.float32), 'gk': jnp.ones((D,), jnp.float32)}
    _L1_xattn_all = _L1_xattn_setup()
    _L1_xattn_in = {k: v for k, v in _L1_xattn_all.items() if k in ('Wq', 'Wk', 'Wv', 'Wo', 'gq', 'gk')}
    del _L1_xattn_all

    def _L1_ffn_setup():
        import jax, jax.numpy as jnp
        import numpy as np
        DIM = 256
        INTER = 176
        E = 16
        TOPK = 4
        G = 4
        TOPK_G = 2
        N_SHARED = 2
        SHARED_INTER = N_SHARED * INTER
        ROUTE_SCALE = 1.0

        def _moe_forward(x, Wg, W1, W3, W2, Ws1, Ws3, Ws2):
            B, S, D = x.shape
            xt = x.reshape(-1, D)
            T = xt.shape[0]
            scores = jax.nn.softmax(xt @ Wg.T, axis=-1)
            sg = scores.reshape(T, G, E // G)
            group_scores = sg.max(axis=-1)
            gidx = jax.lax.top_k(group_scores, TOPK_G)[1]
            gmask = jax.nn.one_hot(gidx, G, dtype=jnp.float32).sum(axis=1) > 0
            masked = jnp.where(gmask[:, :, None], sg, -jnp.inf).reshape(T, E)
            topi = jax.lax.top_k(masked, TOPK)[1]
            weights = jnp.take_along_axis(scores, topi, axis=1) * ROUTE_SCALE
            combine = jnp.zeros((T, E), xt.dtype).at[jnp.arange(T)[:, None], topi].add(weights)
            h = jax.nn.silu(jnp.einsum('td,eid->eti', xt, W1)) * jnp.einsum('td,eid->eti', xt, W3)
            expert_out = jnp.einsum('eti,edi->etd', h, W2)
            y = jnp.einsum('etd,te->td', expert_out, combine)
            z = jax.nn.silu(xt @ Ws1.T) * (xt @ Ws3.T) @ Ws2.T
            return (y + z).reshape(B, S, D)
        key = jax.random.key(seed)
        ks = jax.random.split(key, 8)
        s = 0.02
        x = jax.random.normal(ks[0], (1, 256, DIM), dtype=jnp.float32)
        Wg = jax.random.normal(ks[1], (E, DIM), dtype=jnp.float32) * s
        W1 = jax.random.normal(ks[2], (E, INTER, DIM), dtype=jnp.float32) * s
        W3 = jax.random.normal(ks[3], (E, INTER, DIM), dtype=jnp.float32) * s
        W2 = jax.random.normal(ks[4], (E, DIM, INTER), dtype=jnp.float32) * s
        Ws1 = jax.random.normal(ks[5], (SHARED_INTER, DIM), dtype=jnp.float32) * s
        Ws3 = jax.random.normal(ks[6], (SHARED_INTER, DIM), dtype=jnp.float32) * s
        Ws2 = jax.random.normal(ks[7], (DIM, SHARED_INTER), dtype=jnp.float32) * s
        return {'x': x, 'Wg': Wg, 'W1': W1, 'W3': W3, 'W2': W2, 'Ws1': Ws1, 'Ws3': Ws3, 'Ws2': Ws2}
    _L1_ffn_all = _L1_ffn_setup()
    _L1_ffn_in = {k: v for k, v in _L1_ffn_all.items() if k in ('Wg', 'W1', 'W3', 'W2', 'Ws1', 'Ws3', 'Ws2')}
    del _L1_ffn_all
    return {'x': x, 'ctx_1024': ctx_1024, 'L0_xattn_in_proj_w': _L0_xattn_in['in_proj_w'], 'L0_xattn_conv_w': _L0_xattn_in['conv_w'], 'L0_xattn_conv_b': _L0_xattn_in['conv_b'], 'L0_xattn_x_proj_w': _L0_xattn_in['x_proj_w'], 'L0_xattn_dt_proj_w': _L0_xattn_in['dt_proj_w'], 'L0_xattn_dt_proj_b': _L0_xattn_in['dt_proj_b'], 'L0_xattn_A_log': _L0_xattn_in['A_log'], 'L0_xattn_D': _L0_xattn_in['D'], 'L0_ffn_Wr': _L0_ffn_in['Wr'], 'L0_ffn_Wg': _L0_ffn_in['Wg'], 'L0_ffn_Wu': _L0_ffn_in['Wu'], 'L0_ffn_Wd': _L0_ffn_in['Wd'], 'L0_ffn_Sg': _L0_ffn_in['Sg'], 'L0_ffn_Su': _L0_ffn_in['Su'], 'L0_ffn_Sd': _L0_ffn_in['Sd'], 'L0_ffn_Wsg': _L0_ffn_in['Wsg'], 'L1_xattn_Wq': _L1_xattn_in['Wq'], 'L1_xattn_Wk': _L1_xattn_in['Wk'], 'L1_xattn_Wv': _L1_xattn_in['Wv'], 'L1_xattn_Wo': _L1_xattn_in['Wo'], 'L1_xattn_gq': _L1_xattn_in['gq'], 'L1_xattn_gk': _L1_xattn_in['gk'], 'L1_ffn_Wg': _L1_ffn_in['Wg'], 'L1_ffn_W1': _L1_ffn_in['W1'], 'L1_ffn_W3': _L1_ffn_in['W3'], 'L1_ffn_W2': _L1_ffn_in['W2'], 'L1_ffn_Ws1': _L1_ffn_in['Ws1'], 'L1_ffn_Ws3': _L1_ffn_in['Ws3'], 'L1_ffn_Ws2': _L1_ffn_in['Ws2']}

def reference(x, ctx_1024, L0_xattn_in_proj_w, L0_xattn_conv_w, L0_xattn_conv_b, L0_xattn_x_proj_w, L0_xattn_dt_proj_w, L0_xattn_dt_proj_b, L0_xattn_A_log, L0_xattn_D, L0_ffn_Wr, L0_ffn_Wg, L0_ffn_Wu, L0_ffn_Wd, L0_ffn_Sg, L0_ffn_Su, L0_ffn_Sd, L0_ffn_Wsg, L1_xattn_Wq, L1_xattn_Wk, L1_xattn_Wv, L1_xattn_Wo, L1_xattn_gq, L1_xattn_gk, L1_ffn_Wg, L1_ffn_W1, L1_ffn_W3, L1_ffn_W2, L1_ffn_Ws1, L1_ffn_Ws3, L1_ffn_Ws2):
    import jax
    import jax.numpy as jnp

    def _L0_xattn_ref(hidden_states, z, in_proj_w, conv_w, conv_b, x_proj_w, dt_proj_w, dt_proj_b, A_log, D):
        import jax, jax.numpy as jnp
        import numpy as np
        import math
        B, L, DM = (2, 256, 128)
        DS, DC, EXP = (16, 4, 2)
        DI = EXP * DM
        DR = math.ceil(DM / 16)
        DT_MIN, DT_MAX, DT_FLOOR = (0.001, 0.1, 0.0001)

        def _ssm_forward(hidden_states, z, in_proj_w, conv_w, conv_b, x_proj_w, dt_proj_w, dt_proj_b, A_log, D):
            b = hidden_states.shape[0]
            x = jnp.einsum('ed,bld->bel', in_proj_w, hidden_states)
            xp = jnp.pad(x, ((0, 0), (0, 0), (DC - 1, 0)))
            xc = jax.lax.conv_general_dilated(xp, conv_w[:, None, :], window_strides=(1,), padding='VALID', dimension_numbers=('NCH', 'OIH', 'NCH'), feature_group_count=DI)
            u = jax.nn.silu(xc + conv_b[None, :, None])
            x_dbl = jnp.einsum('ke,bel->bkl', x_proj_w, u)
            dt_lo = x_dbl[:, :DR]
            Bm = x_dbl[:, DR:DR + DS]
            Cm = x_dbl[:, DR + DS:]
            delta = jax.nn.softplus(jnp.einsum('er,brl->bel', dt_proj_w, dt_lo) + dt_proj_b[None, :, None])
            A = -jnp.exp(A_log)

            def step(state, xs):
                d_t, B_t, C_t, u_t = xs
                dA = jnp.exp(d_t[..., None] * A)
                state = state * dA + (d_t * u_t)[..., None] * B_t[:, None, :]
                y_t = jnp.einsum('ben,bn->be', state, C_t)
                return (state, y_t)
            xs = (jnp.moveaxis(delta, -1, 0), jnp.moveaxis(Bm, -1, 0), jnp.moveaxis(Cm, -1, 0), jnp.moveaxis(u, -1, 0))
            state0 = jnp.zeros((b, DI, DS), delta.dtype)
            _, ys = jax.lax.scan(step, state0, xs)
            y = jnp.moveaxis(ys, 0, -1)
            y = y + D[None, :, None] * u
            y = y * jax.nn.silu(z)
            return jnp.swapaxes(y, 1, 2)
        return _ssm_forward(hidden_states, z, in_proj_w, conv_w, conv_b, x_proj_w, dt_proj_w, dt_proj_b, A_log, D)

    def _L0_ffn_ref(hidden_states, Wr, Wg, Wu, Wd, Sg, Su, Sd, Wsg):
        import jax, jax.numpy as jnp
        import numpy as np
        B, S, H = (2, 128, 256)
        E, K = (8, 2)
        F = 176
        FS = 704
        NORM_TOPK = False

        def _swiglu(x, wg, wu, wd):
            return jax.nn.silu(x @ wg) * (x @ wu) @ wd
        b, s, h = hidden_states.shape
        x = hidden_states.reshape(-1, h)
        router_logits = x @ Wr
        probs = jax.nn.softmax(router_logits.astype(jnp.float32), axis=-1)
        routing_weights, selected = jax.lax.top_k(probs, K)
        if NORM_TOPK:
            routing_weights = routing_weights / routing_weights.sum(-1, keepdims=True)
        routing_weights = routing_weights.astype(x.dtype)
        C = jnp.einsum('tk,tke->te', routing_weights, jax.nn.one_hot(selected, E, dtype=x.dtype))
        expert_out = jax.vmap(lambda wg, wu, wd: _swiglu(x, wg, wu, wd))(Wg, Wu, Wd)
        moe_out = jnp.einsum('te,eth->th', C, expert_out)
        shared = _swiglu(x, Sg, Su, Sd)
        shared = jax.nn.sigmoid(x @ Wsg) * shared
        out = (moe_out + shared).reshape(b, s, h)
        return out

    def _L1_xattn_ref(hidden_states, encoder_hidden_states, Wq, Wk, Wv, Wo, gq, gk):
        import jax, jax.numpy as jnp
        import numpy as np
        EPS = 1e-05

        def rmsnorm(x, g, eps=EPS):
            var = jnp.mean(jnp.square(x), axis=-1, keepdims=True)
            return x * jax.lax.rsqrt(var + eps) * g
        B, Sq, _ = hidden_states.shape
        Skv = encoder_hidden_states.shape[1]
        D = gq.shape[0]
        H = Wq.shape[1] // D
        scale = 1.0 / np.sqrt(D)
        q = (hidden_states @ Wq).reshape(B, Sq, H, D)
        k = (encoder_hidden_states @ Wk).reshape(B, Skv, H, D)
        v = (encoder_hidden_states @ Wv).reshape(B, Skv, H, D)
        q = rmsnorm(q, gq)
        k = rmsnorm(k, gk)
        scores = jnp.einsum('bqhd,bkhd->bhqk', q, k) * scale
        attn = jax.nn.softmax(scores, axis=-1)
        out = jnp.einsum('bhqk,bkhd->bqhd', attn, v)
        out = out.reshape(B, Sq, H * D)
        return out @ Wo

    def _L1_ffn_ref(x, Wg, W1, W3, W2, Ws1, Ws3, Ws2):
        import jax, jax.numpy as jnp
        import numpy as np
        DIM = 256
        INTER = 176
        E = 16
        TOPK = 4
        G = 4
        TOPK_G = 2
        N_SHARED = 2
        SHARED_INTER = N_SHARED * INTER
        ROUTE_SCALE = 1.0

        def _moe_forward(x, Wg, W1, W3, W2, Ws1, Ws3, Ws2):
            B, S, D = x.shape
            xt = x.reshape(-1, D)
            T = xt.shape[0]
            scores = jax.nn.softmax(xt @ Wg.T, axis=-1)
            sg = scores.reshape(T, G, E // G)
            group_scores = sg.max(axis=-1)
            gidx = jax.lax.top_k(group_scores, TOPK_G)[1]
            gmask = jax.nn.one_hot(gidx, G, dtype=jnp.float32).sum(axis=1) > 0
            masked = jnp.where(gmask[:, :, None], sg, -jnp.inf).reshape(T, E)
            topi = jax.lax.top_k(masked, TOPK)[1]
            weights = jnp.take_along_axis(scores, topi, axis=1) * ROUTE_SCALE
            combine = jnp.zeros((T, E), xt.dtype).at[jnp.arange(T)[:, None], topi].add(weights)
            h = jax.nn.silu(jnp.einsum('td,eid->eti', xt, W1)) * jnp.einsum('td,eid->eti', xt, W3)
            expert_out = jnp.einsum('eti,edi->etd', h, W2)
            y = jnp.einsum('etd,te->td', expert_out, combine)
            z = jax.nn.silu(xt @ Ws1.T) * (xt @ Ws3.T) @ Ws2.T
            return (y + z).reshape(B, S, D)
        return _moe_forward(x, Wg, W1, W3, W2, Ws1, Ws3, Ws2)
    x = x + _L0_xattn_ref(ctx_1024, _layernorm(x, axis=-1), L0_xattn_in_proj_w, L0_xattn_conv_w, L0_xattn_conv_b, L0_xattn_x_proj_w, L0_xattn_dt_proj_w, L0_xattn_dt_proj_b, L0_xattn_A_log, L0_xattn_D)
    x = x + _L0_ffn_ref(_layernorm(x, axis=-1), L0_ffn_Wr, L0_ffn_Wg, L0_ffn_Wu, L0_ffn_Wd, L0_ffn_Sg, L0_ffn_Su, L0_ffn_Sd, L0_ffn_Wsg)
    x = x + _L1_xattn_ref(_layernorm(x, axis=-1), ctx_1024, L1_xattn_Wq, L1_xattn_Wk, L1_xattn_Wv, L1_xattn_Wo, L1_xattn_gq, L1_xattn_gk)
    x = x + _L1_ffn_ref(_layernorm(x, axis=-1), L1_ffn_Wg, L1_ffn_W1, L1_ffn_W3, L1_ffn_W2, L1_ffn_Ws1, L1_ffn_Ws3, L1_ffn_Ws2)
    return x

_drawn_inputs = setup_inputs


def setup_inputs(seed=0):
    import zlib

    import numpy as np

    out = dict(_drawn_inputs(seed))
    spreads = {'L0_xattn_conv_b': (0.0, 0.1),
     'L0_xattn_D': (1.0, 0.2),
     'L1_xattn_gq': (1.0, 0.6),
     'L1_xattn_gk': (1.0, 0.6)}
    factors = {'L0_xattn_dt_proj_w': 6.846,
     'L0_xattn_dt_proj_b': 2.826,
     'L0_ffn_Wr': 8.0,
     'L0_ffn_Wg': 8.0,
     'L0_ffn_Wu': 8.0,
     'L0_ffn_Wd': 8.0,
     'L0_ffn_Sg': 4.697,
     'L0_ffn_Su': 4.664,
     'L0_ffn_Sd': 4.659,
     'L0_ffn_Wsg': 8.0,
     'L1_ffn_Wg': 8.0,
     'L1_ffn_W1': 8.0,
     'L1_ffn_W3': 8.0,
     'L1_ffn_W2': 8.0,
     'L1_ffn_Ws1': 3.427,
     'L1_ffn_Ws3': 3.366,
     'L1_ffn_Ws2': 3.364}
    for name, (base, spread) in spreads.items():
        noise = np.random.default_rng([zlib.crc32(name.encode()), seed]).standard_normal(out[name].shape)
        drawn = base * np.exp(spread * noise) if base else spread * noise
        out[name] = jnp.asarray(drawn.astype(out[name].dtype))
    for name, factor in factors.items():
        out[name] = (out[name] * factor).astype(out[name].dtype)
    return out
```

```python
from contextlib import ExitStack

import concourse.bass as bass
from concourse import mybir

P = 128
F32 = mybir.dt.float32
F32R = mybir.dt.float32r
BF16 = mybir.dt.bfloat16
ALU = mybir.AluOpType
ACT = mybir.ActivationFunctionType
AX_X = mybir.AxisListType.X

B, L, DM = 4, 256, 256
T = B * L
NT = T // P
KD = DM // P
HALF = T // 2
TPH = HALF // P
CD = 128
EPS = 1e-5

DI, DS, DC, DR = 256, 16, 4, 8
G = DI // P
LP = L + DC - 1
NBC = 2 * DS

FE = 176
H, HD = 16, 128
HP = 2
NPAIR = H // HP

PC_CONV, PC_CB, PC_DTB, PC_D, PC_A = 0, DC, DC + 1, DC + 2, DC + 3
PC_XP = PC_A + DS
PC_N = PC_XP + DR + NBC


def chunks_of(experts, shared):
    return -(-(experts * FE + shared) // P)


def segments(c, experts):
    found, r = [], 0
    while r < P:
        e = min((c * P + r) // FE, experts)
        end = P if e == experts else min(P, (e + 1) * FE - c * P)
        found.append((r, end, e))
        r = end
    if len(found) == 1:
        found = [(0, P // 2, found[0][2]), (P // 2, P, found[0][2])]
    assert len(found) == 2
    return found


class Shared:
    pass


def product3(pe, out, a, b, first, last):
    pe.matmul(out, a[0], b[0], start=first, stop=False, skip_group_check=True)
    pe.matmul(out, a[0], b[1], start=False, stop=False, skip_group_check=True)
    return pe.matmul(out, a[1], b[0], start=False, stop=last, skip_group_check=True)


def mixer_block(nc, sh, d):
    with ExitStack() as ctx:
        def sb(name, shape, dt=F32):
            return ctx.enter_context(nc.sbuf_tensor("m_" + name, shape, dt))

        def sem(name):
            return ctx.enter_context(nc.semaphore("m_" + name))

        x, ident, bank = sh.x, sh.ident, sh.bank
        w_in = sb("w_in", [P, DI])
        chan = sb("chan", [P, G, PC_N])
        bc_w = sb("bc_w", [P, G, 3 * NBC])
        w_dt = sb("w_dt", [DR, DI])
        sel = sb("sel", [3 * NBC, NBC, P], BF16)
        xpad = sb("xpad", [P, G, B, LP])
        conv = sb("conv", [P, G, T])
        u = sb("u", [P, G, T])
        zs = sb("zs", [P, NT, L])
        zn = sb("zn", [P, NT, L])
        st = sb("st", [P, NT, 6])
        mv = sb("mv", [P, NT, 2])
        vare = sb("vare", [P, NT])
        rstd = sb("rstd", [P, NT])
        bc_hi = sb("bc_hi", [3 * NBC, T], BF16)
        bc_r = sb("bc_r", [3 * NBC, T])
        bc_r2 = sb("bc_r2", [3 * NBC, T])
        bc3 = sb("bc3", [3 * NBC, T], BF16)
        dt_lo = sb("dt_lo", [DR, T])
        an = sb("an", [P, G, DS])
        ae = sb("ae", [P, G, DS])
        dgd = sb("dgd", [P, G, P])
        sp_r = sb("sp_r", [P, G, T])
        sp_e = sb("sp_e", [P, G, T])
        sp_w = sb("sp_w", [P, G, T])
        delta = sb("delta", [P, G, T])
        du = sb("du", [P, G, T])
        b_row = sb("b_row", [P, 2, T])
        da = sb("da", [P, 2, G, B, L])
        dbu = sb("dbu", [P, 2, G, T])
        hst = sb("hst", [P, 2, G, T])
        hc = sb("hc", [P, G, T])
        yz = conv

        ctx_in, w_in_in, chan_in, bc_in, dt_in, x_in, sel_in = (
            sem(n) for n in ("ctx_in", "w_in_in", "chan_in", "bc_in", "dt_in", "x_in", "sel_in"))
        pads, zero_da, xin, xpadded, conv_step, u_ready = (
            sem(n) for n in ("pads", "zero_da", "xin", "xpadded", "conv_step", "u_ready"))
        ln_step, ln_var, ln_rstd, zn_ready, z_ready = (
            sem(n) for n in ("ln_step", "ln_var", "ln_rstd", "zn_ready", "z_ready"))
        bc_psum, dt_psum, bc_step, dt_ready, pre = (
            sem(n) for n in ("bc_psum", "dt_psum", "bc_step", "dt_ready", "pre"))
        sp_act, sp_dve, delta_ready, du_ready, a_exp, a_ready, dg_ready = (
            sem(n) for n in ("sp_act", "sp_dve", "delta_ready", "du_ready", "a_exp", "a_ready", "dg_ready"))
        b_psum, c_psum, b_sb, da_ready, dbu_ready, scanned, hc_ready, y_added, y_final = (
            sem(n) for n in ("b_psum", "c_psum", "b_sb", "da_ready", "dbu_ready", "scanned", "hc_ready",
                             "y_added", "y_final"))
        yz_ready, yT, x_added = (sem(n) for n in ("yz_ready", "yT", "x_added"))

        with nc.Block() as block:
            @block.sync
            def _(sp):
                sp.dma_start(sh.ctxT[:, :], d["ctxT"]).then_inc(ctx_in, 16)
                sp.dma_start(w_in[:, :], d["w_in"]).then_inc(w_in_in, 16)
                sp.dma_start(chan[:, :, :], d["chan"]).then_inc(chan_in, 16)
                for r in range(3):
                    sp.dma_start(bc_w[:, :, r * NBC:(r + 1) * NBC],
                                 d["chan"][:, :, PC_XP + DR:PC_N]).then_inc(bc_in, 16)
                sp.dma_start(x[:, :, :], d["x"].rearrange("(t p) f -> p t f", p=P)).then_inc(x_in, 16)
                sp.dma_start(w_dt[:, :], d["w_dt"]).then_inc(dt_in, 16)
                sp.dma_start(ident[:, :], d["ident"]).then_inc(dt_in, 16)
                sp.dma_start(sel[:, :, :], d["sel"].bitcast(BF16)).then_inc(sel_in, 16)

            @block.tensor
            def _(pe):
                pe.wait_ge(ctx_in, 16)
                pe.wait_ge(w_in_in, 16)
                for g in range(G):
                    for h in range(2):
                        pe.matmul(bank(2 * g + h), w_in[:, g * P:(g + 1) * P],
                                  sh.ctxT[:, h * HALF:(h + 1) * HALF], start=True, stop=True).then_inc(xin, 1)
                pe.wait_ge(u_ready, G)
                pe.wait_ge(bc_in, 48)
                for h in range(2):
                    for g in range(G):
                        mm = pe.matmul(bank(4 + h)[0:3 * NBC, :], bc_w[:, g, :], u[:, g, h * HALF:(h + 1) * HALF],
                                       start=(g == 0), stop=(g == G - 1))
                    mm.then_inc(bc_psum, 1)
                for h in range(2):
                    for g in range(G):
                        mm = pe.matmul(bank(6 + h)[0:DR, :], chan[:, g, PC_XP:PC_XP + DR],
                                       u[:, g, h * HALF:(h + 1) * HALF], start=(g == 0), stop=(g == G - 1))
                    mm.then_inc(dt_psum, 1)
                pe.wait_ge(dt_ready, 2)
                pe.wait_ge(dt_in, 32)
                pe.wait_ge(xpadded, 2 * G)
                for g in range(G):
                    for h in range(2):
                        pe.matmul(bank(2 * g + h), w_dt[:, g * P:(g + 1) * P], dt_lo[:, h * HALF:(h + 1) * HALF],
                                  start=True, stop=True).then_inc(pre, 1)
                pe.wait_ge(dg_ready, 1)
                pe.wait_ge(sp_act, 2 * G)
                for g in range(G):
                    for h in range(2):
                        pe.matmul(bank(2 * g + h), dgd[:, g, :], u[:, g, h * HALF:(h + 1) * HALF],
                                  start=True, stop=False, skip_group_check=True)

                pe.wait_ge(sel_in, 16)
                pe.wait_ge(bc_step, 5)
                def b_rows(n):
                    for h in range(2):
                        mm = pe.matmul(bank(4 + h), sel[:, bass.ds(n, 1), :], bc3[:, h * HALF:(h + 1) * HALF],
                                       start=True, stop=True)
                    mm.then_inc(b_psum, 1)

                def state(n, first=False, last=False):
                    if not first:
                        pe.wait_ge(hc_ready, n * G)
                    for h in range(2):
                        mm = pe.matmul(bank(6 + h), sel[:, bass.ds(n + DS, 1), :], bc3[:, h * HALF:(h + 1) * HALF],
                                       start=True, stop=True)
                    mm.then_inc(c_psum, 1)
                    if not last:
                        pe.wait_ge(b_sb, n + 1)
                        b_rows(n + 1)
                    for g in range(G):
                        pe.wait_ge(hc_ready, n * G + (g + 1))
                        for h in range(2):
                            mm = pe.matmul(bank(2 * g + h), ident[:, :], hc[:, g, h * HALF:(h + 1) * HALF],
                                           start=False, stop=False, skip_group_check=True)
                        mm.then_inc(y_added, 1)

                b_rows(0)
                state(0, first=True)
                with pe.Fori(1, DS - 1) as n:
                    state(n)
                state(DS - 1, last=True)
                for t in range(NT):
                    b, lc = t // 2, t % 2
                    for g in range(G):
                        pe.wait_ge(yz_ready, g + 1)
                        mm = pe.transpose(bank(4 + t // 2)[:, (t % 2) * DM + g * P:(t % 2) * DM + (g + 1) * P],
                                          yz[:, g, b * L + lc * P:b * L + (lc + 1) * P], ident[:, :])
                    mm.then_inc(yT, 1)

            @block.scalar
            def _(act):
                for g in range(G):
                    for h in range(2):
                        act.wait_ge(xin, 2 * g + h + 1)
                        act.activation(xpad[:, g, 2 * h:2 * h + 2, DC - 1:LP],
                                       bank(2 * g + h).rearrange("p (b l) -> p b l", b=2),
                                       ACT.Copy).then_inc(xpadded, 1)
                for g in range(G):
                    act.wait_ge(conv_step, DC * (g + 1))
                    act.activation(u[:, g, :], conv[:, g, :], ACT.Silu, bias=chan[:, g, PC_CB:PC_CB + 1]).then_inc(u_ready, 1)
                act.wait_ge(zn_ready, NT)
                act.activation(zs[:, :, :], zn[:, :, :], ACT.Silu).then_inc(z_ready, 1)
                for h in range(2):
                    act.wait_ge(dt_psum, h + 1)
                    act.activation(dt_lo[:, h * HALF:(h + 1) * HALF], bank(6 + h)[0:DR, :], ACT.Copy).then_inc(dt_ready, 1)
                for g in range(G):
                    act.wait_ge(pre, 2 * g + 2)
                    v = sh.banks(2 * g, 2)
                    bias = chan[:, g, PC_DTB:PC_DTB + 1]
                    act.activation(sp_r[:, g, :], v, ACT.Relu, bias=bias).then_inc(sp_act, 1)
                    act.activation(sp_e[:, g, :], v, ACT.Abs, bias=bias).then_inc(sp_act, 1)
                act.wait_ge(sp_act, 2 * G)
                act.activation(sp_e[:, :, :], sp_e[:, :, :], ACT.Exp, scale=-1.0).then_inc(sp_act, 1)
                act.wait_ge(sp_dve, 1)
                act.activation(delta[:, :, :], sp_w[:, :, :], ACT.Ln).then_inc(sp_act, 1)

                act.activation(ae[:, :, :], chan[:, :, PC_A:PC_A + DS], ACT.Exp).then_inc(a_exp, 1)
                act.wait_ge(a_ready, 1)
                act.wait_ge(delta_ready, 1)
                act.wait_ge(zero_da, 2)
                def state(i, par, first=False):
                    n = i * 2 + par
                    act.wait_ge(b_psum, n + 1)
                    if not first:
                        act.wait_ge(dbu_ready, n * G - G)
                    act.activation(b_row[:, par, :], sh.banks(4, 2), ACT.Copy).then_inc(b_sb, 1)
                    for g in range(G):
                        if not first:
                            act.wait_ge(scanned, n * G - (2 * G - g - 1))
                        act.activation(da[:, par, g, :, 1:L],
                                       delta[:, g, :].rearrange("p (b l) -> p b l", b=B)[:, :, 1:L], ACT.Exp,
                                       scale=an[:, g, bass.ds(n, 1)]).then_inc(da_ready, 1)

                for par in range(2):
                    state(0, par, first=True)
                with act.Fori(1, DS // 2) as i:
                    for par in range(2):
                        state(i, par)

            @block.gpsimd
            def _(pool):
                pool.wait_ge(ln_var, 1)
                pool.tensor_tensor(rstd[:, :], vare[:, :], sh.mhalf[:, 0:NT], ALU.pow).then_inc(ln_rstd, 1)
                pool.wait_ge(du_ready, 1)

                def state(i, par, first=False):
                    n = i * 2 + par
                    pool.wait_ge(b_sb, n + 1)
                    for g in range(G):
                        if not first:
                            pool.wait_ge(scanned, n * G - (2 * G - g - 1))
                        pool.tensor_tensor(dbu[:, par, g, :], du[:, g, :], b_row[:, par, :], ALU.mult).then_inc(dbu_ready, 1)

                for par in range(2):
                    state(0, par, first=True)
                with pool.Fori(1, DS // 2) as i:
                    for par in range(2):
                        state(i, par)

            @block.vector
            def _(dve):
                dve.memset(sh.mhalf[:, :], -0.5).then_inc(pads, 1)
                dve.memset(xpad[:, :, :, 0:DC - 1], 0.0).then_inc(pads, 1)
                for n in range(2):
                    dve.memset(da[:, n, :, :, 0:1], 0.0).then_inc(zero_da, 1)
                dve.wait_ge(x_in, 16)
                for t in range(NT):
                    dve.bn_stats(st[:, t, :], x[:, t, :]).then_inc(ln_step, 1)
                for t in range(NT):
                    dve.wait_ge(ln_step, t + 1)
                    dve.bn_aggr(mv[:, t, :], st[:, t, :]).then_inc(ln_step, 1)
                dve.wait_ge(ln_step, 2 * NT)
                dve.wait_ge(pads, 2)
                dve.tensor_scalar(vare[:, :], mv[:, :, 1], EPS, None, ALU.add).then_inc(ln_var, 1)

                def tap(g, j):
                    src = xpad[:, g, :, j:j + L]
                    out = conv[:, g, :].rearrange("p (b l) -> p b l", b=B)
                    w = chan[:, g, PC_CONV + j:PC_CONV + j + 1]
                    if j == 0:
                        dve.tensor_scalar(out, src, w, None, ALU.mult).then_inc(conv_step, 1)
                    else:
                        dve.wait_ge(conv_step, DC * g + j)
                        dve.scalar_tensor_tensor(out, src, w, out, ALU.mult, ALU.add).then_inc(conv_step, 1)

                dve.wait_ge(chan_in, 16)
                for g in range(G):
                    dve.wait_ge(xpadded, 2 * g + 2)
                    for j in range(DC):
                        tap(g, j)
                dve.wait_ge(ln_rstd, 1)
                for t in range(NT):
                    dve.tensor_scalar(zn[:, t, :], x[:, t, :], mv[:, t, 0:1], rstd[:, t:t + 1],
                                      ALU.subtract, ALU.mult).then_inc(zn_ready, 1)
                dve.wait_ge(dt_in, 32)
                for g in range(G):
                    ins = dve.tensor_scalar(dgd[:, g, :], ident[:, :], chan[:, g, PC_D:PC_D + 1], None, ALU.mult)
                ins.then_inc(dg_ready, 1)

                dve.wait_ge(bc_psum, 2)
                v = sh.banks(4, 2)[0:3 * NBC, :]
                dve.tensor_copy(bc_hi[:, :], v).then_inc(bc_step, 1)
                dve.wait_ge(bc_step, 1)
                dve.tensor_tensor(bc_r[:, :], v, bc_hi[:, :], ALU.subtract).then_inc(bc_step, 1)
                dve.wait_ge(bc_step, 2)
                dve.tensor_copy(bc3[:, :], bc_r[:, :]).then_inc(bc_step, 1)
                dve.wait_ge(bc_step, 3)
                dve.tensor_copy(bc3[0:NBC, :], bc_hi[0:NBC, :]).then_inc(bc_step, 1)
                dve.tensor_tensor(bc3[2 * NBC:3 * NBC, :], bc_r[2 * NBC:3 * NBC, :], bc3[2 * NBC:3 * NBC, :],
                                  ALU.subtract).then_inc(bc_step, 1)

                dve.wait_ge(sp_act, 2 * G + 1)
                dve.tensor_scalar(sp_w[:, :, :], sp_e[:, :, :], 1.0, None, ALU.add).then_inc(sp_dve, 1)
                dve.wait_ge(sp_dve, 1)
                dve.scalar_tensor_tensor(sp_e[:, :, :], sp_w[:, :, :], -1.0, sp_e[:, :, :],
                                         ALU.add, ALU.subtract).then_inc(sp_dve, 1)
                dve.wait_ge(sp_dve, 2)
                dve.tensor_tensor(sp_r[:, :, :], sp_r[:, :, :], sp_e[:, :, :], ALU.subtract).then_inc(sp_dve, 1)
                dve.wait_ge(sp_dve, 3)
                dve.wait_ge(sp_act, 2 * G + 2)
                dve.tensor_tensor(delta[:, :, :], delta[:, :, :], sp_r[:, :, :], ALU.add).then_inc(delta_ready, 1)
                dve.wait_ge(a_exp, 1)
                dve.tensor_scalar(an[:, :, :], ae[:, :, :], -1.0, None, ALU.mult).then_inc(a_ready, 1)
                dve.wait_ge(delta_ready, 1)
                dve.wait_ge(u_ready, G)
                dve.tensor_tensor(du[:, :, :], delta[:, :, :], u[:, :, :], ALU.mult).then_inc(du_ready, 1)

                def states(i, first=False):
                    for par in range(2):
                        n = i * 2 * G
                        for g in range(G):
                            dve.wait_ge(da_ready, n + (par * G + g + 1))
                            dve.wait_ge(dbu_ready, n + (par * G + g + 1))
                            dve.tensor_tensor_scan(hst[:, par, g, :], da[:, par, g, :, :].rearrange("p b l -> p (b l)"),
                                                   dbu[:, par, g, :], 0.0, ALU.mult, ALU.add).then_inc(scanned, 1)
                        dve.wait_ge(c_psum, i * 2 + (par + 1))
                        for g in range(G):
                            dve.wait_ge(scanned, n + (par * G + g + 1))
                            if not (first and par == 0):
                                dve.wait_ge(y_added, n + par * G)
                            dve.tensor_tensor(hc[:, g, :], hst[:, par, g, :], sh.banks(6, 2), ALU.mult).then_inc(hc_ready, 1)

                states(0, first=True)
                with dve.Fori(1, DS // 2) as i:
                    states(i)

                dve.wait_ge(z_ready, 1)
                dve.wait_ge(y_added, G * DS)
                for g in range(G):
                    z = zs[:, :, :].rearrange("p (b g) l -> p b g l", g=G)[:, :, g, :]
                    dve.tensor_tensor(yz[:, g, :].rearrange("p (b l) -> p b l", b=B),
                                      sh.banks(2 * g, 2).rearrange("p (b l) -> p b l", b=B),
                                      z, ALU.mult).then_inc(yz_ready, 1)
                for q in range(NT // 2):
                    dve.wait_ge(yT, 2 * q + 2)
                    xs = x[:, 2 * q:2 * q + 2, :].rearrange("p t f -> p (t f)")
                    dve.tensor_tensor(xs, xs, bank(4 + q), ALU.add).then_inc(x_added, 1)


class NormSems:

    def __init__(self, sem):
        self.step, self.var, self.rstd, self.normed, self.turned, self.hi, self.lo, self.full = (
            sem("n_" + n) for n in ("step", "var", "rstd", "normed", "turned", "hi", "lo", "full"))


def norm_vector(dve, sh, s):
    for h in range(2):
        tiles = range(h * TPH, (h + 1) * TPH)
        for t in tiles:
            dve.bn_stats(sh.st[:, t, :], sh.x[:, t, :]).then_inc(s.step, 1)
        for n, t in enumerate(tiles):
            dve.wait_ge(s.step, 2 * TPH * h + n + 1)
            dve.bn_aggr(sh.mv[:, t, :], sh.st[:, t, :]).then_inc(s.step, 1)
        dve.wait_ge(s.step, 2 * TPH * (h + 1))
        dve.tensor_scalar(sh.vare[:, h * TPH:(h + 1) * TPH], sh.mv[:, h * TPH:(h + 1) * TPH, 1], EPS, None,
                          ALU.add).then_inc(s.var, 1)
    for h in range(2):
        dve.wait_ge(s.rstd, h + 1)
        for t in range(h * TPH, (h + 1) * TPH):
            dve.tensor_scalar(sh.xn[:, t, :], sh.x[:, t, :], sh.mv[:, t, 0:1], sh.rstd[:, t:t + 1],
                              ALU.subtract, ALU.mult).then_inc(s.normed, 1)


def norm_gpsimd(pool, sh, s):
    for h in range(2):
        pool.wait_ge(s.var, h + 1)
        pool.tensor_tensor(sh.rstd[:, h * TPH:(h + 1) * TPH], sh.vare[:, h * TPH:(h + 1) * TPH],
                           sh.mhalf[:, 0:TPH], ALU.pow).then_inc(s.rstd, 1)


def norm_tensor(pe, sh, s):
    for h in range(2):
        for t in range(h * TPH, (h + 1) * TPH):
            pe.wait_ge(s.normed, t + 1)
            for k in range(KD):
                mm = pe.transpose(sh.bank(4 + 2 * h + k)[:, (t % TPH) * P:(t % TPH + 1) * P],
                                  sh.xn[:, t, k * P:(k + 1) * P], sh.ident[:, :])
        mm.then_inc(s.turned, 1)


def turned_view(sh, h):
    return sh.banks(4 + 2 * h, 2).rearrange("p (k t) -> p k t", k=KD)


def norm_scalar(act, sh, s):
    for h in range(2):
        act.wait_ge(s.turned, h + 1)
        act.activation(sh.xT_hi[:, :, h * HALF:(h + 1) * HALF], turned_view(sh, h), ACT.Copy).then_inc(s.hi, 1)


def norm_lo_vector(dve, sh, s, full):
    for h in range(2):
        dve.wait_ge(s.hi, h + 1)
        if full is not None:
            dve.tensor_copy(full[:, :, h * HALF:(h + 1) * HALF], turned_view(sh, h)).then_inc(s.full, 1)
        dve.tensor_tensor(sh.xT_lo[:, :, h * HALF:(h + 1) * HALF], turned_view(sh, h),
                          sh.xT_hi[:, :, h * HALF:(h + 1) * HALF], ALU.subtract).then_inc(s.lo, 1)


GU = 2 * KD * P
WCH = GU + DM
HS = 4


def moe_block(nc, sh, tag, weights, router, scratch, experts, shared, groups, gated, out):
    NC = chunks_of(experts, shared)
    NU = 2 * NC
    ER = experts + (1 if gated else 0)
    E1 = experts + 1
    assert NC % 2 == 1
    with ExitStack() as ctx:
        def sb(name, shape, dt=F32):
            return ctx.enter_context(nc.sbuf_tensor(f"{tag}_{name}", shape, dt))

        def sem(name):
            return ctx.enter_context(nc.semaphore(f"{tag}_{name}"))

        bank, ident, x = sh.bank, sh.ident, sh.x
        raw = sb("raw", [P, 2, WCH])
        gu_hi = sb("gu_hi", [P, 2, GU], F32R)
        gu_lo = sb("gu_lo", [P, 2, GU], F32R)
        dn_hi = sb("dn_hi", [P, 2, DM], F32R)
        dn_lo = sb("dn_lo", [P, 2, DM], F32R)
        comb = sb("comb", [P, 2, T])
        sg = sb("sg", [P, HS, HALF])
        su = sb("su", [P, HS, HALF])
        hid = sb("hid", [P, HS, HALF])
        h_hi = sb("h_hi", [P, HS, HALF], F32R)
        h_lo = sb("h_lo", [P, HS, HALF], F32R)
        xT = sb("xT", [P, KD, T])
        wr = sb("wr", [P, KD, ER])
        lg = sb("lg", [P, NT, ER])
        neg = sb("neg", [P, NT])
        ex = sb("ex", [P, NT, ER])
        den = sb("den", [P, NT])
        pr = sb("pr", [P, NT, 16])
        top = sb("top", [P, NT, 8])
        left = sb("left", [P, NT, 16])
        gs = sb("gs", [P, NT, 16])
        gtop = sb("gtop", [P, NT, 8])
        gleft = sb("gleft", [P, NT, 16])
        gmask = sb("gmask", [P, NT, 4])
        gminus = sb("gminus", [P, NT, 4])
        msk = sb("msk", [P, NT, 16])
        cw = sb("cw", [P, NT, E1])
        cT = sb("cT", [E1, T])

        s = NormSems(sem)
        wr_in, logits, route, ex_ready, cw_ready, cT_psum, cT_ready, cT_out = (
            sem(n) for n in ("wr_in", "logits", "route", "ex_ready", "cw_ready", "cT_psum", "cT_ready", "cT_out"))
        raw_in = [sem(f"raw_in{i}") for i in range(2)]
        comb_in = [sem(f"comb_in{i}") for i in range(2)]
        gu_hi_s, gu_lo_s, dn_hi_s, dn_lo_s = (sem(n) for n in ("gu_hi_done", "gu_lo_done", "dn_hi_done", "dn_lo_done"))
        gate_ps, up_ps, silu_s, su_s, hid_s, h_hi_s, h_lo_s, down_s = (
            sem(n) for n in ("gate_ps", "up_ps", "silu_done", "su_done", "hid_done", "h_hi_done", "h_lo_done", "down_done"))
        x_back, stored = sem("x_back"), sem("stored")

        def gate_bank(half):
            return bank(4 + 2 * half)

        def up_bank(half):
            return bank(5 + 2 * half)

        with nc.Block() as block:
            def broadcast(sp, c):
                if c >= 2:
                    sp.wait_ge(hid_s, 2 * (c - 2) + 2)
                for a, b, e in segments(c, experts):
                    sp.dma_start(comb[a:b, c % 2, :], scratch[e:e + 1, :].to_broadcast([b - a, T])).then_inc(comb_in[c % 2], 16)

            @block.sync
            def _(sp):
                sp.dma_start(wr[:, :, :], router).then_inc(wr_in, 16)
                for c in range(NC):
                    if c >= 2:
                        sp.wait_ge(dn_lo_s, c - 1)
                    sp.dma_start(raw[:, c % 2, :], weights[c]).then_inc(raw_in[c % 2], 16)
                    if c == 1:
                        sp.wait_ge(cT_ready, 2)
                        sp.dma_start(scratch, cT[:, :]).then_inc(cT_out, 16)
                        sp.wait_ge(cT_out, 16)
                        broadcast(sp, 0)
                    if c >= 1:
                        broadcast(sp, c)
                if out is not None:
                    sp.wait_ge(x_back, NT // 2)
                    for q in range(NT // 2):
                        sp.dma_start(out.rearrange("(t p) f -> p t f", p=P)[:, 2 * q:2 * q + 2, :],
                                     x[:, 2 * q:2 * q + 2, :]).then_inc(stored, 16)
                    sp.wait_ge(stored, 16 * (NT // 2))

            @block.tensor
            def _(pe):
                norm_tensor(pe, sh, s)
                pe.wait_ge(wr_in, 16)
                for t in range(NT):
                    pe.wait_ge(s.full, t // TPH + 1)
                    for k in range(KD):
                        mm = pe.matmul(bank(0)[:, t * ER:(t + 1) * ER], xT[:, k, t * P:(t + 1) * P], wr[:, k, :],
                                       start=(k == 0), stop=(k == KD - 1))
                mm.then_inc(logits, 1)

                def gate_up(j, slot, half):
                    tok = slice(half * HALF, (half + 1) * HALF)
                    for what, (dst, done) in enumerate(((gate_bank(half), gate_ps), (up_bank(half), up_ps))):
                        for k in range(KD):
                            w = slice((what * KD + k) * P, (what * KD + k + 1) * P)
                            mm = product3(pe, dst, (gu_hi[:, slot, w], gu_lo[:, slot, w]),
                                          (sh.xT_hi[:, k, tok], sh.xT_lo[:, k, tok]), k == 0, k == KD - 1)
                        mm.then_inc(done, 1)

                def down(slot, hslot, half):
                    for n in range(TPH):
                        t = half * TPH + n
                        tok = slice(n * P, (n + 1) * P)
                        mm = product3(pe, bank(t // 2)[:, (t % 2) * DM:(t % 2 + 1) * DM],
                                      (h_hi[:, hslot, tok], h_lo[:, hslot, tok]),
                                      (dn_hi[:, slot, :], dn_lo[:, slot, :]), False, False)
                    mm.then_inc(down_s, 1)

                pe.wait_ge(s.lo, 2)
                pe.wait_ge(gu_lo_s, 1)
                for half in range(2):
                    gate_up(half, 0, half)
                pe.wait_ge(cw_ready, 1)
                for h in range(2):
                    for n in range(TPH):
                        mm = pe.transpose(bank(1 + h)[0:E1, n * P:(n + 1) * P], cw[:, h * TPH + n, :], ident[:, :])
                    mm.then_inc(cT_psum, 1)
                pe.wait_ge(cT_ready, 2)
                for q in range(NT // 2):
                    pe.matmul(bank(q), ident[:, :], x[:, 2 * q:2 * q + 2, :].rearrange("p t f -> p (t f)"),
                              start=True, stop=False, skip_group_check=True)

                with pe.Fori(0, (NU - 2) // HS) as i:
                    for q in range(HS):
                        half, slot = q % 2, (q // 2 + 1) % 2
                        j = i * HS + q
                        if half == 0:
                            pe.wait_ge(gu_lo_s, i * 2 + q // 2 + 2)
                        pe.wait_ge(silu_s, j + 1)
                        pe.wait_ge(su_s, j + 1)
                        gate_up(None, slot, half)
                        pe.wait_ge(h_lo_s, j + 1)
                        pe.wait_ge(dn_lo_s, i * 2 + q // 2 + 1)
                        down(q // 2, q, half)
                for q in range(2):
                    j = NU - 2 + q
                    pe.wait_ge(h_lo_s, j + 1)
                    pe.wait_ge(dn_lo_s, NC)
                    down((NC - 1) % 2, j % HS, q)

            @block.scalar
            def _(act):
                act.wait_ge(raw_in[0], 16)
                act.activation(gu_hi[:, 0, :], raw[:, 0, 0:GU], ACT.Copy).then_inc(gu_hi_s, 1)
                norm_scalar(act, sh, s)
                act.wait_ge(route, 2)
                act.activation(ex[:, :, 0:experts], ex[:, :, 0:experts], ACT.Exp).then_inc(ex_ready, 1)
                if gated:
                    act.activation(ex[:, :, experts:ER], lg[:, :, experts:ER], ACT.Exp, scale=-1.0).then_inc(ex_ready, 1)

                def copies_out():
                    for h in range(2):
                        act.wait_ge(cT_psum, h + 1)
                        act.activation(cT[:, h * HALF:(h + 1) * HALF], bank(1 + h)[0:E1, :], ACT.Copy).then_inc(cT_ready, 1)

                def chunk(c, par, pair, first=False, last=False):
                    for half in range(2):
                        j = 2 * c + half
                        hs = 2 * par + half
                        act.wait_ge(gate_ps, j + 1)
                        if not first:
                            act.wait_ge(su_s, j - HS + 1)
                        act.activation(sg[:, hs, :], gate_bank(half), ACT.Silu).then_inc(silu_s, 1)
                        if first and par == 0 and half == 1:
                            copies_out()
                        if half == 0:
                            if not last:
                                act.wait_ge(raw_in[(par + 1) % 2], (pair + (par + 1) // 2) * 16 + 16)
                                if not (first and par == 0):
                                    act.wait_ge(up_ps, 2 * c)
                                act.activation(gu_hi[:, (par + 1) % 2, :], raw[:, (par + 1) % 2, 0:GU],
                                               ACT.Copy).then_inc(gu_hi_s, 1)
                            if not first:
                                act.wait_ge(down_s, 2 * c - 2)
                            act.activation(dn_hi[:, par, :], raw[:, par, GU:WCH], ACT.Copy).then_inc(dn_hi_s, 1)
                        if first and par == 0 and half == 0:
                            continue
                        if first and par == 0:
                            hi_part(0, 0, True)
                        hi_part(j, hs, first)

                def hi_part(j, hs, first):
                    act.wait_ge(hid_s, j + 1)
                    if not first:
                        act.wait_ge(down_s, j - HS + 1)
                    act.activation(h_hi[:, hs, :], hid[:, hs, :], ACT.Copy).then_inc(h_hi_s, 1)

                for par in range(2):
                    chunk(par, par, 0, first=True)
                with act.Fori(1, NC // 2) as i:
                    for par in range(2):
                        chunk(2 * i + par, par, i)
                chunk(NC - 1, 0, NC // 2, last=True)
                act.wait_ge(down_s, NU)
                for q in (1, 3):
                    act.activation(x[:, 2 * q:2 * q + 2, :].rearrange("p t f -> p (t f)"), bank(q), ACT.Copy)\
                        .then_inc(x_back, 1)

            @block.gpsimd
            def _(pool):
                norm_gpsimd(pool, sh, s)

                def lo_part(out, whole, hi):
                    return pool.tensor_tensor(out, whole, hi, ALU.subtract)

                pool.wait_ge(gu_hi_s, 1)
                lo_part(gu_lo[:, 0, :], raw[:, 0, 0:GU], gu_hi[:, 0, :]).then_inc(gu_lo_s, 1)

                def chunk(c, par, last=False):
                    if not last:
                        pool.wait_ge(gu_hi_s, c + 2)
                        lo_part(gu_lo[:, (par + 1) % 2, :], raw[:, (par + 1) % 2, 0:GU],
                                gu_hi[:, (par + 1) % 2, :]).then_inc(gu_lo_s, 1)
                    pool.wait_ge(dn_hi_s, c + 1)
                    lo_part(dn_lo[:, par, :], raw[:, par, GU:WCH], dn_hi[:, par, :]).then_inc(dn_lo_s, 1)
                    for half in range(2):
                        pool.wait_ge(h_hi_s, 2 * c + half + 1)
                        hs = 2 * par + half
                        lo_part(h_lo[:, hs, :], hid[:, hs, :], h_hi[:, hs, :]).then_inc(h_lo_s, 1)

                with pool.Fori(0, NC // 2) as i:
                    for par in range(2):
                        chunk(2 * i + par, par)
                chunk(NC - 1, 0, last=True)

            @block.vector
            def _(dve):
                norm_vector(dve, sh, s)
                norm_lo_vector(dve, sh, s, xT)

                steps = [0]

                def step(ins):
                    steps[0] += 1
                    ins.then_inc(route, 1)
                    dve.wait_ge(route, steps[0])

                def spread(v, n):
                    return v.unsqueeze(2).to_broadcast([P, NT, n])

                dve.wait_ge(logits, 1)
                view = bank(0)[:, 0:NT * ER].rearrange("p (t e) -> p t e", t=NT)
                dve.tensor_copy(lg[:, :, :], view)
                step(dve.tensor_reduce(neg[:, :], view[:, :, 0:experts], AX_X, ALU.max))
                step(dve.tensor_tensor(ex[:, :, 0:experts], lg[:, :, 0:experts], spread(neg[:, :], experts), ALU.subtract))
                dve.wait_ge(ex_ready, 2 if gated else 1)
                step(dve.tensor_reduce(den[:, :], ex[:, :, 0:experts], AX_X, ALU.add))
                step(dve.reciprocal(den[:, :], den[:, :]))
                if experts < 16:
                    step(dve.memset(pr[:, :, experts:16], -1.0))
                step(dve.tensor_tensor(pr[:, :, 0:experts], ex[:, :, 0:experts], spread(den[:, :], experts), ALU.mult))
                pick = pr
                k = 2
                if groups:
                    per = experts // groups
                    step(dve.memset(gs[:, :, groups:16], -1.0))
                    step(dve.tensor_reduce(gs[:, :, 0:groups], pr[:, :, :].rearrange("p t (g e) -> p (t g) e", g=groups),
                                           AX_X, ALU.max))
                    for t in range(NT):
                        ins = dve.max(gtop[:, t, :], gs[:, t, :])
                    step(ins)
                    step(dve.memset(gtop[:, :, 2:8], -1.0))
                    for t in range(NT):
                        ins = dve.match_replace(gleft[:, t, :], gtop[:, t, :], gs[:, t, :], -2.0)
                    step(ins)
                    step(dve.tensor_scalar(gmask[:, :, :], gleft[:, :, 0:groups], -2.0, None, ALU.is_equal))
                    step(dve.tensor_scalar(gminus[:, :, :], gmask[:, :, :], -1.0, None, ALU.add))
                    for dst, a, b, op in ((msk, pr, gmask, ALU.mult), (msk, msk, gminus, ALU.add)):
                        v = [y[:, :, :].rearrange("p t (g e) -> p (t g) e", g=groups) for y in (dst, a)]
                        m = b[:, :, :].rearrange("p t g -> p (t g)").unsqueeze(2).to_broadcast([P, NT * groups, per])
                        step(dve.tensor_tensor(v[0], v[1], m, op))
                    pick, k = msk, 4
                for t in range(NT):
                    ins = dve.max(top[:, t, :], pick[:, t, :])
                step(ins)
                step(dve.memset(top[:, :, k:8], -1.0))
                for t in range(NT):
                    ins = dve.match_replace(left[:, t, :], top[:, t, :], pick[:, t, :], -2.0)
                step(ins)
                step(dve.tensor_scalar(left[:, :, :], left[:, :, :], -2.0, None, ALU.is_equal))
                if gated:
                    step(dve.tensor_scalar(ex[:, :, experts:ER], ex[:, :, experts:ER], 1.0, None, ALU.add))
                    step(dve.reciprocal(cw[:, :, experts:E1], ex[:, :, experts:ER]))
                else:
                    step(dve.memset(cw[:, :, experts:E1], 1.0))
                dve.scalar_tensor_tensor(cw[:, :, 0:experts], pick[:, :, 0:experts], 0.0, left[:, :, 0:experts],
                                         ALU.max, ALU.mult).then_inc(cw_ready, 1)

                def gated_up(j, hs, half):
                    dve.wait_ge(silu_s, j + 1)
                    dve.wait_ge(up_ps, j + 1)
                    dve.tensor_tensor(su[:, hs, :], sg[:, hs, :], up_bank(half), ALU.mult).then_inc(su_s, 1)

                def combined(j, par, pair, half, first=False):
                    dve.wait_ge(su_s, j + 1)
                    dve.wait_ge(comb_in[par], pair * 32 + 32)
                    if not first:
                        dve.wait_ge(h_lo_s, j - HS + 1)
                    dve.tensor_tensor(hid[:, 2 * par + half, :], su[:, 2 * par + half, :],
                                      comb[:, par, half * HALF:(half + 1) * HALF], ALU.mult).then_inc(hid_s, 1)

                def pair_of_chunks(i, chunks, first=False):
                    for par in range(chunks):
                        for half in range(2):
                            j = i * HS + 2 * par + half
                            gated_up(j, 2 * par + half, half)
                            combined(j, par, i, half, first)

                pair_of_chunks(0, 2, first=True)
                with dve.Fori(1, NC // 2) as i:
                    pair_of_chunks(i, 2)
                pair_of_chunks(NC // 2, 1)
                dve.wait_ge(down_s, NU)
                for q in (0, 2):
                    dve.tensor_copy(x[:, 2 * q:2 * q + 2, :].rearrange("p t f -> p (t f)"), bank(q)).then_inc(x_back, 1)


QKV = (KD + 2) * HP * HD
WPAIR = QKV + HP * DM
NUA = NPAIR * B
UW = HP * L


def attention_block(nc, sh, d):
    with ExitStack() as ctx:
        def sb(name, shape, dt=F32):
            return ctx.enter_context(nc.sbuf_tensor("a_" + name, shape, dt))

        def sem(name):
            return ctx.enter_context(nc.semaphore("a_" + name))

        bank, ident, x = sh.bank, sh.ident, sh.x
        raw = sb("raw", [P, 2, WPAIR])
        w_hi = sb("w_hi", [P, 2, QKV], F32R)
        w_lo = sb("w_lo", [P, 2, QKV], F32R)
        c_hi = sb("c_hi", [P, T], F32R)
        c_lo = sb("c_lo", [P, T], F32R)
        gq = sb("gq", [P, HD])
        gk = sb("gk", [P, HD])
        gg = sb("gg", [P, HD])
        sq = sb("sq", [P, 2, 2 * UW])
        ss = sb("ss", [P, 2, 8])
        rr = sb("rr", [P, 2, 8])
        qn = sb("qn", [P, 2, UW])
        kn = sb("kn", [P, 2, UW])
        qT = sb("qT", [P, 2, UW])
        kT = sb("kT", [P, 2, UW])
        v = sb("v", [P, 4, UW])
        nmax = sb("nmax", [P, 2, 4])
        rsum = sb("rsum", [P, 2, 4])
        rinv = sb("rinv", [P, 2, 4])
        pe_ = sb("p_exp", [P, 2, 4, L])
        pn = sb("p_norm", [P, 2, 4, L])
        pT = sb("pT", [P, 2, HP, UW])
        oT = sb("oT", [P, 2, UW])

        s = NormSems(sem)
        g_in, gg_ready, c_hi_s, c_lo_s = (sem(n) for n in ("g_in", "gg_ready", "c_hi_done", "c_lo_done"))
        raw_in = [sem(f"raw_in{i}") for i in range(2)]
        w_hi_s, w_lo_s = sem("w_hi_done"), sem("w_lo_done")
        qk_ps, v_ps, sq_s, v_s, ssum, ms, rr_s, qn_s, kn_s = (
            sem(n) for n in ("qk_ps", "v_ps", "sq_done", "v_done", "ssum", "ms_done", "rr_done", "qn_done", "kn_done"))
        turn_ps, qT_s, kT_s, sc_ps, max_s, exp_s, rinv_s, pn_s = (
            sem(n) for n in ("turn_ps", "qT_done", "kT_done", "sc_ps", "max_done", "exp_done", "rinv_done", "pn_done"))
        pT_ps, pT0_s, pT1_s, o_ps, oT_s, out_ps, out_s = (
            sem(n) for n in ("pT_ps", "pT0_done", "pT1_done", "o_ps", "oT_done", "out_ps", "out_done"))

        def steps(eng, body):
            for n in range(ATT_PEEL):
                body(0, n)
            with eng.Fori(0, ATT_LOOPS) as i:
                for n in range(ATT_PEEL, ATT_PEEL + ATT_BODY):
                    body(i, n)
            for n in range(ATT_PEEL, NUA + 1 - ATT_LOOPS * ATT_BODY):
                body(ATT_LOOPS, n)

        Q, K, V, QT, KT, OW = (bank(n) for n in (2, 3, 4, 5, 6, 7))

        with nc.Block() as block:
            @block.sync
            def _(sp):
                sp.dma_start(raw[:, 0, :], d["w_pair"][0]).then_inc(raw_in[0], 16)
                sp.dma_start(gq[:, :], d["gq"].to_broadcast([P, HD])).then_inc(g_in, 16)
                sp.dma_start(gk[:, :], d["gk"].to_broadcast([P, HD])).then_inc(g_in, 16)
                sp.dma_start(raw[:, 1, :], d["w_pair"][1]).then_inc(raw_in[1], 16)
                for p in range(2, NPAIR):
                    sp.wait_ge(w_lo_s, p - 1)
                    sp.wait_ge(out_ps, B * (p - 1))
                    sp.dma_start(raw[:, p % 2, :], d["w_pair"][p]).then_inc(raw_in[p % 2], 16)

            @block.tensor
            def _(pe):
                norm_tensor(pe, sh, s)

                def project(t, n):
                    slot, b = (n // B) % 2, n % B
                    for which, (dst, base, ks) in enumerate(((Q, 0, KD), (K, KD, 1), (V, KD + 1, 1))):
                        for tile in range(2):
                            tok = slice(b * L + tile * P, b * L + (tile + 1) * P)
                            for k in range(ks):
                                a = (sh.xT_hi[:, k, tok], sh.xT_lo[:, k, tok]) if which == 0 else (c_hi[:, tok], c_lo[:, tok])
                                w = slice((base + k) * HP * HD, (base + k + 1) * HP * HD)
                                mm = product3(pe, dst[:, tile * HP * HD:(tile + 1) * HP * HD], a,
                                              (w_hi[:, slot, w], w_lo[:, slot, w]), k == 0, k == ks - 1)
                        if which:
                            mm.then_inc((qk_ps, v_ps)[which - 1], 1)

                def heads_turned(n):
                    for dst, src in ((QT, qn), (KT, kn)):
                        for hh in range(HP):
                            for tile in range(2):
                                mm = pe.transpose(dst[:, hh * L + tile * P:hh * L + (tile + 1) * P],
                                                  src[:, n % 2, (tile * HP + hh) * HD:(tile * HP + hh + 1) * HD],
                                                  ident[:, :])
                    mm.then_inc(turn_ps, 1)

                def scores(n):
                    for hh in range(HP):
                        for tile in range(2):
                            mm = pe.matmul(bank(hh)[:, tile * L:(tile + 1) * L],
                                           qT[:, n % 2, hh * L + tile * P:hh * L + (tile + 1) * P],
                                           kT[:, n % 2, hh * L:(hh + 1) * L], start=True, stop=True)
                        mm.then_inc(sc_ps, 1)

                def probabilities_turned(t, n):
                    for hh in range(HP):
                        pe.wait_ge(pn_s, HP * t + hh + 1)
                        for kt in range(2):
                            for tile in range(2):
                                mm = pe.transpose(bank(hh)[:, kt * L + tile * P:kt * L + (tile + 1) * P],
                                                  pn[:, n % 2, 2 * hh + tile, kt * P:(kt + 1) * P], ident[:, :])
                        mm.then_inc(pT_ps, 1)

                def values(n):
                    for hh in range(HP):
                        for kt in range(2):
                            mm = pe.matmul(OW[:, hh * L:(hh + 1) * L],
                                           v[:, n % 4, (kt * HP + hh) * HD:(kt * HP + hh + 1) * HD],
                                           pT[:, n % 2, hh, kt * L:(kt + 1) * L], start=(kt == 0), stop=(kt == 1))
                    mm.then_inc(o_ps, 1)

                def output(n):
                    slot = (n // B) % 2
                    for tile in range(2):
                        for hh in range(HP):
                            mm = pe.matmul(OW[:, tile * DM:(tile + 1) * DM],
                                           oT[:, n % 2, hh * L + tile * P:hh * L + (tile + 1) * P],
                                           raw[:, slot, QKV + hh * DM:QKV + (hh + 1) * DM],
                                           start=(hh == 0), stop=(hh == HP - 1))
                    mm.then_inc(out_ps, 1)

                def step(i, n):
                    t = i * ATT_BODY + n
                    static = isinstance(i, int)
                    first, last = static and t < 2, static and t > NUA - 3
                    end = static and t == NUA
                    if not end:
                        pe.wait_ge(qT_s, t + 1)
                        pe.wait_ge(kT_s, t + 1)
                        if not (static and t == 0):
                            pe.wait_ge(pT0_s, t)
                            pe.wait_ge(pT1_s, t)
                        scores(n)
                    if not last:
                        if n % B == 2:
                            pe.wait_ge(w_lo_s, i * 2 + ((n + 2) // B + 1))
                        pe.wait_ge(qn_s, t + 2)
                        pe.wait_ge(kn_s, t + 2)
                        pe.wait_ge(v_s, t + 2)
                        project(t, n + 2)
                    if not (static and t == 0):
                        pe.wait_ge(pT0_s, t)
                        pe.wait_ge(pT1_s, t)
                        pe.wait_ge(v_s, t)
                        if not first:
                            pe.wait_ge(out_s, t - 1)
                        values(n - 1)
                    if not (static and t >= NUA - 1):
                        pe.wait_ge(qn_s, t + 2)
                        pe.wait_ge(kn_s, t + 2)
                        heads_turned(n + 1)
                    if not end:
                        probabilities_turned(t, n)
                    if not (static and t == 0):
                        pe.wait_ge(oT_s, t)
                        output(n - 1)

                pe.wait_ge(s.lo, 2)
                pe.wait_ge(c_lo_s, 1)
                pe.wait_ge(w_lo_s, 1)
                project(0, 0)
                pe.wait_ge(qn_s, 1)
                pe.wait_ge(kn_s, 1)
                pe.wait_ge(v_s, 1)
                project(1, 1)
                heads_turned(0)
                steps(pe, step)

            @block.scalar
            def _(act):
                act.wait_ge(raw_in[0], 16)
                act.activation(w_hi[:, 0, :], raw[:, 0, 0:QKV], ACT.Copy).then_inc(w_hi_s, 1)
                act.activation(c_hi[:, :], sh.ctxT[:, :], ACT.Copy).then_inc(c_hi_s, 1)
                norm_scalar(act, sh, s)

                def squares(t, n):
                    act.wait_ge(qk_ps, t + 1)
                    if not (isinstance(t, int) and t < 2):
                        act.wait_ge(ssum, t - 1)
                    act.activation(sq[:, n % 2, :], sh.banks(2, 2), ACT.Square).then_inc(sq_s, 1)
                    act.wait_ge(v_ps, t + 1)
                    if not (isinstance(t, int) and t < 4):
                        act.wait_ge(o_ps, t - 3)
                    act.activation(v[:, n % 4, :], V, ACT.Copy).then_inc(v_s, 1)

                def turned(t, n):
                    act.wait_ge(turn_ps, t + 1)
                    if not (isinstance(t, int) and t < 2):
                        act.wait_ge(sc_ps, HP * (t - 1))
                    act.activation(qT[:, n % 2, :], QT, ACT.Copy).then_inc(qT_s, 1)
                    act.activation(kT[:, n % 2, :], KT, ACT.Copy).then_inc(kT_s, 1)

                def softmax(t, n):
                    for hh in range(HP):
                        act.wait_ge(max_s, HP * t + hh + 1)
                        if not (isinstance(t, int) and t < 2):
                            act.wait_ge(pn_s, HP * (t - 2) + hh + 1)
                        for tile in range(2):
                            m = 2 * hh + tile
                            ins = act.activation(pe_[:, n % 2, m, :], bank(hh)[:, tile * L:(tile + 1) * L], ACT.Exp,
                                                 bias=nmax[:, n % 2, m:m + 1], accum_out=rsum[:, n % 2, m:m + 1])
                        ins.then_inc(exp_s, 1)

                def probabilities(t, n):
                    act.wait_ge(pT_ps, HP * t + 2)
                    if not (isinstance(t, int) and t < 2):
                        act.wait_ge(o_ps, t - 1)
                    act.activation(pT[:, n % 2, 1, :], bank(1), ACT.Copy).then_inc(pT1_s, 1)

                squares(0, 0)
                squares(1, 1)
                turned(0, 0)

                def step(i, n):
                    t = i * ATT_BODY + n
                    static = isinstance(i, int)
                    if static and t >= NUA:
                        return
                    softmax(t, n)
                    if not (static and t > NUA - 3):
                        squares(t + 2, n + 2)
                        if n % B == 1 and not (static and t > NUA - B):
                            ahead = n // B + 1
                            slot = ahead % 2
                            act.wait_ge(raw_in[slot], i * 16 + (ahead // 2 * 16 + 16))
                            if not (static and t < B):
                                act.wait_ge(v_ps, t - n % B)
                            act.activation(w_hi[:, slot, :], raw[:, slot, 0:QKV], ACT.Copy).then_inc(w_hi_s, 1)
                    if not (static and t >= NUA - 1):
                        turned(t + 1, n + 1)
                    probabilities(t, n)

                steps(act, step)

            @block.gpsimd
            def _(pool):
                norm_gpsimd(pool, sh, s)
                pool.wait_ge(w_hi_s, 1)
                pool.tensor_tensor(w_lo[:, 0, :], raw[:, 0, 0:QKV], w_hi[:, 0, :], ALU.subtract).then_inc(w_lo_s, 1)
                pool.wait_ge(c_hi_s, 1)
                pool.tensor_tensor(c_lo[:, :], sh.ctxT[:, :], c_hi[:, :], ALU.subtract).then_inc(c_lo_s, 1)

                def rms(t, n):
                    pool.wait_ge(ms, t + 1)
                    if not (isinstance(t, int) and t < 2):
                        pool.wait_ge(kn_s, t - 1)
                    pool.tensor_tensor(rr[:, n % 2, :], ss[:, n % 2, :], sh.mhalf[:, 0:8], ALU.pow).then_inc(rr_s, 1)

                rms(0, 0)
                rms(1, 1)

                def step(i, n):
                    t = i * ATT_BODY + n
                    static = isinstance(i, int)
                    if static and t > NUA - 3:
                        return
                    rms(t + 2, n + 2)
                    if n % B == 1 and not (static and t > NUA - B):
                        slot = (n // B + 1) % 2
                        pool.wait_ge(w_hi_s, i * 2 + (n // B + 2))
                        pool.tensor_tensor(w_lo[:, slot, :], raw[:, slot, 0:QKV], w_hi[:, slot, :], ALU.subtract)\
                            .then_inc(w_lo_s, 1)

                steps(pool, step)

            @block.vector
            def _(dve):
                norm_vector(dve, sh, s)
                norm_lo_vector(dve, sh, s, None)
                dve.wait_ge(g_in, 32)
                dve.scalar_tensor_tensor(gg[:, :], gq[:, :], HD ** -0.5, gk[:, :], ALU.mult, ALU.mult).then_inc(gg_ready, 1)

                def mean_squares(t, n):
                    dve.wait_ge(sq_s, t + 1)
                    dve.tensor_reduce(ss[:, n % 2, :], sq[:, n % 2, :].rearrange("p (a f) -> p a f", f=HD), AX_X,
                                      ALU.add).then_inc(ssum, 1)
                    dve.wait_ge(ssum, t + 1)
                    dve.tensor_scalar(ss[:, n % 2, :], ss[:, n % 2, :], 1.0 / HD, EPS, ALU.mult, ALU.add).then_inc(ms, 1)

                def normed(t, n):
                    dve.wait_ge(rr_s, t + 1)
                    if not (isinstance(t, int) and t < 2):
                        dve.wait_ge(turn_ps, t - 1)
                    dve.tensor_tensor(qn[:, n % 2, :].rearrange("p (a f) -> p a f", f=HD),
                                      Q.rearrange("p (a f) -> p a f", f=HD),
                                      rr[:, n % 2, 0:4].unsqueeze(2).to_broadcast([P, 4, HD]), ALU.mult).then_inc(qn_s, 1)
                    for a in range(4):
                        ins = dve.scalar_tensor_tensor(kn[:, n % 2, a * HD:(a + 1) * HD], K[:, a * HD:(a + 1) * HD],
                                                       rr[:, n % 2, 4 + a:5 + a], gg[:, :], ALU.mult, ALU.mult)
                    ins.then_inc(kn_s, 1)

                def maxima(t, n):
                    for hh in range(HP):
                        dve.wait_ge(sc_ps, HP * t + hh + 1)
                        dve.tensor_reduce(nmax[:, n % 2, 2 * hh:2 * hh + 2], bank(hh).rearrange("p (a k) -> p a k", k=L),
                                          AX_X, ALU.max, negate=True).then_inc(max_s, 1)

                def normalised(t, n, hh):
                    dve.wait_ge(exp_s, HP * t + hh + 1)
                    dve.reciprocal(rinv[:, n % 2, 2 * hh:2 * hh + 2], rsum[:, n % 2, 2 * hh:2 * hh + 2]).then_inc(rinv_s, 1)
                    dve.wait_ge(rinv_s, HP * t + hh + 1)
                    for m in range(2 * hh, 2 * hh + 2):
                        ins = dve.tensor_scalar(pn[:, n % 2, m, :], pe_[:, n % 2, m, :], rinv[:, n % 2, m:m + 1], None, ALU.mult)
                    ins.then_inc(pn_s, 1)

                def first_probabilities(t, n):
                    dve.wait_ge(pT_ps, HP * t + 1)
                    if not (isinstance(t, int) and t < 2):
                        dve.wait_ge(o_ps, t - 1)
                    dve.tensor_copy(pT[:, n % 2, 0, :], bank(0)).then_inc(pT0_s, 1)

                def values_out(t, n):
                    dve.wait_ge(o_ps, t + 1)
                    if not (isinstance(t, int) and t < 2):
                        dve.wait_ge(out_ps, t - 1)
                    dve.tensor_copy(oT[:, n % 2, :], OW).then_inc(oT_s, 1)

                def residual(t, n):
                    b = n % B
                    dve.wait_ge(out_ps, t + 1)
                    xs = x[:, 2 * b:2 * b + 2, :].rearrange("p t f -> p (t f)")
                    dve.tensor_tensor(xs, xs, OW, ALU.add).then_inc(out_s, 1)

                dve.wait_ge(gg_ready, 1)
                for t in range(2):
                    mean_squares(t, t)
                    normed(t, t)

                def step(i, n):
                    t = i * ATT_BODY + n
                    static = isinstance(i, int)
                    if static and t > NUA:
                        return
                    if not (static and t >= NUA):
                        maxima(t, n)
                        for hh in range(HP):
                            normalised(t, n, hh)
                    if not (static and t == 0):
                        values_out(t - 1, n - 1)
                    if not (static and t > NUA - 3):
                        mean_squares(t + 2, n + 2)
                    if not (static and t >= NUA):
                        first_probabilities(t, n)
                    if not (static and t == 0):
                        residual(t - 1, n - 1)
                    if not (static and t > NUA - 3):
                        normed(t + 2, n + 2)

                steps(dve, step)


ATT_BODY = 2 * B
ATT_PEEL = 4
ATT_LOOPS = 3


def build(nc, d, out, stages=4):
    with ExitStack() as ctx:
        sh = Shared()

        def sb(name, shape, dt=F32):
            return ctx.enter_context(nc.sbuf_tensor(name, shape, dt))

        psum = ctx.enter_context(nc.psum_tensor("psum", [P, 8, 512], F32))
        sh.bank = lambda n: psum[:, n, :]
        sh.banks = lambda n, k: psum[:, n:n + k, :].rearrange("p b n -> p (b n)")
        sh.x = sb("x", [P, NT, DM])
        sh.xn = sb("xn", [P, NT, DM])
        sh.ident = sb("ident", [P, P])
        sh.ctxT = sb("ctxT", [P, T])
        sh.mhalf = sb("mhalf", [P, 8])
        sh.st = sb("st", [P, NT, 6])
        sh.mv = sb("mv", [P, NT, 2])
        sh.vare = sb("vare", [P, NT])
        sh.rstd = sb("rstd", [P, NT])

        mixer_block(nc, sh, d)
        sh.xT_hi = sb("xT_hi", [P, KD, T], F32R)
        sh.xT_lo = sb("xT_lo", [P, KD, T], F32R)
        if stages >= 2:
            moe_block(nc, sh, "f0", d["moe0"], d["route0"], d["scratch0"], 8, 704, 0, True, out if stages == 2 else None)
        if stages >= 3:
            attention_block(nc, sh, d)
        if stages >= 4:
            moe_block(nc, sh, "f1", d["moe1"], d["route1"], d["scratch1"], 16, 352, 4, False, out)
        if stages in (1, 3):
            stored = ctx.enter_context(nc.semaphore("stored"))
            with nc.Block() as block:
                @block.sync
                def _(sp):
                    sp.dma_start(out.rearrange("(t p) f -> p t f", p=P), sh.x[:, :, :]).then_inc(stored, 16)
                    sp.wait_ge(stored, 16)


def layout(a):
    import numpy as np

    c = np.ascontiguousarray
    a = {k: np.asarray(v) for k, v in a.items()}

    def channels(v):
        return v.reshape(G, P, -1).transpose(1, 0, 2)

    def moe(gate, up, down, n):
        pad = n * P - gate.shape[1]
        gate, up = (np.pad(w, ((0, 0), (0, pad))).reshape(KD, P, n, P).transpose(2, 1, 0, 3) for w in (gate, up))
        down = np.pad(down, ((0, pad), (0, 0))).reshape(n, P, DM)
        return c(np.concatenate([gate.reshape(n, P, -1), up.reshape(n, P, -1), down], axis=2))

    def wide(w, shared):
        return np.concatenate([w.transpose(1, 0, 2).reshape(DM, -1), shared], axis=1)

    m = "L0_xattn_"
    f = "L0_ffn_"
    q = "L1_xattn_"
    e = "L1_ffn_"
    out = {
        "ctxT": c(a["ctx_1024"].reshape(T, CD).T),
        "x": c(a["x"].reshape(T, DM)),
        "w_in": c(a[m + "in_proj_w"].T),
        "w_dt": c(a[m + "dt_proj_w"].T),
        "chan": c(channels(np.concatenate([
            a[m + "conv_w"], a[m + "conv_b"][:, None], a[m + "dt_proj_b"][:, None], a[m + "D"][:, None],
            a[m + "A_log"], a[m + "x_proj_w"].T], axis=1))),
        "ident": np.eye(P, dtype=np.float32),
        "moe0": moe(wide(a[f + "Wg"], a[f + "Sg"]), wide(a[f + "Wu"], a[f + "Su"]),
                    np.concatenate([a[f + "Wd"].reshape(-1, DM), a[f + "Sd"]], axis=0), chunks_of(8, 704)),
        "route0": c(np.concatenate([a[f + "Wr"], a[f + "Wsg"]], axis=1).reshape(KD, P, -1).transpose(1, 0, 2)),
        "moe1": moe(wide(a[e + "W1"].transpose(0, 2, 1), a[e + "Ws1"].T), wide(a[e + "W3"].transpose(0, 2, 1), a[e + "Ws3"].T),
                    np.concatenate([a[e + "W2"].transpose(0, 2, 1).reshape(-1, DM), a[e + "Ws2"].T], axis=0), chunks_of(16, 352)),
        "route1": c(a[e + "Wg"].T.reshape(KD, P, -1).transpose(1, 0, 2)),
        "gq": a[q + "gq"].reshape(1, HD),
        "gk": a[q + "gk"].reshape(1, HD),
    }
    pair = [a[q + "Wq"].reshape(KD, P, NPAIR, HP * HD).transpose(2, 1, 0, 3).reshape(NPAIR, P, -1),
            a[q + "Wk"].reshape(P, NPAIR, HP * HD).transpose(1, 0, 2),
            a[q + "Wv"].reshape(P, NPAIR, HP * HD).transpose(1, 0, 2),
            a[q + "Wo"].reshape(NPAIR, HP, HD, DM).transpose(0, 2, 1, 3).reshape(NPAIR, HD, -1)]
    out["w_pair"] = c(np.concatenate(pair, axis=2))
    sel = np.zeros((3, NBC, NBC, P), np.uint16)
    for r in range(NBC):
        sel[:, r, r, :] = 0x3F80
    out["sel"] = c(sel.reshape(3 * NBC, NBC, P))
    return out


def program(nc, arrays, stages=4):
    d = {name: nc.dram_tensor(f"in_{name}", v.shape, mybir.dt.from_np(v.dtype), kind="ExternalInput").ap()
         for name, v in arrays.items()}
    d["scratch0"] = nc.dram_tensor("scratch0", (9, T), F32).ap()
    d["scratch1"] = nc.dram_tensor("scratch1", (17, T), F32).ap()
    out = nc.dram_tensor("out", (T, DM), F32, kind="ExternalOutput").ap()
    build(nc, d, out, stages)


def kernel(**inputs):
    import concourse.bacc as bacc
    from concourse.bass_utils import run_bass_kernel_spmd

    arrays = layout(inputs)
    nc = bacc.Bacc("TRN2", target_bir_lowering=False, num_devices=1)
    program(nc, arrays)
    r = run_bass_kernel_spmd(nc, [{f"in_{k}": v for k, v in arrays.items()}], core_ids=[0])
    return r.results[0]["out"].reshape(B, L, DM)
```

```python
from contextlib import ExitStack

import concourse.bass as bass
from concourse import mybir

P = 128
F32 = mybir.dt.float32
F32R = mybir.dt.float32r
BF16 = mybir.dt.bfloat16
ALU = mybir.AluOpType
ACT = mybir.ActivationFunctionType
AX_X = mybir.AxisListType.X

B, L, DM = 4, 256, 256
T = B * L
NT = T // P
KD = DM // P
HALF = T // 2
TPH = HALF // P
CD = 128
EPS = 1e-5

DI, DS, DC, DR = 256, 16, 4, 8
G = DI // P
LP = L + DC - 1
NBC = 2 * DS

FE = 176
H, HD = 16, 128
HP = 2
NPAIR = H // HP

PC_CONV, PC_CB, PC_DTB, PC_D, PC_A = 0, DC, DC + 1, DC + 2, DC + 3
PC_XP = PC_A + DS
PC_N = PC_XP + DR + NBC


def chunks_of(experts, shared):
    return -(-(experts * FE + shared) // P)


def segments(c, experts):
    found, r = [], 0
    while r < P:
        e = min((c * P + r) // FE, experts)
        end = P if e == experts else min(P, (e + 1) * FE - c * P)
        found.append((r, end, e))
        r = end
    if len(found) == 1:
        found = [(0, P // 2, found[0][2]), (P // 2, P, found[0][2])]
    assert len(found) == 2
    return found


class Shared:
    pass


def product3(pe, out, a, b, first, last):
    pe.matmul(out, a[0], b[0], start=first, stop=False, skip_group_check=True)
    pe.matmul(out, a[0], b[1], start=False, stop=False, skip_group_check=True)
    return pe.matmul(out, a[1], b[0], start=False, stop=last, skip_group_check=True)


def mixer_block(nc, sh, d):
    with ExitStack() as ctx:
        def sb(name, shape, dt=F32):
            return ctx.enter_context(nc.sbuf_tensor("m_" + name, shape, dt))

        def sem(name):
            return ctx.enter_context(nc.semaphore("m_" + name))

        x, ident, bank = sh.x, sh.ident, sh.bank
        w_in = sb("w_in", [P, DI])
        chan = sb("chan", [P, G, PC_N])
        bc_w = sb("bc_w", [P, G, 3 * NBC])
        w_dt = sb("w_dt", [DR + 1, DI])
        sel = sb("sel", [3 * NBC, NBC, P], BF16)
        xpad = sb("xpad", [P, G, B, LP])
        conv = sb("conv", [P, G, T])
        u = sb("u", [P, G, T])
        zs = sb("zs", [P, NT, L])
        st = sb("st", [P, NT, 6])
        mv = sb("mv", [P, NT, 2])
        vare = sb("vare", [P, NT])
        rstd = sb("rstd", [P, NT])
        nmr = sb("nmr", [P, NT])
        bc_hi = sb("bc_hi", [3 * NBC, T], BF16)
        bc_r = sb("bc_r", [3 * NBC, T])
        bc_r2 = sb("bc_r2", [3 * NBC, T])
        bc3 = sb("bc3", [3 * NBC, T], BF16)
        dt_lo = sb("dt_lo", [DR + 1, T])
        an = sb("an", [P, G, DS])
        ae = sb("ae", [P, G, DS])
        dgd = sb("dgd", [P, G, P])
        sp_r = sb("sp_r", [P, G, T])
        sp_e = sb("sp_e", [P, G, T])
        sp_w = sb("sp_w", [P, G, T])
        delta = sb("delta", [P, G, T])
        du = sb("du", [P, G, T])
        b_row = sb("b_row", [P, 2, T])
        da = sb("da", [P, 2, G, B, L])
        dbu = sb("dbu", [P, 2, G, T])
        hst = sb("hst", [P, 2, G, T])
        hc = (sb("hc", [P, G, T]), sp_r)
        c_row = sp_e
        yz = conv

        ctx_in, w_in_in, chan_in, bc_in, dt_in, x_in, sel_in = (
            sem(n) for n in ("ctx_in", "w_in_in", "chan_in", "bc_in", "dt_in", "x_in", "sel_in"))
        pads, zero_da, xin, xpadded, conv_step, u_ready = (
            sem(n) for n in ("pads", "zero_da", "xin", "xpadded", "conv_step", "u_ready"))
        ln_step, ln_var, ln_rstd, ln_shift, z_ready = (
            sem(n) for n in ("ln_step", "ln_var", "ln_rstd", "ln_shift", "z_ready"))
        bc_psum, dt_psum, bc_step, dt_ready, pre = (
            sem(n) for n in ("bc_psum", "dt_psum", "bc_step", "dt_ready", "pre"))
        sp_abs, sp_exp, sp_w_s, sp_t, sp_r_s, sp_ln = (
            sem(n) for n in ("sp_abs", "sp_exp", "sp_w_done", "sp_t_done", "sp_r_done", "sp_ln"))
        delta_ready, du_ready, a_exp, a_ready, dg_ready = (
            sem(n) for n in ("delta_ready", "du_ready", "a_exp", "a_ready", "dg_ready"))
        b_psum, c_psum, b_sb, c_sb, da_ready, dbu_ready, scanned, hc_ready, y_added = (
            sem(n) for n in ("b_psum", "c_psum", "b_sb", "c_sb", "da_ready", "dbu_ready", "scanned", "hc_ready", "y_added"))
        yz_ready, yT, x_added = (sem(n) for n in ("yz_ready", "yT", "x_added"))

        with nc.Block() as block:
            @block.sync
            def _(sp):
                sp.dma_start(sh.ctxT[:, :], d["ctxT"]).then_inc(ctx_in, 16)
                sp.dma_start(w_in[:, :], d["w_in"]).then_inc(w_in_in, 16)
                sp.dma_start(chan[:, :, :], d["chan"]).then_inc(chan_in, 16)
                for r in range(3):
                    sp.dma_start(bc_w[:, :, r * NBC:(r + 1) * NBC],
                                 d["chan"][:, :, PC_XP + DR:PC_N]).then_inc(bc_in, 16)
                sp.dma_start(x[:, :, :], d["x"].rearrange("(t p) f -> p t f", p=P)).then_inc(x_in, 16)
                sp.dma_start(w_dt[:, :], d["w_dt"]).then_inc(dt_in, 16)
                sp.dma_start(ident[:, :], d["ident"]).then_inc(dt_in, 16)
                sp.dma_start(sel[:, :, :], d["sel"].bitcast(BF16)).then_inc(sel_in, 16)

            @block.tensor
            def _(pe):
                pe.wait_ge(ctx_in, 16)
                pe.wait_ge(w_in_in, 16)
                for g in range(G):
                    for h in range(2):
                        pe.matmul(bank(2 * g + h), w_in[:, g * P:(g + 1) * P],
                                  sh.ctxT[:, h * HALF:(h + 1) * HALF], start=True, stop=True).then_inc(xin, 1)
                pe.wait_ge(bc_in, 48)
                for g in range(G):
                    pe.wait_ge(u_ready, g + 1)
                    for h in range(2):
                        mm = pe.matmul(bank(6 + h)[0:DR, :], chan[:, g, PC_XP:PC_XP + DR],
                                       u[:, g, h * HALF:(h + 1) * HALF], start=(g == 0), stop=(g == G - 1),
                                       skip_group_check=True)
                        if g == G - 1:
                            mm.then_inc(dt_psum, 1)
                    for h in range(2):
                        mm = pe.matmul(bank(4 + h)[0:3 * NBC, :], bc_w[:, g, :], u[:, g, h * HALF:(h + 1) * HALF],
                                       start=(g == 0), stop=(g == G - 1), skip_group_check=True)
                        if g == G - 1:
                            mm.then_inc(bc_psum, 1)
                pe.wait_ge(dt_in, 32)
                pe.wait_ge(xpadded, 2 * G)
                for g in range(G):
                    for h in range(2):
                        pe.wait_ge(dt_ready, h + 1)
                        mm = pe.matmul(bank(2 * g + h), w_dt[:, g * P:(g + 1) * P], dt_lo[:, h * HALF:(h + 1) * HALF],
                                       start=True, stop=True)
                    mm.then_inc(pre, 1)

                def rows(n):
                    for psum, sem_, at in ((4, b_psum, 0), (6, c_psum, DS)):
                        if not (isinstance(n, int) and n == 0):
                            pe.wait_ge((c_sb if at else b_sb), n)
                        for h in range(2):
                            mm = pe.matmul(bank(psum + h), sel[:, bass.ds(n + at, 1), :], bc3[:, h * HALF:(h + 1) * HALF],
                                           start=True, stop=True)
                        mm.then_inc(sem_, 1)

                pe.wait_ge(sel_in, 16)
                pe.wait_ge(bc_step, 5)
                rows(0)
                pe.wait_ge(dg_ready, 1)
                for g in range(G):
                    pe.wait_ge(sp_abs, g + 1)
                    pe.wait_ge(sp_r_s, g + 1)
                    for h in range(2):
                        pe.matmul(bank(2 * g + h), dgd[:, g, :], u[:, g, h * HALF:(h + 1) * HALF],
                                  start=True, stop=False, skip_group_check=True)

                rows(1)

                def state(i, par, last=False):
                    n = i * 2 + par
                    if not last:
                        rows(n + 2)
                    for g in range(G):
                        pe.wait_ge(hc_ready, n * G + (g + 1))
                        for h in range(2):
                            mm = pe.matmul(bank(2 * g + h), ident[:, :], hc[par][:, g, h * HALF:(h + 1) * HALF],
                                           start=False, stop=False, skip_group_check=True)
                        mm.then_inc(y_added, 1)

                with pe.Fori(0, DS // 2 - 1) as i:
                    for par in range(2):
                        state(i, par)
                for par in range(2):
                    state(DS // 2 - 1, par, last=True)
                for g in range(G):
                    pe.wait_ge(yz_ready, g + 1)
                    for t in range(NT):
                        b, lc = t // 2, t % 2
                        mm = pe.transpose(bank(4 + t // 2)[:, (t % 2) * DM + g * P:(t % 2) * DM + (g + 1) * P],
                                          yz[:, g, b * L + lc * P:b * L + (lc + 1) * P], ident[:, :])
                        if g == G - 1:
                            mm.then_inc(yT, 1)

            @block.scalar
            def _(act):
                for g in range(G):
                    for h in range(2):
                        act.wait_ge(xin, 2 * g + h + 1)
                        act.activation(xpad[:, g, 2 * h:2 * h + 2, DC - 1:LP],
                                       bank(2 * g + h).rearrange("p (b l) -> p b l", b=2),
                                       ACT.Copy).then_inc(xpadded, 1)
                for g in range(G):
                    act.wait_ge(conv_step, DC * (g + 1))
                    act.activation(u[:, g, :], conv[:, g, :], ACT.Silu, bias=chan[:, g, PC_CB:PC_CB + 1]).then_inc(u_ready, 1)
                act.wait_ge(pads, 3)
                for h in range(2):
                    act.wait_ge(dt_psum, h + 1)
                    act.activation(dt_lo[0:DR, h * HALF:(h + 1) * HALF], bank(6 + h)[0:DR, :], ACT.Copy).then_inc(dt_ready, 1)
                for g in range(G):
                    act.wait_ge(pre, g + 1)
                    act.activation(sp_e[:, g, :], sh.banks(2 * g, 2), ACT.Abs).then_inc(sp_abs, 1)
                for g in range(G):
                    act.wait_ge(sp_abs, g + 1)
                    act.activation(sp_e[:, g, :], sp_e[:, g, :], ACT.Exp, scale=-1.0).then_inc(sp_exp, 1)
                act.activation(ae[:, :, :], chan[:, :, PC_A:PC_A + DS], ACT.Exp).then_inc(a_exp, 1)
                act.wait_ge(b_psum, 1)
                act.activation(b_row[:, 0, :], sh.banks(4, 2), ACT.Copy).then_inc(b_sb, 1)
                for g in range(G):
                    act.wait_ge(sp_w_s, g + 1)
                    act.activation(delta[:, g, :], sp_w[:, g, :], ACT.Ln).then_inc(sp_ln, 1)

                act.wait_ge(a_ready, 1)
                act.wait_ge(zero_da, 2)

                def state(i, par, first=False):
                    n = i * 2 + par
                    if not (first and par == 0):
                        act.wait_ge(b_psum, n + 1)
                        if not first:
                            act.wait_ge(dbu_ready, n * G - G)
                        act.activation(b_row[:, par, :], sh.banks(4, 2), ACT.Copy).then_inc(b_sb, 1)
                    for g in range(G):
                        if first:
                            act.wait_ge(delta_ready, g + 1)
                        else:
                            act.wait_ge(scanned, n * G - (2 * G - g - 1))
                        act.activation(da[:, par, g, :, 1:L],
                                       delta[:, g, :].rearrange("p (b l) -> p b l", b=B)[:, :, 1:L], ACT.Exp,
                                       scale=an[:, g, bass.ds(n, 1)]).then_inc(da_ready, 1)
                    act.wait_ge(c_psum, n + 1)
                    if not first:
                        act.wait_ge(hc_ready, n * G - G)
                    act.activation(c_row[:, par, :], sh.banks(6, 2), ACT.Copy).then_inc(c_sb, 1)

                for par in range(2):
                    state(0, par, first=True)
                with act.Fori(1, DS // 2) as i:
                    for par in range(2):
                        state(i, par)
                act.wait_ge(ln_shift, 1)
                for t in range(NT):
                    ins = act.activation(zs[:, t, :], x[:, t, :], ACT.Silu, bias=nmr[:, t:t + 1], scale=rstd[:, t:t + 1])
                ins.then_inc(z_ready, 1)

            @block.gpsimd
            def _(pool):
                pool.wait_ge(ln_var, 1)
                pool.tensor_tensor(rstd[:, :], vare[:, :], sh.mhalf[:, 0:NT], ALU.pow).then_inc(ln_rstd, 1)

                def state(i, par, first=False):
                    n = i * 2 + par
                    pool.wait_ge(b_sb, n + 1)
                    for g in range(G):
                        if first:
                            pool.wait_ge(du_ready, g + 1)
                        else:
                            pool.wait_ge(scanned, n * G - (2 * G - g - 1))
                        pool.tensor_tensor(dbu[:, par, g, :], du[:, g, :], b_row[:, par, :], ALU.mult).then_inc(dbu_ready, 1)

                for par in range(2):
                    state(0, par, first=True)
                with pool.Fori(1, DS // 2) as i:
                    for par in range(2):
                        state(i, par)

            @block.vector
            def _(dve):
                dve.memset(sh.mhalf[:, :], -0.5).then_inc(pads, 1)
                dve.memset(xpad[:, :, :, 0:DC - 1], 0.0).then_inc(pads, 1)
                for n in range(2):
                    dve.memset(da[:, n, :, :, 0:1], 0.0).then_inc(zero_da, 1)
                dve.memset(dt_lo[:, :], 1.0).then_inc(pads, 1)

                def tap(g, j):
                    src = xpad[:, g, :, j:j + L]
                    out = conv[:, g, :].rearrange("p (b l) -> p b l", b=B)
                    w = chan[:, g, PC_CONV + j:PC_CONV + j + 1]
                    if j == 0:
                        dve.tensor_scalar(out, src, w, None, ALU.mult).then_inc(conv_step, 1)
                    else:
                        dve.wait_ge(conv_step, DC * g + j)
                        dve.scalar_tensor_tensor(out, src, w, out, ALU.mult, ALU.add).then_inc(conv_step, 1)

                dve.wait_ge(pads, 3)
                dve.wait_ge(chan_in, 16)
                for g in range(G):
                    dve.wait_ge(xpadded, 2 * g + 2)
                    for j in range(DC):
                        tap(g, j)
                dve.wait_ge(x_in, 16)
                for t in range(NT):
                    dve.bn_stats(st[:, t, :], x[:, t, :]).then_inc(ln_step, 1)
                for t in range(NT):
                    dve.wait_ge(ln_step, t + 1)
                    dve.bn_aggr(mv[:, t, :], st[:, t, :]).then_inc(ln_step, 1)
                dve.wait_ge(ln_step, 2 * NT)
                dve.tensor_scalar(vare[:, :], mv[:, :, 1], EPS, None, ALU.add).then_inc(ln_var, 1)
                dve.wait_ge(dt_in, 32)
                for g in range(G):
                    ins = dve.tensor_scalar(dgd[:, g, :], ident[:, :], chan[:, g, PC_D:PC_D + 1], None, ALU.mult)
                ins.then_inc(dg_ready, 1)

                dve.wait_ge(bc_psum, 2)
                v = sh.banks(4, 2)[0:3 * NBC, :]
                dve.tensor_copy(bc_hi[:, :], v).then_inc(bc_step, 1)
                dve.wait_ge(bc_step, 1)
                dve.tensor_tensor(bc_r[:, :], v, bc_hi[:, :], ALU.subtract).then_inc(bc_step, 1)
                dve.wait_ge(bc_step, 2)
                dve.tensor_copy(bc3[:, :], bc_r[:, :]).then_inc(bc_step, 1)
                dve.wait_ge(bc_step, 3)
                dve.tensor_copy(bc3[0:NBC, :], bc_hi[0:NBC, :]).then_inc(bc_step, 1)
                dve.tensor_tensor(bc3[2 * NBC:3 * NBC, :], bc_r[2 * NBC:3 * NBC, :], bc3[2 * NBC:3 * NBC, :],
                                  ALU.subtract).then_inc(bc_step, 1)

                for g in range(G):
                    dve.wait_ge(sp_exp, g + 1)
                    dve.tensor_scalar(sp_w[:, g, :], sp_e[:, g, :], 1.0, None, ALU.add).then_inc(sp_w_s, 1)
                for g in range(G):
                    dve.wait_ge(sp_w_s, g + 1)
                    dve.scalar_tensor_tensor(sp_e[:, g, :], sp_w[:, g, :], -1.0, sp_e[:, g, :],
                                             ALU.add, ALU.subtract).then_inc(sp_t, 1)
                    dve.wait_ge(sp_t, g + 1)
                    dve.scalar_tensor_tensor(sp_r[:, g, :], sh.banks(2 * g, 2), 0.0, sp_e[:, g, :],
                                             ALU.max, ALU.subtract).then_inc(sp_r_s, 1)
                dve.wait_ge(a_exp, 1)
                dve.tensor_scalar(an[:, :, :], ae[:, :, :], -1.0, None, ALU.mult).then_inc(a_ready, 1)
                for g in range(G):
                    dve.wait_ge(sp_r_s, g + 1)
                    dve.wait_ge(sp_ln, g + 1)
                    dve.tensor_tensor(delta[:, g, :], delta[:, g, :], sp_r[:, g, :], ALU.add).then_inc(delta_ready, 1)
                    dve.wait_ge(delta_ready, g + 1)
                    dve.wait_ge(u_ready, G)
                    dve.tensor_tensor(du[:, g, :], delta[:, g, :], u[:, g, :], ALU.mult).then_inc(du_ready, 1)

                dve.wait_ge(ln_rstd, 1)
                dve.scalar_tensor_tensor(nmr[:, :], mv[:, :, 0], -1.0, rstd[:, :], ALU.mult, ALU.mult).then_inc(ln_shift, 1)

                def states(i, first=False):
                    for par in range(2):
                        n = i * 2 * G
                        for g in range(G):
                            dve.wait_ge(da_ready, n + (par * G + g + 1))
                            dve.wait_ge(dbu_ready, n + (par * G + g + 1))
                            dve.tensor_tensor_scan(hst[:, par, g, :], da[:, par, g, :, :].rearrange("p b l -> p (b l)"),
                                                   dbu[:, par, g, :], 0.0, ALU.mult, ALU.add).then_inc(scanned, 1)
                        dve.wait_ge(c_sb, i * 2 + (par + 1))
                        for g in range(G):
                            dve.wait_ge(scanned, n + (par * G + g + 1))
                            if not first:
                                dve.wait_ge(y_added, n + (par * G - 2 * G + g + 1))
                            dve.tensor_tensor(hc[par][:, g, :], hst[:, par, g, :], c_row[:, par, :], ALU.mult)\
                                .then_inc(hc_ready, 1)

                states(0, first=True)
                with dve.Fori(1, DS // 2) as i:
                    states(i)

                dve.wait_ge(z_ready, 1)
                for g in range(G):
                    dve.wait_ge(y_added, G * DS - G + g + 1)
                    z = zs[:, :, :].rearrange("p (b g) l -> p b g l", g=G)[:, :, g, :]
                    dve.tensor_tensor(yz[:, g, :].rearrange("p (b l) -> p b l", b=B),
                                      sh.banks(2 * g, 2).rearrange("p (b l) -> p b l", b=B),
                                      z, ALU.mult).then_inc(yz_ready, 1)
                for q in range(NT // 2):
                    dve.wait_ge(yT, 2 * q + 2)
                    xs = x[:, 2 * q:2 * q + 2, :].rearrange("p t f -> p (t f)")
                    dve.tensor_tensor(xs, xs, bank(4 + q), ALU.add).then_inc(x_added, 1)


class NormSems:

    def __init__(self, sem):
        self.step, self.var, self.rstd, self.normed, self.turned, self.hi, self.lo, self.full = (
            sem("n_" + n) for n in ("step", "var", "rstd", "normed", "turned", "hi", "lo", "full"))


def norm_vector(dve, sh, s):
    for h in range(2):
        tiles = range(h * TPH, (h + 1) * TPH)
        for t in tiles:
            dve.bn_stats(sh.st[:, t, :], sh.x[:, t, :]).then_inc(s.step, 1)
        for n, t in enumerate(tiles):
            dve.wait_ge(s.step, 2 * TPH * h + n + 1)
            dve.bn_aggr(sh.mv[:, t, :], sh.st[:, t, :]).then_inc(s.step, 1)
        dve.wait_ge(s.step, 2 * TPH * (h + 1))
        dve.tensor_scalar(sh.vare[:, h * TPH:(h + 1) * TPH], sh.mv[:, h * TPH:(h + 1) * TPH, 1], EPS, None,
                          ALU.add).then_inc(s.var, 1)
    for h in range(2):
        dve.wait_ge(s.rstd, h + 1)
        for t in range(h * TPH, (h + 1) * TPH):
            dve.tensor_scalar(sh.xn[:, t, :], sh.x[:, t, :], sh.mv[:, t, 0:1], sh.rstd[:, t:t + 1],
                              ALU.subtract, ALU.mult).then_inc(s.normed, 1)


def norm_gpsimd(pool, sh, s):
    for h in range(2):
        pool.wait_ge(s.var, h + 1)
        pool.tensor_tensor(sh.rstd[:, h * TPH:(h + 1) * TPH], sh.vare[:, h * TPH:(h + 1) * TPH],
                           sh.mhalf[:, 0:TPH], ALU.pow).then_inc(s.rstd, 1)


def norm_tensor(pe, sh, s):
    for h in range(2):
        for t in range(h * TPH, (h + 1) * TPH):
            pe.wait_ge(s.normed, t + 1)
            for k in range(KD):
                mm = pe.transpose(sh.bank(4 + 2 * h + k)[:, (t % TPH) * P:(t % TPH + 1) * P],
                                  sh.xn[:, t, k * P:(k + 1) * P], sh.ident[:, :])
        mm.then_inc(s.turned, 1)


def turned_view(sh, h):
    return sh.banks(4 + 2 * h, 2).rearrange("p (k t) -> p k t", k=KD)


def norm_scalar(act, sh, s):
    for h in range(2):
        act.wait_ge(s.turned, h + 1)
        act.activation(sh.xT_hi[:, :, h * HALF:(h + 1) * HALF], turned_view(sh, h), ACT.Copy).then_inc(s.hi, 1)


def norm_lo_vector(dve, sh, s, full):
    for h in range(2):
        dve.wait_ge(s.hi, h + 1)
        if full is not None:
            dve.tensor_copy(full[:, :, h * HALF:(h + 1) * HALF], turned_view(sh, h)).then_inc(s.full, 1)
        dve.tensor_tensor(sh.xT_lo[:, :, h * HALF:(h + 1) * HALF], turned_view(sh, h),
                          sh.xT_hi[:, :, h * HALF:(h + 1) * HALF], ALU.subtract).then_inc(s.lo, 1)


GU = 2 * KD * P
WCH = GU + DM
HS = 4


def moe_block(nc, sh, tag, weights, router, scratch, experts, shared, groups, gated, out):
    NC = chunks_of(experts, shared)
    NU = 2 * NC
    ER = experts + (1 if gated else 0)
    E1 = experts + 1
    assert NC % 2 == 1
    with ExitStack() as ctx:
        def sb(name, shape, dt=F32):
            return ctx.enter_context(nc.sbuf_tensor(f"{tag}_{name}", shape, dt))

        def sem(name):
            return ctx.enter_context(nc.semaphore(f"{tag}_{name}"))

        bank, ident, x = sh.bank, sh.ident, sh.x
        raw = sb("raw", [P, 2, WCH])
        gu_hi = sb("gu_hi", [P, 2, GU], F32R)
        gu_lo = sb("gu_lo", [P, 2, GU], F32R)
        dn_hi = sb("dn_hi", [P, 2, DM], F32R)
        dn_lo = sb("dn_lo", [P, 2, DM], F32R)
        comb = sb("comb", [P, 2, T])
        sg = sb("sg", [P, HS, HALF])
        su = sb("su", [P, HS, HALF])
        hid = sb("hid", [P, HS, HALF])
        h_hi = sb("h_hi", [P, HS, HALF], F32R)
        h_lo = sb("h_lo", [P, HS, HALF], F32R)
        xT = sb("xT", [P, KD, T])
        wr = sb("wr", [P, KD, ER])
        lg = sb("lg", [P, NT, ER])
        neg = sb("neg", [P, NT])
        ex = sb("ex", [P, NT, ER])
        den = sb("den", [P, NT])
        pr = sb("pr", [P, NT, 16])
        top = sb("top", [P, NT, 8])
        left = sb("left", [P, NT, 16])
        gs = sb("gs", [P, NT, 16])
        gtop = sb("gtop", [P, NT, 8])
        gleft = sb("gleft", [P, NT, 16])
        gmask = sb("gmask", [P, NT, 4])
        gminus = sb("gminus", [P, NT, 4])
        msk = sb("msk", [P, NT, 16])
        cw = sb("cw", [P, NT, E1])
        cT = sb("cT", [E1, T])

        s = NormSems(sem)
        wr_in, logits, route, ex_ready, cw_ready, cT_psum, cT_ready, cT_out = (
            sem(n) for n in ("wr_in", "logits", "route", "ex_ready", "cw_ready", "cT_psum", "cT_ready", "cT_out"))
        raw_in = [sem(f"raw_in{i}") for i in range(2)]
        comb_in = [sem(f"comb_in{i}") for i in range(2)]
        gu_hi_s, gu_lo_s, dn_hi_s, dn_lo_s = (sem(n) for n in ("gu_hi_done", "gu_lo_done", "dn_hi_done", "dn_lo_done"))
        gate_ps, up_ps, silu_s, su_s, hid_s, h_hi_s, h_lo_s, down_s = (
            sem(n) for n in ("gate_ps", "up_ps", "silu_done", "su_done", "hid_done", "h_hi_done", "h_lo_done", "down_done"))
        x_back, stored = sem("x_back"), sem("stored")

        def gate_bank(half):
            return bank(4 + 2 * half)

        def up_bank(half):
            return bank(5 + 2 * half)

        with nc.Block() as block:
            def broadcast(sp, c):
                if c >= 2:
                    sp.wait_ge(hid_s, 2 * (c - 2) + 2)
                for a, b, e in segments(c, experts):
                    sp.dma_start(comb[a:b, c % 2, :], scratch[e:e + 1, :].to_broadcast([b - a, T])).then_inc(comb_in[c % 2], 16)

            @block.sync
            def _(sp):
                sp.dma_start(wr[:, :, :], router).then_inc(wr_in, 16)
                for c in range(NC):
                    if c >= 2:
                        sp.wait_ge(dn_lo_s, c - 1)
                    sp.dma_start(raw[:, c % 2, :], weights[c]).then_inc(raw_in[c % 2], 16)
                    if c == 1:
                        sp.wait_ge(cT_ready, 2)
                        sp.dma_start(scratch, cT[:, :]).then_inc(cT_out, 16)
                        sp.wait_ge(cT_out, 16)
                        broadcast(sp, 0)
                    if c >= 1:
                        broadcast(sp, c)
                if out is not None:
                    sp.wait_ge(x_back, NT // 2)
                    for q in range(NT // 2):
                        sp.dma_start(out.rearrange("(t p) f -> p t f", p=P)[:, 2 * q:2 * q + 2, :],
                                     x[:, 2 * q:2 * q + 2, :]).then_inc(stored, 16)
                    sp.wait_ge(stored, 16 * (NT // 2))

            @block.tensor
            def _(pe):
                norm_tensor(pe, sh, s)
                pe.wait_ge(wr_in, 16)
                for t in range(NT):
                    pe.wait_ge(s.full, t // TPH + 1)
                    for k in range(KD):
                        mm = pe.matmul(bank(0)[:, t * ER:(t + 1) * ER], xT[:, k, t * P:(t + 1) * P], wr[:, k, :],
                                       start=(k == 0), stop=(k == KD - 1))
                mm.then_inc(logits, 1)

                def gate_up(j, slot, half):
                    tok = slice(half * HALF, (half + 1) * HALF)
                    for what, (dst, done) in enumerate(((gate_bank(half), gate_ps), (up_bank(half), up_ps))):
                        for k in range(KD):
                            w = slice((what * KD + k) * P, (what * KD + k + 1) * P)
                            mm = product3(pe, dst, (gu_hi[:, slot, w], gu_lo[:, slot, w]),
                                          (sh.xT_hi[:, k, tok], sh.xT_lo[:, k, tok]), k == 0, k == KD - 1)
                        mm.then_inc(done, 1)

                def down(slot, hslot, half):
                    for n in range(TPH):
                        t = half * TPH + n
                        tok = slice(n * P, (n + 1) * P)
                        mm = product3(pe, bank(t // 2)[:, (t % 2) * DM:(t % 2 + 1) * DM],
                                      (h_hi[:, hslot, tok], h_lo[:, hslot, tok]),
                                      (dn_hi[:, slot, :], dn_lo[:, slot, :]), False, False)
                    mm.then_inc(down_s, 1)

                pe.wait_ge(s.lo, 2)
                pe.wait_ge(gu_lo_s, 1)
                for half in range(2):
                    gate_up(half, 0, half)
                pe.wait_ge(cw_ready, 1)
                for h in range(2):
                    for n in range(TPH):
                        mm = pe.transpose(bank(1 + h)[0:E1, n * P:(n + 1) * P], cw[:, h * TPH + n, :], ident[:, :])
                    mm.then_inc(cT_psum, 1)
                pe.wait_ge(cT_ready, 2)
                for q in range(NT // 2):
                    pe.matmul(bank(q), ident[:, :], x[:, 2 * q:2 * q + 2, :].rearrange("p t f -> p (t f)"),
                              start=True, stop=False, skip_group_check=True)

                with pe.Fori(0, (NU - 2) // HS) as i:
                    for q in range(HS):
                        half, slot = q % 2, (q // 2 + 1) % 2
                        j = i * HS + q
                        if half == 0:
                            pe.wait_ge(gu_lo_s, i * 2 + q // 2 + 2)
                        pe.wait_ge(silu_s, j + 1)
                        pe.wait_ge(su_s, j + 1)
                        gate_up(None, slot, half)
                        pe.wait_ge(h_lo_s, j + 1)
                        pe.wait_ge(dn_lo_s, i * 2 + q // 2 + 1)
                        down(q // 2, q, half)
                for q in range(2):
                    j = NU - 2 + q
                    pe.wait_ge(h_lo_s, j + 1)
                    pe.wait_ge(dn_lo_s, NC)
                    down((NC - 1) % 2, j % HS, q)

            @block.scalar
            def _(act):
                act.wait_ge(raw_in[0], 16)
                act.activation(gu_hi[:, 0, :], raw[:, 0, 0:GU], ACT.Copy).then_inc(gu_hi_s, 1)
                norm_scalar(act, sh, s)
                act.wait_ge(route, 2)
                act.activation(ex[:, :, 0:experts], ex[:, :, 0:experts], ACT.Exp).then_inc(ex_ready, 1)
                if gated:
                    act.activation(ex[:, :, experts:ER], lg[:, :, experts:ER], ACT.Exp, scale=-1.0).then_inc(ex_ready, 1)

                def copies_out():
                    for h in range(2):
                        act.wait_ge(cT_psum, h + 1)
                        act.activation(cT[:, h * HALF:(h + 1) * HALF], bank(1 + h)[0:E1, :], ACT.Copy).then_inc(cT_ready, 1)

                def chunk(c, par, pair, first=False, last=False):
                    for half in range(2):
                        j = 2 * c + half
                        hs = 2 * par + half
                        act.wait_ge(gate_ps, j + 1)
                        if not first:
                            act.wait_ge(su_s, j - HS + 1)
                        act.activation(sg[:, hs, :], gate_bank(half), ACT.Silu).then_inc(silu_s, 1)
                        if first and par == 0 and half == 1:
                            copies_out()
                        if half == 0:
                            if not last:
                                act.wait_ge(raw_in[(par + 1) % 2], (pair + (par + 1) // 2) * 16 + 16)
                                if not (first and par == 0):
                                    act.wait_ge(up_ps, 2 * c)
                                act.activation(gu_hi[:, (par + 1) % 2, :], raw[:, (par + 1) % 2, 0:GU],
                                               ACT.Copy).then_inc(gu_hi_s, 1)
                            if not first:
                                act.wait_ge(down_s, 2 * c - 2)
                            act.activation(dn_hi[:, par, :], raw[:, par, GU:WCH], ACT.Copy).then_inc(dn_hi_s, 1)
                        if first and par == 0 and half == 0:
                            continue
                        if first and par == 0:
                            hi_part(0, 0, True)
                        hi_part(j, hs, first)

                def hi_part(j, hs, first):
                    act.wait_ge(hid_s, j + 1)
                    if not first:
                        act.wait_ge(down_s, j - HS + 1)
                    act.activation(h_hi[:, hs, :], hid[:, hs, :], ACT.Copy).then_inc(h_hi_s, 1)

                for par in range(2):
                    chunk(par, par, 0, first=True)
                with act.Fori(1, NC // 2) as i:
                    for par in range(2):
                        chunk(2 * i + par, par, i)
                chunk(NC - 1, 0, NC // 2, last=True)
                act.wait_ge(down_s, NU)
                for q in (1, 3):
                    act.activation(x[:, 2 * q:2 * q + 2, :].rearrange("p t f -> p (t f)"), bank(q), ACT.Copy)\
                        .then_inc(x_back, 1)

            @block.gpsimd
            def _(pool):
                norm_gpsimd(pool, sh, s)

                def lo_part(out, whole, hi):
                    return pool.tensor_tensor(out, whole, hi, ALU.subtract)

                pool.wait_ge(gu_hi_s, 1)
                lo_part(gu_lo[:, 0, :], raw[:, 0, 0:GU], gu_hi[:, 0, :]).then_inc(gu_lo_s, 1)

                def chunk(c, par, last=False):
                    if not last:
                        pool.wait_ge(gu_hi_s, c + 2)
                        lo_part(gu_lo[:, (par + 1) % 2, :], raw[:, (par + 1) % 2, 0:GU],
                                gu_hi[:, (par + 1) % 2, :]).then_inc(gu_lo_s, 1)
                    pool.wait_ge(dn_hi_s, c + 1)
                    lo_part(dn_lo[:, par, :], raw[:, par, GU:WCH], dn_hi[:, par, :]).then_inc(dn_lo_s, 1)
                    for half in range(2):
                        pool.wait_ge(h_hi_s, 2 * c + half + 1)
                        hs = 2 * par + half
                        lo_part(h_lo[:, hs, :], hid[:, hs, :], h_hi[:, hs, :]).then_inc(h_lo_s, 1)

                with pool.Fori(0, NC // 2) as i:
                    for par in range(2):
                        chunk(2 * i + par, par)
                chunk(NC - 1, 0, last=True)

            @block.vector
            def _(dve):
                norm_vector(dve, sh, s)
                norm_lo_vector(dve, sh, s, xT)

                steps = [0]

                def step(ins):
                    steps[0] += 1
                    ins.then_inc(route, 1)
                    dve.wait_ge(route, steps[0])

                def spread(v, n):
                    return v.unsqueeze(2).to_broadcast([P, NT, n])

                dve.wait_ge(logits, 1)
                view = bank(0)[:, 0:NT * ER].rearrange("p (t e) -> p t e", t=NT)
                dve.tensor_copy(lg[:, :, :], view)
                step(dve.tensor_reduce(neg[:, :], view[:, :, 0:experts], AX_X, ALU.max))
                step(dve.tensor_tensor(ex[:, :, 0:experts], lg[:, :, 0:experts], spread(neg[:, :], experts), ALU.subtract))
                dve.wait_ge(ex_ready, 2 if gated else 1)
                step(dve.tensor_reduce(den[:, :], ex[:, :, 0:experts], AX_X, ALU.add))
                step(dve.reciprocal(den[:, :], den[:, :]))
                if experts < 16:
                    step(dve.memset(pr[:, :, experts:16], -1.0))
                step(dve.tensor_tensor(pr[:, :, 0:experts], ex[:, :, 0:experts], spread(den[:, :], experts), ALU.mult))
                pick = pr
                k = 2
                if groups:
                    per = experts // groups
                    step(dve.memset(gs[:, :, groups:16], -1.0))
                    step(dve.tensor_reduce(gs[:, :, 0:groups], pr[:, :, :].rearrange("p t (g e) -> p (t g) e", g=groups),
                                           AX_X, ALU.max))
                    for t in range(NT):
                        ins = dve.max(gtop[:, t, :], gs[:, t, :])
                    step(ins)
                    step(dve.memset(gtop[:, :, 2:8], -1.0))
                    for t in range(NT):
                        ins = dve.match_replace(gleft[:, t, :], gtop[:, t, :], gs[:, t, :], -2.0)
                    step(ins)
                    step(dve.tensor_scalar(gmask[:, :, :], gleft[:, :, 0:groups], -2.0, None, ALU.is_equal))
                    step(dve.tensor_scalar(gminus[:, :, :], gmask[:, :, :], -1.0, None, ALU.add))
                    for dst, a, b, op in ((msk, pr, gmask, ALU.mult), (msk, msk, gminus, ALU.add)):
                        v = [y[:, :, :].rearrange("p t (g e) -> p (t g) e", g=groups) for y in (dst, a)]
                        m = b[:, :, :].rearrange("p t g -> p (t g)").unsqueeze(2).to_broadcast([P, NT * groups, per])
                        step(dve.tensor_tensor(v[0], v[1], m, op))
                    pick, k = msk, 4
                for t in range(NT):
                    ins = dve.max(top[:, t, :], pick[:, t, :])
                step(ins)
                step(dve.memset(top[:, :, k:8], -1.0))
                for t in range(NT):
                    ins = dve.match_replace(left[:, t, :], top[:, t, :], pick[:, t, :], -2.0)
                step(ins)
                step(dve.tensor_scalar(left[:, :, :], left[:, :, :], -2.0, None, ALU.is_equal))
                if gated:
                    step(dve.tensor_scalar(ex[:, :, experts:ER], ex[:, :, experts:ER], 1.0, None, ALU.add))
                    step(dve.reciprocal(cw[:, :, experts:E1], ex[:, :, experts:ER]))
                else:
                    step(dve.memset(cw[:, :, experts:E1], 1.0))
                dve.scalar_tensor_tensor(cw[:, :, 0:experts], pick[:, :, 0:experts], 0.0, left[:, :, 0:experts],
                                         ALU.max, ALU.mult).then_inc(cw_ready, 1)

                def gated_up(j, hs, half):
                    dve.wait_ge(silu_s, j + 1)
                    dve.wait_ge(up_ps, j + 1)
                    dve.tensor_tensor(su[:, hs, :], sg[:, hs, :], up_bank(half), ALU.mult).then_inc(su_s, 1)

                def combined(j, par, pair, half, first=False):
                    dve.wait_ge(su_s, j + 1)
                    dve.wait_ge(comb_in[par], pair * 32 + 32)
                    if not first:
                        dve.wait_ge(h_lo_s, j - HS + 1)
                    dve.tensor_tensor(hid[:, 2 * par + half, :], su[:, 2 * par + half, :],
                                      comb[:, par, half * HALF:(half + 1) * HALF], ALU.mult).then_inc(hid_s, 1)

                def pair_of_chunks(i, chunks, first=False):
                    for par in range(chunks):
                        for half in range(2):
                            j = i * HS + 2 * par + half
                            gated_up(j, 2 * par + half, half)
                            combined(j, par, i, half, first)

                pair_of_chunks(0, 2, first=True)
                with dve.Fori(1, NC // 2) as i:
                    pair_of_chunks(i, 2)
                pair_of_chunks(NC // 2, 1)
                dve.wait_ge(down_s, NU)
                for q in (0, 2):
                    dve.tensor_copy(x[:, 2 * q:2 * q + 2, :].rearrange("p t f -> p (t f)"), bank(q)).then_inc(x_back, 1)


QKV = (KD + 2) * HP * HD
WPAIR = QKV + HP * DM
NUA = NPAIR * B
UW = HP * L


def attention_block(nc, sh, d):
    with ExitStack() as ctx:
        def sb(name, shape, dt=F32):
            return ctx.enter_context(nc.sbuf_tensor("a_" + name, shape, dt))

        def sem(name):
            return ctx.enter_context(nc.semaphore("a_" + name))

        bank, ident, x = sh.bank, sh.ident, sh.x
        raw = sb("raw", [P, 2, WPAIR])
        w_hi = sb("w_hi", [P, 2, QKV], F32R)
        w_lo = sb("w_lo", [P, 2, QKV], F32R)
        c_hi = sb("c_hi", [P, T], F32R)
        c_lo = sb("c_lo", [P, T], F32R)
        gq = sb("gq", [HD, 1])
        gk = sb("gk", [HD, 1])
        gg = sb("gg", [HD, 1])
        eps = sb("eps", [P, 8])
        sq = sb("sq", [P, 2, 2 * UW])
        ss = sb("ss", [P, 2, 8])
        rr = sb("rr", [P, 2, 8])
        qkn = sb("qkn", [P, 2, 2 * UW])
        qT = sb("qT", [P, 2, UW])
        kT = sb("kT", [P, 2, UW])
        v = sb("v", [P, 4, UW])
        nmax = sb("nmax", [P, 2, 4])
        rsum = sb("rsum", [P, 2, 4])
        rinv = sb("rinv", [P, 2, 4])
        pe_ = sb("p_exp", [P, 2, 4, L])
        pn = sb("p_norm", [P, 2, 4, L])
        pT = sb("pT", [P, 2, HP, UW])
        oT = sb("oT", [P, 2, UW])

        s = NormSems(sem)
        g_in, eps_s, gg_ready, c_hi_s, c_lo_s = (sem(n) for n in ("g_in", "eps_done", "gg_ready", "c_hi_done", "c_lo_done"))
        raw_in = [sem(f"raw_in{i}") for i in range(2)]
        w_hi_s, w_lo_s = sem("w_hi_done"), sem("w_lo_done")
        qk_ps, v_ps, sq_s, v_s, ms, mse_s, rr_s, qkn_s = (
            sem(n) for n in ("qk_ps", "v_ps", "sq_done", "v_done", "ms_done", "mse_done", "rr_done", "qkn_done"))
        turn_ps, qT_s, kT_s, sc_ps, max_s, exp_s, rinv_s, pn_s = (
            sem(n) for n in ("turn_ps", "qT_done", "kT_done", "sc_ps", "max_done", "exp_done", "rinv_done", "pn_done"))
        pT_ps, pT0_s, pT1_s, o_ps, oT_s, out_ps, out_s = (
            sem(n) for n in ("pT_ps", "pT0_done", "pT1_done", "o_ps", "oT_done", "out_ps", "out_done"))

        def steps(eng, body):
            for n in range(ATT_PEEL):
                body(0, n)
            with eng.Fori(0, ATT_LOOPS) as i:
                for n in range(ATT_PEEL, ATT_PEEL + ATT_BODY):
                    body(i, n)
            for n in range(ATT_PEEL, NUA + 1 - ATT_LOOPS * ATT_BODY):
                body(ATT_LOOPS, n)

        Q, K, V, QT, KT, OW = (bank(n) for n in (2, 3, 4, 5, 6, 7))

        with nc.Block() as block:
            @block.sync
            def _(sp):
                sp.dma_start(raw[:, 0, :], d["w_pair"][0]).then_inc(raw_in[0], 16)
                sp.dma_start(gq[:, :], d["gq"]).then_inc(g_in, 16)
                sp.dma_start(gk[:, :], d["gk"]).then_inc(g_in, 16)
                sp.dma_start(raw[:, 1, :], d["w_pair"][1]).then_inc(raw_in[1], 16)
                for p in range(2, NPAIR):
                    sp.wait_ge(w_lo_s, p - 1)
                    sp.wait_ge(out_ps, B * (p - 1))
                    sp.dma_start(raw[:, p % 2, :], d["w_pair"][p]).then_inc(raw_in[p % 2], 16)

            @block.tensor
            def _(pe):
                norm_tensor(pe, sh, s)

                def project(t, n):
                    slot, b = (n // B) % 2, n % B
                    for which, (dst, base, ks) in enumerate(((Q, 0, KD), (K, KD, 1), (V, KD + 1, 1))):
                        for tile in range(2):
                            tok = slice(b * L + tile * P, b * L + (tile + 1) * P)
                            for k in range(ks):
                                a = (sh.xT_hi[:, k, tok], sh.xT_lo[:, k, tok]) if which == 0 else (c_hi[:, tok], c_lo[:, tok])
                                w = slice((base + k) * HP * HD, (base + k + 1) * HP * HD)
                                mm = product3(pe, dst[:, tile * HP * HD:(tile + 1) * HP * HD], a,
                                              (w_hi[:, slot, w], w_lo[:, slot, w]), k == 0, k == ks - 1)
                        if which:
                            mm.then_inc((qk_ps, v_ps)[which - 1], 1)

                def heads_turned(n):
                    for which, dst in enumerate((QT, KT)):
                        for hh in range(HP):
                            for tile in range(2):
                                mm = pe.transpose(dst[:, hh * L + tile * P:hh * L + (tile + 1) * P],
                                                  qkn[:, n % 2, ((which * 2 + tile) * HP + hh) * HD:((which * 2 + tile) * HP + hh + 1) * HD],
                                                  ident[:, :])
                    mm.then_inc(turn_ps, 1)

                def scores(n):
                    for hh in range(HP):
                        for tile in range(2):
                            mm = pe.matmul(bank(hh)[:, tile * L:(tile + 1) * L],
                                           qT[:, n % 2, hh * L + tile * P:hh * L + (tile + 1) * P],
                                           kT[:, n % 2, hh * L:(hh + 1) * L], start=True, stop=True)
                        mm.then_inc(sc_ps, 1)

                def probabilities_turned(t, n):
                    for hh in range(HP):
                        pe.wait_ge(pn_s, HP * t + hh + 1)
                        for kt in range(2):
                            for tile in range(2):
                                mm = pe.transpose(bank(hh)[:, kt * L + tile * P:kt * L + (tile + 1) * P],
                                                  pn[:, n % 2, 2 * hh + tile, kt * P:(kt + 1) * P], ident[:, :])
                        mm.then_inc(pT_ps, 1)

                def values(n):
                    for hh in range(HP):
                        for kt in range(2):
                            mm = pe.matmul(OW[:, hh * L:(hh + 1) * L],
                                           v[:, n % 4, (kt * HP + hh) * HD:(kt * HP + hh + 1) * HD],
                                           pT[:, n % 2, hh, kt * L:(kt + 1) * L], start=(kt == 0), stop=(kt == 1))
                    mm.then_inc(o_ps, 1)

                def output(n):
                    slot = (n // B) % 2
                    for tile in range(2):
                        for hh in range(HP):
                            mm = pe.matmul(OW[:, tile * DM:(tile + 1) * DM],
                                           oT[:, n % 2, hh * L + tile * P:hh * L + (tile + 1) * P],
                                           raw[:, slot, QKV + hh * DM:QKV + (hh + 1) * DM],
                                           start=(hh == 0), stop=(hh == HP - 1))
                    mm.then_inc(out_ps, 1)

                def step(i, n):
                    t = i * ATT_BODY + n
                    static = isinstance(i, int)
                    first, last = static and t < 2, static and t > NUA - 3
                    end = static and t == NUA
                    if not end:
                        pe.wait_ge(qT_s, t + 1)
                        pe.wait_ge(kT_s, t + 1)
                        if not (static and t == 0):
                            pe.wait_ge(pT0_s, t)
                            pe.wait_ge(pT1_s, t)
                        scores(n)
                    if not last:
                        if n % B == 2:
                            pe.wait_ge(w_lo_s, i * 2 + ((n + 2) // B + 1))
                        pe.wait_ge(qkn_s, t + 2)
                        pe.wait_ge(v_s, t + 2)
                        project(t, n + 2)
                    if not (static and t == 0):
                        pe.wait_ge(pT0_s, t)
                        pe.wait_ge(pT1_s, t)
                        pe.wait_ge(v_s, t)
                        if not first:
                            pe.wait_ge(out_s, t - 1)
                        values(n - 1)
                    if not (static and t >= NUA - 1):
                        pe.wait_ge(qkn_s, t + 2)
                        heads_turned(n + 1)
                    if not end:
                        probabilities_turned(t, n)
                    if not (static and t == 0):
                        pe.wait_ge(oT_s, t)
                        output(n - 1)

                pe.wait_ge(s.lo, 2)
                pe.wait_ge(c_lo_s, 1)
                pe.wait_ge(w_lo_s, 1)
                project(0, 0)
                pe.wait_ge(qkn_s, 1)
                pe.wait_ge(v_s, 1)
                project(1, 1)
                heads_turned(0)
                steps(pe, step)

            @block.scalar
            def _(act):
                act.wait_ge(raw_in[0], 16)
                act.activation(w_hi[:, 0, :], raw[:, 0, 0:QKV], ACT.Copy).then_inc(w_hi_s, 1)
                act.activation(c_hi[:, :], sh.ctxT[:, :], ACT.Copy).then_inc(c_hi_s, 1)
                norm_scalar(act, sh, s)

                def squares(t, n):
                    act.wait_ge(qk_ps, t + 1)
                    if not (isinstance(t, int) and t < 2):
                        act.wait_ge(ms, t - 1)
                    act.activation(sq[:, n % 2, :], sh.banks(2, 2), ACT.Square, scale=HD ** -0.5).then_inc(sq_s, 1)
                    act.wait_ge(v_ps, t + 1)
                    if not (isinstance(t, int) and t < 4):
                        act.wait_ge(o_ps, t - 3)
                    act.activation(v[:, n % 4, :], V, ACT.Copy).then_inc(v_s, 1)

                def turned(t, n):
                    act.wait_ge(turn_ps, t + 1)
                    if not (isinstance(t, int) and t < 2):
                        act.wait_ge(sc_ps, HP * (t - 1))
                    act.activation(qT[:, n % 2, :], QT, ACT.Copy).then_inc(qT_s, 1)
                    act.activation(kT[:, n % 2, :], KT, ACT.Copy, scale=gg[:, :]).then_inc(kT_s, 1)

                def softmax(t, n):
                    for hh in range(HP):
                        act.wait_ge(max_s, HP * t + hh + 1)
                        if not (isinstance(t, int) and t < 2):
                            act.wait_ge(pn_s, HP * (t - 2) + hh + 1)
                        for tile in range(2):
                            m = 2 * hh + tile
                            ins = act.activation(pe_[:, n % 2, m, :], bank(hh)[:, tile * L:(tile + 1) * L], ACT.Exp,
                                                 bias=nmax[:, n % 2, m:m + 1], accum_out=rsum[:, n % 2, m:m + 1])
                        ins.then_inc(exp_s, 1)

                def probabilities(t, n):
                    act.wait_ge(pT_ps, HP * t + 2)
                    if not (isinstance(t, int) and t < 2):
                        act.wait_ge(o_ps, t - 1)
                    act.activation(pT[:, n % 2, 1, :], bank(1), ACT.Copy).then_inc(pT1_s, 1)

                squares(0, 0)
                squares(1, 1)
                act.wait_ge(gg_ready, 1)
                turned(0, 0)

                def step(i, n):
                    t = i * ATT_BODY + n
                    static = isinstance(i, int)
                    if static and t >= NUA:
                        return
                    softmax(t, n)
                    if not (static and t > NUA - 3):
                        squares(t + 2, n + 2)
                        if n % B == 1 and not (static and t > NUA - B):
                            ahead = n // B + 1
                            slot = ahead % 2
                            act.wait_ge(raw_in[slot], i * 16 + (ahead // 2 * 16 + 16))
                            if not (static and t < B):
                                act.wait_ge(v_ps, t - n % B)
                            act.activation(w_hi[:, slot, :], raw[:, slot, 0:QKV], ACT.Copy).then_inc(w_hi_s, 1)
                    if not (static and t >= NUA - 1):
                        turned(t + 1, n + 1)
                    probabilities(t, n)

                steps(act, step)

            @block.gpsimd
            def _(pool):
                norm_gpsimd(pool, sh, s)
                pool.wait_ge(w_hi_s, 1)
                pool.tensor_tensor(w_lo[:, 0, :], raw[:, 0, 0:QKV], w_hi[:, 0, :], ALU.subtract).then_inc(w_lo_s, 1)
                pool.wait_ge(c_hi_s, 1)
                pool.tensor_tensor(c_lo[:, :], sh.ctxT[:, :], c_hi[:, :], ALU.subtract).then_inc(c_lo_s, 1)

                def rms(t, n):
                    pool.wait_ge(ms, t + 1)
                    if not (isinstance(t, int) and t < 2):
                        pool.wait_ge(qkn_s, t - 1)
                    pool.tensor_tensor(rr[:, n % 2, :], ss[:, n % 2, :], eps[:, :], ALU.add).then_inc(mse_s, 1)
                    pool.wait_ge(mse_s, t + 1)
                    pool.tensor_tensor(rr[:, n % 2, :], rr[:, n % 2, :], sh.mhalf[:, 0:8], ALU.pow).then_inc(rr_s, 1)

                pool.memset(eps[:, :], EPS).then_inc(eps_s, 1)
                pool.wait_ge(eps_s, 1)
                rms(0, 0)
                rms(1, 1)

                def step(i, n):
                    t = i * ATT_BODY + n
                    static = isinstance(i, int)
                    if static and t > NUA - 3:
                        return
                    rms(t + 2, n + 2)
                    if n % B == 1 and not (static and t > NUA - B):
                        slot = (n // B + 1) % 2
                        pool.wait_ge(w_hi_s, i * 2 + (n // B + 2))
                        pool.tensor_tensor(w_lo[:, slot, :], raw[:, slot, 0:QKV], w_hi[:, slot, :], ALU.subtract)\
                            .then_inc(w_lo_s, 1)

                steps(pool, step)

            @block.vector
            def _(dve):
                norm_vector(dve, sh, s)
                norm_lo_vector(dve, sh, s, None)
                dve.wait_ge(g_in, 32)
                dve.scalar_tensor_tensor(gg[:, :], gq[:, :], HD ** -0.5, gk[:, :], ALU.mult, ALU.mult).then_inc(gg_ready, 1)

                def mean_squares(t, n):
                    if not (isinstance(t, int) and t < 2):
                        dve.wait_ge(rr_s, t - 1)
                    dve.wait_ge(sq_s, t + 1)
                    dve.tensor_reduce(ss[:, n % 2, :], sq[:, n % 2, :].rearrange("p (a f) -> p a f", f=HD), AX_X,
                                      ALU.add).then_inc(ms, 1)

                def normed(t, n):
                    dve.wait_ge(rr_s, t + 1)
                    if not (isinstance(t, int) and t < 2):
                        dve.wait_ge(turn_ps, t - 1)
                    dve.tensor_tensor(qkn[:, n % 2, :].rearrange("p (a f) -> p a f", f=HD),
                                      sh.banks(2, 2).rearrange("p (a f) -> p a f", f=HD),
                                      rr[:, n % 2, :].unsqueeze(2).to_broadcast([P, 8, HD]), ALU.mult).then_inc(qkn_s, 1)

                def maxima(t, n):
                    for hh in range(HP):
                        dve.wait_ge(sc_ps, HP * t + hh + 1)
                        dve.tensor_reduce(nmax[:, n % 2, 2 * hh:2 * hh + 2], bank(hh).rearrange("p (a k) -> p a k", k=L),
                                          AX_X, ALU.max, negate=True).then_inc(max_s, 1)

                def normalised(t, n, hh):
                    dve.wait_ge(exp_s, HP * t + hh + 1)
                    dve.reciprocal(rinv[:, n % 2, 2 * hh:2 * hh + 2], rsum[:, n % 2, 2 * hh:2 * hh + 2]).then_inc(rinv_s, 1)
                    dve.wait_ge(rinv_s, HP * t + hh + 1)
                    for m in range(2 * hh, 2 * hh + 2):
                        ins = dve.tensor_scalar(pn[:, n % 2, m, :], pe_[:, n % 2, m, :], rinv[:, n % 2, m:m + 1], None, ALU.mult)
                    ins.then_inc(pn_s, 1)

                def first_probabilities(t, n):
                    dve.wait_ge(pT_ps, HP * t + 1)
                    if not (isinstance(t, int) and t < 2):
                        dve.wait_ge(o_ps, t - 1)
                    dve.tensor_copy(pT[:, n % 2, 0, :], bank(0)).then_inc(pT0_s, 1)

                def values_out(t, n):
                    dve.wait_ge(o_ps, t + 1)
                    if not (isinstance(t, int) and t < 2):
                        dve.wait_ge(out_ps, t - 1)
                    dve.tensor_copy(oT[:, n % 2, :], OW).then_inc(oT_s, 1)

                def residual(t, n):
                    b = n % B
                    dve.wait_ge(out_ps, t + 1)
                    xs = x[:, 2 * b:2 * b + 2, :].rearrange("p t f -> p (t f)")
                    dve.tensor_tensor(xs, xs, OW, ALU.add).then_inc(out_s, 1)

                for t in range(2):
                    mean_squares(t, t)
                    normed(t, t)

                def step(i, n):
                    t = i * ATT_BODY + n
                    static = isinstance(i, int)
                    if static and t > NUA:
                        return
                    if not (static and t >= NUA):
                        maxima(t, n)
                        for hh in range(HP):
                            normalised(t, n, hh)
                    if not (static and t > NUA - 3):
                        mean_squares(t + 2, n + 2)
                    if not (static and t == 0):
                        values_out(t - 1, n - 1)
                    if not (static and t >= NUA):
                        first_probabilities(t, n)
                    if not (static and t > NUA - 3):
                        normed(t + 2, n + 2)
                    if not (static and t == 0):
                        residual(t - 1, n - 1)

                steps(dve, step)


ATT_BODY = 2 * B
ATT_PEEL = 4
ATT_LOOPS = 3


def build(nc, d, out, stages=4):
    with ExitStack() as ctx:
        sh = Shared()

        def sb(name, shape, dt=F32):
            return ctx.enter_context(nc.sbuf_tensor(name, shape, dt))

        psum = ctx.enter_context(nc.psum_tensor("psum", [P, 8, 512], F32))
        sh.bank = lambda n: psum[:, n, :]
        sh.banks = lambda n, k: psum[:, n:n + k, :].rearrange("p b n -> p (b n)")
        sh.x = sb("x", [P, NT, DM])
        sh.xn = sb("xn", [P, NT, DM])
        sh.ident = sb("ident", [P, P])
        sh.ctxT = sb("ctxT", [P, T])
        sh.mhalf = sb("mhalf", [P, 8])
        sh.st = sb("st", [P, NT, 6])
        sh.mv = sb("mv", [P, NT, 2])
        sh.vare = sb("vare", [P, NT])
        sh.rstd = sb("rstd", [P, NT])

        mixer_block(nc, sh, d)
        sh.xT_hi = sb("xT_hi", [P, KD, T], F32R)
        sh.xT_lo = sb("xT_lo", [P, KD, T], F32R)
        if stages >= 2:
            moe_block(nc, sh, "f0", d["moe0"], d["route0"], d["scratch0"], 8, 704, 0, True, out if stages == 2 else None)
        if stages >= 3:
            attention_block(nc, sh, d)
        if stages >= 4:
            moe_block(nc, sh, "f1", d["moe1"], d["route1"], d["scratch1"], 16, 352, 4, False, out)
        if stages in (1, 3):
            stored = ctx.enter_context(nc.semaphore("stored"))
            with nc.Block() as block:
                @block.sync
                def _(sp):
                    sp.dma_start(out.rearrange("(t p) f -> p t f", p=P), sh.x[:, :, :]).then_inc(stored, 16)
                    sp.wait_ge(stored, 16)


def layout(a):
    import numpy as np

    c = np.ascontiguousarray
    a = {k: np.asarray(v) for k, v in a.items()}

    def channels(v):
        return v.reshape(G, P, -1).transpose(1, 0, 2)

    def moe(gate, up, down, n):
        pad = n * P - gate.shape[1]
        gate, up = (np.pad(w, ((0, 0), (0, pad))).reshape(KD, P, n, P).transpose(2, 1, 0, 3) for w in (gate, up))
        down = np.pad(down, ((0, pad), (0, 0))).reshape(n, P, DM)
        return c(np.concatenate([gate.reshape(n, P, -1), up.reshape(n, P, -1), down], axis=2))

    def wide(w, shared):
        return np.concatenate([w.transpose(1, 0, 2).reshape(DM, -1), shared], axis=1)

    m = "L0_xattn_"
    f = "L0_ffn_"
    q = "L1_xattn_"
    e = "L1_ffn_"
    out = {
        "ctxT": c(a["ctx_1024"].reshape(T, CD).T),
        "x": c(a["x"].reshape(T, DM)),
        "w_in": c(a[m + "in_proj_w"].T),
        "w_dt": c(np.concatenate([a[m + "dt_proj_w"].T, a[m + "dt_proj_b"][None, :]], axis=0)),
        "chan": c(channels(np.concatenate([
            a[m + "conv_w"], a[m + "conv_b"][:, None], a[m + "dt_proj_b"][:, None], a[m + "D"][:, None],
            a[m + "A_log"], a[m + "x_proj_w"].T], axis=1))),
        "ident": np.eye(P, dtype=np.float32),
        "moe0": moe(wide(a[f + "Wg"], a[f + "Sg"]), wide(a[f + "Wu"], a[f + "Su"]),
                    np.concatenate([a[f + "Wd"].reshape(-1, DM), a[f + "Sd"]], axis=0), chunks_of(8, 704)),
        "route0": c(np.concatenate([a[f + "Wr"], a[f + "Wsg"]], axis=1).reshape(KD, P, -1).transpose(1, 0, 2)),
        "moe1": moe(wide(a[e + "W1"].transpose(0, 2, 1), a[e + "Ws1"].T), wide(a[e + "W3"].transpose(0, 2, 1), a[e + "Ws3"].T),
                    np.concatenate([a[e + "W2"].transpose(0, 2, 1).reshape(-1, DM), a[e + "Ws2"].T], axis=0), chunks_of(16, 352)),
        "route1": c(a[e + "Wg"].T.reshape(KD, P, -1).transpose(1, 0, 2)),
        "gq": a[q + "gq"].reshape(HD, 1),
        "gk": a[q + "gk"].reshape(HD, 1),
    }
    pair = [a[q + "Wq"].reshape(KD, P, NPAIR, HP * HD).transpose(2, 1, 0, 3).reshape(NPAIR, P, -1),
            a[q + "Wk"].reshape(P, NPAIR, HP * HD).transpose(1, 0, 2),
            a[q + "Wv"].reshape(P, NPAIR, HP * HD).transpose(1, 0, 2),
            a[q + "Wo"].reshape(NPAIR, HP, HD, DM).transpose(0, 2, 1, 3).reshape(NPAIR, HD, -1)]
    out["w_pair"] = c(np.concatenate(pair, axis=2))
    sel = np.zeros((3, NBC, NBC, P), np.uint16)
    for r in range(NBC):
        sel[:, r, r, :] = 0x3F80
    out["sel"] = c(sel.reshape(3 * NBC, NBC, P))
    return out


def program(nc, arrays, stages=4):
    d = {name: nc.dram_tensor(f"in_{name}", v.shape, mybir.dt.from_np(v.dtype), kind="ExternalInput").ap()
         for name, v in arrays.items()}
    d["scratch0"] = nc.dram_tensor("scratch0", (9, T), F32).ap()
    d["scratch1"] = nc.dram_tensor("scratch1", (17, T), F32).ap()
    out = nc.dram_tensor("out", (T, DM), F32, kind="ExternalOutput").ap()
    build(nc, d, out, stages)


def kernel(**inputs):
    import concourse.bacc as bacc
    from concourse.bass_utils import run_bass_kernel_spmd

    arrays = layout(inputs)
    nc = bacc.Bacc("TRN2", target_bir_lowering=False, num_devices=1)
    program(nc, arrays)
    r = run_bass_kernel_spmd(nc, [{f"in_{k}": v for k, v in arrays.items()}], core_ids=[0])
    return r.results[0]["out"].reshape(B, L, DM)
```

```python
from contextlib import ExitStack

import concourse.bass as bass
from concourse import mybir

P = 128
F32 = mybir.dt.float32
F32R = mybir.dt.float32r
BF16 = mybir.dt.bfloat16
ALU = mybir.AluOpType
ACT = mybir.ActivationFunctionType
AX_X = mybir.AxisListType.X

B, L, DM = 4, 256, 256
T = B * L
NT = T // P
KD = DM // P
HALF = T // 2
TPH = HALF // P
CD = 128
EPS = 1e-5

DI, DS, DC, DR = 256, 16, 4, 8
G = DI // P
LP = L + DC - 1
NBC = 2 * DS

FE = 176
H, HD = 16, 128
HP = 2
NPAIR = H // HP

PC_CONV, PC_CB, PC_DTB, PC_D, PC_A = 0, DC, DC + 1, DC + 2, DC + 3
PC_XP = PC_A + DS
PC_N = PC_XP + DR + NBC


def shared_chunks(shared):
    return -(-shared // P)


def chunks_of(experts, shared):
    assert experts * FE % P == 0
    return shared_chunks(shared) + experts * FE // P


def segments(c):
    e = c * P // FE
    cut = (e + 1) * FE - c * P
    if cut >= P:
        return [(0, P // 2, e), (P // 2, P, e)]
    return [(0, cut, e), (cut, P, e + 1)]


class Shared:
    pass


def keep_warm(pe, sh, n, count):
    for _ in range(count):
        pe.matmul(sh.bank(n), sh.zeros[:, 0:P], sh.zeros[:, :], start=True, stop=True, skip_group_check=True)


def product3(pe, out, a, b, first, last):
    pe.matmul(out, a[0], b[0], start=first, stop=False, skip_group_check=True)
    pe.matmul(out, a[0], b[1], start=False, stop=False, skip_group_check=True)
    return pe.matmul(out, a[1], b[0], start=False, stop=last, skip_group_check=True)


def mixer_block(nc, sh, d, after):
    with ExitStack() as ctx:
        def sb(name, shape, dt=F32):
            return ctx.enter_context(nc.sbuf_tensor("m_" + name, shape, dt))

        def sem(name):
            return ctx.enter_context(nc.semaphore("m_" + name))

        x, ident, bank = sh.x, sh.ident, sh.bank
        w_in = sb("w_in", [P, DI])
        chan = sb("chan", [P, G, PC_N])
        bc_w = sb("bc_w", [P, G, 3 * NBC])
        w_dt = sb("w_dt", [DR + 1, DI])
        sel = sb("sel", [3 * NBC, NBC, P], BF16)
        xpad = sb("xpad", [P, G, B, LP])
        conv = sb("conv", [P, G, T])
        u = sb("u", [P, G, T])
        zs = sb("zs", [P, NT, L])
        st = sb("st", [P, NT, 6])
        mv = sb("mv", [P, NT, 2])
        vare = sb("vare", [P, NT])
        rstd = sb("rstd", [P, NT])
        nmr = sb("nmr", [P, NT])
        bc_hi = sb("bc_hi", [3 * NBC, T], BF16)
        bc_r = sb("bc_r", [3 * NBC, T])
        bc_r2 = sb("bc_r2", [3 * NBC, T])
        bc3 = sb("bc3", [3 * NBC, T], BF16)
        dt_lo = sb("dt_lo", [DR + 1, T])
        an = sb("an", [P, G, DS])
        ae = sb("ae", [P, G, DS])
        dgd = sb("dgd", [P, G, P])
        sp_r = sb("sp_r", [P, G, T])
        sp_e = sb("sp_e", [P, G, T])
        sp_w = sb("sp_w", [P, G, T])
        delta = sb("delta", [P, G, T])
        du = sb("du", [P, G, T])
        b_row = sb("b_row", [P, 2, T])
        da = sb("da", [P, 2, G, B, L])
        dbu = sb("dbu", [P, 2, G, T])
        hst = sb("hst", [P, 2, G, T])
        hc = (sb("hc", [P, G, T]), sp_r)
        c_row = sp_e
        yz = conv

        ctx_in = [sem(f"ctx_in{h}") for h in range(2)]
        chan_in, bc_in, dt_in, x_in, sel_in = (
            sem(n) for n in ("chan_in", "bc_in", "dt_in", "x_in", "sel_in"))
        pads, xin, xpadded, conv_step, u_ready = (
            sem(n) for n in ("pads", "xin", "xpadded", "conv_step", "u_ready"))
        ln_step, ln_var, ln_rstd, ln_shift, z_ready = (
            sem(n) for n in ("ln_step", "ln_var", "ln_rstd", "ln_shift", "z_ready"))
        bc_psum, dt_psum, bc_step, dt_ready, pre = (
            sem(n) for n in ("bc_psum", "dt_psum", "bc_step", "dt_ready", "pre"))
        sp_abs, sp_exp, sp_w_s, sp_t, sp_r_s, sp_ln = (
            sem(n) for n in ("sp_abs", "sp_exp", "sp_w_done", "sp_t_done", "sp_r_done", "sp_ln"))
        delta_ready, du_ready, a_exp, a_ready, dg_ready = (
            sem(n) for n in ("delta_ready", "du_ready", "a_exp", "a_ready", "dg_ready"))
        b_psum, c_psum, b_sb, c_sb, da_ready, dbu_ready, scanned, hc_ready, y_added = (
            sem(n) for n in ("b_psum", "c_psum", "b_sb", "c_sb", "da_ready", "dbu_ready", "scanned", "hc_ready", "y_added"))
        yz_ready, yT, x_new, c_hi_s = (sem(n) for n in ("yz_ready", "yT", "x_new", "c_hi_done"))

        with nc.Block() as block:
            @block.sync
            def _(sp):
                sp.dma_start(w_in[:, :], d["w_in"]).then_inc(ctx_in[0], 16)
                for h in range(2):
                    tok = slice(h * HALF, (h + 1) * HALF)
                    sp.dma_start(sh.ctxT[:, tok], d["ctxT"][:, tok]).then_inc(ctx_in[h], 16)
                sp.dma_start(chan[:, :, :], d["chan"]).then_inc(chan_in, 16)
                for r in range(3):
                    sp.dma_start(bc_w[:, :, r * NBC:(r + 1) * NBC],
                                 d["chan"][:, :, PC_XP + DR:PC_N]).then_inc(bc_in, 16)
                sp.dma_start(x[:, :, :], d["x"].rearrange("(t p) f -> p t f", p=P)).then_inc(x_in, 16)
                sp.dma_start(w_dt[:, :], d["w_dt"]).then_inc(dt_in, 16)
                sp.dma_start(ident[:, :], d["ident"]).then_inc(dt_in, 16)
                sp.dma_start(sel[:, :, :], d["sel"].bitcast(BF16)).then_inc(sel_in, 16)

            @block.tensor
            def _(pe):
                pe.wait_ge(pads, 1)
                keep_warm(pe, sh, 7, 4)
                for g in range(G):
                    for h in range(2):
                        pe.wait_ge(ctx_in[h], 32 if h == 0 else 16)
                        pe.matmul(bank(2 * g + h), w_in[:, g * P:(g + 1) * P],
                                  sh.ctxT[:, h * HALF:(h + 1) * HALF], start=True, stop=True).then_inc(xin, 1)
                pe.wait_ge(bc_in, 48)
                for g in range(G):
                    for h in range(2):
                        pe.wait_ge(u_ready, 2 * g + h + 1)
                        mm = pe.matmul(bank(6 + h)[0:DR, :], chan[:, g, PC_XP:PC_XP + DR],
                                       u[:, g, h * HALF:(h + 1) * HALF], start=(g == 0), stop=(g == G - 1),
                                       skip_group_check=True)
                        if g == G - 1:
                            mm.then_inc(dt_psum, 1)
                    for h in range(2):
                        mm = pe.matmul(bank(4 + h)[0:3 * NBC, :], bc_w[:, g, :], u[:, g, h * HALF:(h + 1) * HALF],
                                       start=(g == 0), stop=(g == G - 1), skip_group_check=True)
                        if g == G - 1:
                            mm.then_inc(bc_psum, 1)
                pe.wait_ge(dt_in, 32)
                pe.wait_ge(xpadded, 2 * G)
                for g in range(G):
                    for h in range(2):
                        pe.wait_ge(dt_ready, h + 1)
                        mm = pe.matmul(bank(2 * g + h), w_dt[:, g * P:(g + 1) * P], dt_lo[:, h * HALF:(h + 1) * HALF],
                                       start=True, stop=True)
                    mm.then_inc(pre, 1)

                def b_rows(n):
                    if not (isinstance(n, int) and n == 0):
                        pe.wait_ge(b_sb, n)
                    for h in range(2):
                        mm = pe.matmul(bank(4 + h), sel[:, bass.ds(n, 1), :], bc3[:, h * HALF:(h + 1) * HALF],
                                       start=True, stop=True)
                    mm.then_inc(b_psum, 1)

                def c_rows(n):
                    if not (isinstance(n, int) and n == 0):
                        pe.wait_ge(c_sb, n)
                    for h in range(2):
                        mm = pe.matmul(bank(6 + h), sel[:, bass.ds(n + DS, 1), :], bc3[:, h * HALF:(h + 1) * HALF],
                                       start=True, stop=True)
                    mm.then_inc(c_psum, 1)

                pe.wait_ge(sel_in, 16)
                pe.wait_ge(bc_step, 5)
                b_rows(0)
                c_rows(0)
                b_rows(1)
                pe.wait_ge(dg_ready, 1)
                for g in range(G):
                    pe.wait_ge(sp_abs, g + 1)
                    pe.wait_ge(sp_r_s, g + 1)
                    for h in range(2):
                        pe.matmul(bank(2 * g + h), dgd[:, g, :], u[:, g, h * HALF:(h + 1) * HALF],
                                  start=True, stop=False, skip_group_check=True)
                c_rows(1)

                def state(i, par, last=False):
                    n = i * 2 + par
                    if not last:
                        b_rows(n + 2)
                        c_rows(n + 2)
                    for g in range(G):
                        pe.wait_ge(hc_ready, n * G + (g + 1))
                        for h in range(2):
                            mm = pe.matmul(bank(2 * g + h), ident[:, :], hc[par][:, g, h * HALF:(h + 1) * HALF],
                                           start=False, stop=False, skip_group_check=True)
                        mm.then_inc(y_added, 1)

                with pe.Fori(0, DS // 2 - 1) as i:
                    for par in range(2):
                        state(i, par)
                for par in range(2):
                    state(DS // 2 - 1, par, last=True)
                for g in range(G):
                    pe.wait_ge(yz_ready, g + 1)
                    for t in range(NT):
                        b, lc = t // 2, t % 2
                        mm = pe.transpose(bank(4 + t // 2)[:, (t % 2) * DM + g * P:(t % 2) * DM + (g + 1) * P],
                                          yz[:, g, b * L + lc * P:b * L + (lc + 1) * P], ident[:, :])
                        if g == G - 1:
                            mm.then_inc(yT, 1)

            @block.scalar
            def _(act):
                for g in range(G):
                    for h in range(2):
                        act.wait_ge(xin, 2 * g + h + 1)
                        act.activation(xpad[:, g, 2 * h:2 * h + 2, DC - 1:LP],
                                       bank(2 * g + h).rearrange("p (b l) -> p b l", b=2),
                                       ACT.Copy).then_inc(xpadded, 1)
                act.activation(sh.c_hi[:, :], sh.ctxT[:, :], ACT.Copy).then_inc(c_hi_s, 1)
                for g in range(G):
                    for h in range(2):
                        tok = slice(h * HALF, (h + 1) * HALF)
                        act.wait_ge(conv_step, DC * (2 * g + h + 1))
                        act.activation(u[:, g, tok], conv[:, g, tok], ACT.Silu, bias=chan[:, g, PC_CB:PC_CB + 1])\
                            .then_inc(u_ready, 1)
                act.wait_ge(pads, 7)
                for h in range(2):
                    act.wait_ge(dt_psum, h + 1)
                    act.activation(dt_lo[0:DR, h * HALF:(h + 1) * HALF], bank(6 + h)[0:DR, :], ACT.Copy).then_inc(dt_ready, 1)
                for g in range(G):
                    act.wait_ge(pre, g + 1)
                    act.activation(sp_e[:, g, :], sh.banks(2 * g, 2), ACT.Abs).then_inc(sp_abs, 1)
                    act.wait_ge(sp_abs, g + 1)
                    act.activation(sp_e[:, g, :], sp_e[:, g, :], ACT.Exp, scale=-1.0).then_inc(sp_exp, 1)
                act.activation(ae[:, :, :], chan[:, :, PC_A:PC_A + DS], ACT.Exp).then_inc(a_exp, 1)
                for g in range(G):
                    act.wait_ge(sp_w_s, g + 1)
                    act.activation(delta[:, g, :], sp_w[:, g, :], ACT.Ln).then_inc(sp_ln, 1)
                for n in range(2):
                    act.wait_ge(b_psum, n + 1)
                    act.activation(b_row[:, n, :], sh.banks(4, 2), ACT.Copy).then_inc(b_sb, 1)

                act.wait_ge(a_ready, 1)
                def state(i, par, first=False):
                    n = i * 2 + par
                    if not first:
                        act.wait_ge(b_psum, n + 1)
                        act.wait_ge(dbu_ready, n * G - G)
                        act.activation(b_row[:, par, :], sh.banks(4, 2), ACT.Copy).then_inc(b_sb, 1)
                    for g in range(G):
                        if first:
                            act.wait_ge(delta_ready, g + 1)
                        else:
                            act.wait_ge(scanned, n * G - (2 * G - g - 1))
                        act.activation(da[:, par, g, :, 1:L],
                                       delta[:, g, :].rearrange("p (b l) -> p b l", b=B)[:, :, 1:L], ACT.Exp,
                                       scale=an[:, g, bass.ds(n, 1)]).then_inc(da_ready, 1)
                    act.wait_ge(c_psum, n + 1)
                    if not first:
                        act.wait_ge(hc_ready, n * G - G)
                    act.activation(c_row[:, par, :], sh.banks(6, 2), ACT.Copy).then_inc(c_sb, 1)

                for par in range(2):
                    state(0, par, first=True)
                with act.Fori(1, DS // 2) as i:
                    for par in range(2):
                        state(i, par)
                act.wait_ge(ln_shift, 1)
                for t in range(NT):
                    ins = act.activation(zs[:, t, :], x[:, t, :], ACT.Silu, bias=nmr[:, t:t + 1], scale=rstd[:, t:t + 1])
                ins.then_inc(z_ready, 1)

            @block.gpsimd
            def _(pool):
                pool.wait_ge(c_hi_s, 1)
                pool.tensor_tensor(sh.c_lo[:, :], sh.ctxT[:, :], sh.c_hi[:, :], ALU.subtract)
                pool.wait_ge(ln_var, 1)
                pool.tensor_tensor(rstd[:, :], vare[:, :], sh.mhalf[:, 0:NT], ALU.pow).then_inc(ln_rstd, 1)

                def state(i, par, first=False):
                    n = i * 2 + par
                    pool.wait_ge(b_sb, n + 1)
                    for g in range(G):
                        if first:
                            pool.wait_ge(du_ready, g + 1)
                        else:
                            pool.wait_ge(scanned, n * G - (2 * G - g - 1))
                        pool.tensor_tensor(dbu[:, par, g, :], du[:, g, :], b_row[:, par, :], ALU.mult).then_inc(dbu_ready, 1)

                for par in range(2):
                    state(0, par, first=True)
                with pool.Fori(1, DS // 2) as i:
                    for par in range(2):
                        state(i, par)
                norm_deviation(pool, sh, after, 0)

            @block.vector
            def _(dve):
                dve.memset(sh.zeros[:, :], 0.0).then_inc(pads, 1)
                dve.memset(sh.mhalf[:, :], -0.5).then_inc(pads, 1)
                dve.memset(sh.eps[:, :], EPS).then_inc(pads, 1)
                dve.memset(xpad[:, :, :, 0:DC - 1], 0.0).then_inc(pads, 1)
                for n in range(2):
                    dve.memset(da[:, n, :, :, 0:1], 0.0).then_inc(pads, 1)
                dve.memset(dt_lo[:, :], 1.0).then_inc(pads, 1)

                def tap(g, h, j):
                    src = xpad[:, g, 2 * h:2 * h + 2, j:j + L]
                    out = conv[:, g, h * HALF:(h + 1) * HALF].rearrange("p (b l) -> p b l", b=2)
                    w = chan[:, g, PC_CONV + j:PC_CONV + j + 1]
                    if j == 0:
                        dve.tensor_scalar(out, src, w, None, ALU.mult).then_inc(conv_step, 1)
                    else:
                        dve.wait_ge(conv_step, DC * (2 * g + h) + j)
                        dve.scalar_tensor_tensor(out, src, w, out, ALU.mult, ALU.add).then_inc(conv_step, 1)

                dve.wait_ge(pads, 7)
                dve.wait_ge(chan_in, 16)
                for g in range(G):
                    for h in range(2):
                        dve.wait_ge(xpadded, 2 * g + h + 1)
                        for j in range(DC):
                            tap(g, h, j)
                dve.wait_ge(x_in, 16)
                for t in range(NT):
                    dve.bn_stats(st[:, t, :], x[:, t, :]).then_inc(ln_step, 1)
                for t in range(NT):
                    dve.wait_ge(ln_step, t + 1)
                    dve.bn_aggr(mv[:, t, :], st[:, t, :]).then_inc(ln_step, 1)
                dve.wait_ge(ln_step, 2 * NT)
                dve.tensor_scalar(vare[:, :], mv[:, :, 1], EPS, None, ALU.add).then_inc(ln_var, 1)
                dve.wait_ge(dt_in, 32)
                for g in range(G):
                    ins = dve.tensor_scalar(dgd[:, g, :], ident[:, :], chan[:, g, PC_D:PC_D + 1], None, ALU.mult)
                ins.then_inc(dg_ready, 1)

                dve.wait_ge(bc_psum, 2)
                v = sh.banks(4, 2)[0:3 * NBC, :]
                dve.tensor_copy(bc_hi[:, :], v).then_inc(bc_step, 1)
                dve.wait_ge(bc_step, 1)
                dve.tensor_tensor(bc_r[:, :], v, bc_hi[:, :], ALU.subtract).then_inc(bc_step, 1)
                dve.wait_ge(bc_step, 2)
                dve.tensor_copy(bc3[:, :], bc_r[:, :]).then_inc(bc_step, 1)
                dve.wait_ge(bc_step, 3)
                dve.tensor_copy(bc3[0:NBC, :], bc_hi[0:NBC, :]).then_inc(bc_step, 1)
                dve.tensor_tensor(bc3[2 * NBC:3 * NBC, :], bc_r[2 * NBC:3 * NBC, :], bc3[2 * NBC:3 * NBC, :],
                                  ALU.subtract).then_inc(bc_step, 1)

                def w_part(g):
                    dve.wait_ge(sp_exp, g + 1)
                    dve.tensor_scalar(sp_w[:, g, :], sp_e[:, g, :], 1.0, None, ALU.add).then_inc(sp_w_s, 1)

                def t_part(g):
                    dve.wait_ge(sp_w_s, g + 1)
                    dve.scalar_tensor_tensor(sp_e[:, g, :], sp_w[:, g, :], -1.0, sp_e[:, g, :],
                                             ALU.add, ALU.subtract).then_inc(sp_t, 1)

                def r_part(g):
                    dve.wait_ge(sp_t, g + 1)
                    dve.scalar_tensor_tensor(sp_r[:, g, :], sh.banks(2 * g, 2), 0.0, sp_e[:, g, :],
                                             ALU.max, ALU.subtract).then_inc(sp_r_s, 1)

                def delta_part(g):
                    dve.wait_ge(sp_r_s, g + 1)
                    dve.wait_ge(sp_ln, g + 1)
                    dve.tensor_tensor(delta[:, g, :], delta[:, g, :], sp_r[:, g, :], ALU.add).then_inc(delta_ready, 1)
                    dve.wait_ge(delta_ready, g + 1)
                    dve.wait_ge(u_ready, 2 * G)
                    dve.tensor_tensor(du[:, g, :], delta[:, g, :], u[:, g, :], ALU.mult).then_inc(du_ready, 1)

                w_part(0)
                t_part(0)
                w_part(1)
                dve.wait_ge(a_exp, 1)
                dve.tensor_scalar(an[:, :, :], ae[:, :, :], -1.0, None, ALU.mult).then_inc(a_ready, 1)
                r_part(0)
                t_part(1)
                delta_part(0)
                r_part(1)
                delta_part(1)

                dve.wait_ge(ln_rstd, 1)
                dve.scalar_tensor_tensor(nmr[:, :], mv[:, :, 0], -1.0, rstd[:, :], ALU.mult, ALU.mult).then_inc(ln_shift, 1)

                def states(i, first=False):
                    for par in range(2):
                        n = i * 2 * G
                        for g in range(G):
                            dve.wait_ge(da_ready, n + (par * G + g + 1))
                            dve.wait_ge(dbu_ready, n + (par * G + g + 1))
                            dve.tensor_tensor_scan(hst[:, par, g, :], da[:, par, g, :, :].rearrange("p b l -> p (b l)"),
                                                   dbu[:, par, g, :], 0.0, ALU.mult, ALU.add).then_inc(scanned, 1)
                        dve.wait_ge(c_sb, i * 2 + (par + 1))
                        for g in range(G):
                            dve.wait_ge(scanned, n + (par * G + g + 1))
                            if not first:
                                dve.wait_ge(y_added, n + (par * G - 2 * G + g + 1))
                            dve.tensor_tensor(hc[par][:, g, :], hst[:, par, g, :], c_row[:, par, :], ALU.mult)\
                                .then_inc(hc_ready, 1)

                states(0, first=True)
                with dve.Fori(1, DS // 2) as i:
                    states(i)

                dve.wait_ge(z_ready, 1)
                for g in range(G):
                    dve.wait_ge(y_added, G * DS - G + g + 1)
                    z = zs[:, :, :].rearrange("p (b g) l -> p b g l", g=G)[:, :, g, :]
                    dve.tensor_tensor(yz[:, g, :].rearrange("p (b l) -> p b l", b=B),
                                      sh.banks(2 * g, 2).rearrange("p (b l) -> p b l", b=B),
                                      z, ALU.mult).then_inc(yz_ready, 1)
                for q in range(NT // 2):
                    dve.wait_ge(yT, 2 * q + 2)
                    xs = x[:, 2 * q:2 * q + 2, :].rearrange("p t f -> p (t f)")
                    dve.tensor_tensor(xs, xs, bank(4 + q), ALU.add).then_inc(x_new, 1)
                    if q == 1:
                        dve.wait_ge(x_new, 2)
                        norm_statistics(dve, sh, after, 0)


class NormSems:

    def __init__(self, sem, routed):
        self.step, self.var, self.rstd, self.normed, self.turned, self.hi, self.lo = (
            sem(n) for n in ("step", "var", "rstd", "normed", "turned", "hi", "lo"))
        if routed:
            self.full = sem("full")


def norm_statistics(dve, sh, s, h):
    tiles = range(h * TPH, (h + 1) * TPH)
    for t in tiles:
        dve.bn_stats(sh.st[:, t, :], sh.x[:, t, :]).then_inc(s.step, 1)
    for n, t in enumerate(tiles):
        dve.wait_ge(s.step, 2 * TPH * h + n + 1)
        dve.bn_aggr(sh.mv[:, t, :], sh.st[:, t, :]).then_inc(s.step, 1)
    dve.wait_ge(s.step, 2 * TPH * (h + 1))
    dve.tensor_scalar(sh.vare[:, h * TPH:(h + 1) * TPH], sh.mv[:, h * TPH:(h + 1) * TPH, 1], EPS, None,
                      ALU.add).then_inc(s.var, 1)


def norm_deviation(pool, sh, s, h):
    pool.wait_ge(s.var, h + 1)
    pool.tensor_tensor(sh.rstd[:, h * TPH:(h + 1) * TPH], sh.vare[:, h * TPH:(h + 1) * TPH],
                       sh.mhalf[:, 0:TPH], ALU.pow).then_inc(s.rstd, 1)


def norm_vector(dve, sh, s):
    norm_statistics(dve, sh, s, 1)
    for h in range(2):
        dve.wait_ge(s.rstd, h + 1)
        for t in range(h * TPH, (h + 1) * TPH):
            dve.tensor_scalar(sh.xn[:, t, :], sh.x[:, t, :], sh.mv[:, t, 0:1], sh.rstd[:, t:t + 1],
                              ALU.subtract, ALU.mult).then_inc(s.normed, 1)


def norm_tensor(pe, sh, s):
    keep_warm(pe, sh, 0, 12)
    for h in range(2):
        for k in range(KD):
            for t in range(h * TPH, (h + 1) * TPH):
                pe.wait_ge(s.normed, t + 1)
                mm = pe.transpose(sh.bank(4 + KD * h + k)[:, (t % TPH) * P:(t % TPH + 1) * P],
                                  sh.xn[:, t, k * P:(k + 1) * P], sh.ident[:, :])
            mm.then_inc(s.turned, 1)


def norm_scalar(act, sh, s, full=None):
    for h in range(2):
        tok = slice(h * HALF, (h + 1) * HALF)
        for k in range(KD):
            act.wait_ge(s.turned, KD * h + k + 1)
            act.activation(sh.xT_hi[:, k, tok], sh.bank(4 + KD * h + k), ACT.Copy).then_inc(s.hi, 1)
            if full is not None:
                act.activation(full[:, k, tok], sh.bank(4 + KD * h + k), ACT.Copy).then_inc(s.full, 1)


def norm_lo_vector(dve, sh, s, full=None):
    for h in range(2):
        tok = slice(h * HALF, (h + 1) * HALF)
        for k in range(KD):
            dve.wait_ge(s.hi if full is None else s.full, KD * h + k + 1)
            whole = sh.bank(4 + KD * h + k) if full is None else full[:, k, tok]
            dve.tensor_tensor(sh.xT_lo[:, k, tok], whole, sh.xT_hi[:, k, tok], ALU.subtract).then_inc(s.lo, 1)


GU = 2 * KD * P
WCH = GU + DM
HS = 4


def moe_block(nc, sh, tag, s, after, weights, router, scratch, experts, shared, groups, gated, out):
    NC = chunks_of(experts, shared)
    NU = 2 * NC
    SC = shared_chunks(shared)
    ER = experts + (1 if gated else 0)
    SP = -(-SC // 2)
    assert NC % 2 == 1 and SC >= 3
    with ExitStack() as ctx:
        def sb(name, shape, dt=F32):
            return ctx.enter_context(nc.sbuf_tensor(f"{tag}_{name}", shape, dt))

        def sem(name):
            return ctx.enter_context(nc.semaphore(f"{tag}_{name}"))

        bank, ident, x = sh.bank, sh.ident, sh.x
        raw = sb("raw", [P, 2, WCH])
        gu_hi = sb("gu_hi", [P, 2, GU], F32R)
        gu_lo = sb("gu_lo", [P, 2, GU], F32R)
        dn_hi = sb("dn_hi", [P, 2, DM], F32R)
        dn_lo = sb("dn_lo", [P, 2, DM], F32R)
        comb = sb("comb", [P, 2, T])
        sg = sb("sg", [P, HS, HALF])
        su = sb("su", [P, HS, HALF])
        hid = sb("hid", [P, HS, HALF])
        h_hi = sb("h_hi", [P, HS, HALF], F32R)
        h_lo = sb("h_lo", [P, HS, HALF], F32R)
        xT = sb("xT", [P, KD, T])
        wr = sb("wr", [P, KD, ER])
        lg = sb("lg", [P, NT, experts])
        neg = sb("neg", [P, NT])
        ex = sb("ex", [P, NT, experts])
        den = sb("den", [P, NT])
        pr = sb("pr", [P, NT, 16])
        top = sb("top", [P, NT, 8])
        left = sb("left", [P, NT, 16])
        gs = sb("gs", [P, NT, 16])
        gtop = sb("gtop", [P, NT, 8])
        gleft = sb("gleft", [P, NT, 16])
        gmask = sb("gmask", [P, NT, 4])
        gminus = sb("gminus", [P, NT, 4])
        msk = sb("msk", [P, NT, 16])
        cw = sb("cw", [P, NT, experts])
        cT = sb("cT", [NT * experts, P])
        gw_hi = sb("gw_hi", [P, KD, P], F32R)
        gw_lo = sb("gw_lo", [P, KD, P], F32R)

        wr_in, logits, route, ex_ready, cw_ready, cT_psum, cT_ready, cT_out = (
            sem(n) for n in ("wr_in", "logits", "route", "ex_ready", "cw_ready", "cT_psum", "cT_ready", "cT_out"))
        raw_in = [sem(f"raw_in{i}") for i in range(2)]
        comb_in = [sem(f"comb_in{i}") for i in range(2)]
        gu_hi_s, gu_lo_s, dn_hi_s, dn_lo_s = (sem(n) for n in ("gu_hi_done", "gu_lo_done", "dn_hi_done", "dn_lo_done"))
        gate_ps, up_ps, silu_s, su_s, hid_s, h_hi_s, h_lo_s, down_s = (
            sem(n) for n in ("gate_ps", "up_ps", "silu_done", "su_done", "hid_done", "h_hi_done", "h_lo_done", "down_done"))
        shared_ready = sem("shared_ready")
        if gated:
            gw_ready, gate_logit = sem("gw_ready"), sem("gate_logit")
        x_back = sem("x_back")
        if out is not None:
            stored = sem("stored")

        def gate_bank(half):
            return bank(4 + 2 * half)

        def up_bank(half):
            return bank(5 + 2 * half)

        with nc.Block() as block:
            def broadcast(sp, c):
                sp.wait_ge(hid_s, 2 * (c - 2) + 2)
                for a, b, e in segments(c - SC):
                    sp.dma_start(comb[a:b, c % 2, :], scratch[e:e + 1, :].to_broadcast([b - a, T])).then_inc(comb_in[c % 2], 16)

            @block.sync
            def _(sp):
                sp.dma_start(wr[:, :, :], router).then_inc(wr_in, 16)
                for c in range(NC):
                    if c >= 2:
                        sp.wait_ge(dn_lo_s, c - 1)
                    sp.dma_start(raw[:, c % 2, :], weights[c]).then_inc(raw_in[c % 2], 16)
                    if c == 3:
                        sp.wait_ge(cT_ready, 1)
                        for t in range(NT):
                            sp.dma_start(scratch[:, t * P:(t + 1) * P],
                                         cT[t * experts:(t + 1) * experts, :]).then_inc(cT_out, 16)
                        sp.wait_ge(cT_out, 16 * NT)
                    if c >= SC:
                        broadcast(sp, c)
                if out is not None:
                    for q in range(NT // 2):
                        sp.wait_ge(x_back, q + 1)
                        sp.dma_start(out.rearrange("(t p) f -> p t f", p=P)[:, 2 * q:2 * q + 2, :],
                                     x[:, 2 * q:2 * q + 2, :]).then_inc(stored, 16)
                    sp.wait_ge(stored, 16 * (NT // 2))

            @block.tensor
            def _(pe):
                norm_tensor(pe, sh, s)
                def gate_up(j, slot, half):
                    tok = slice(half * HALF, (half + 1) * HALF)
                    for what, (dst, done) in enumerate(((gate_bank(half), gate_ps), (up_bank(half), up_ps))):
                        for k in range(KD):
                            w = slice((what * KD + k) * P, (what * KD + k + 1) * P)
                            mm = product3(pe, dst, (gu_hi[:, slot, w], gu_lo[:, slot, w]),
                                          (sh.xT_hi[:, k, tok], sh.xT_lo[:, k, tok]), k == 0, k == KD - 1)
                        mm.then_inc(done, 1)

                def down(slot, hslot, half, first=False):
                    for n in range(TPH):
                        t = half * TPH + n
                        tok = slice(n * P, (n + 1) * P)
                        mm = product3(pe, bank(t // 2)[:, (t % 2) * DM:(t % 2 + 1) * DM],
                                      (h_hi[:, hslot, tok], h_lo[:, hslot, tok]),
                                      (dn_hi[:, slot, :], dn_lo[:, slot, :]), first and t % 2 == 0, False)
                    mm.then_inc(down_s, 1)

                pe.wait_ge(gu_lo_s, 1)
                pe.wait_ge(s.lo, KD)
                pe.wait_ge(s.full, KD)
                gate_up(0, 0, 0)
                pe.wait_ge(s.lo, 2 * KD)
                if gated:
                    pe.wait_ge(gw_ready, 2)
                    for h in range(2):
                        tok = slice(h * HALF, (h + 1) * HALF)
                        for k in range(KD):
                            mm = product3(pe, bank(2 + h), (gw_hi[:, k, :], gw_lo[:, k, :]),
                                          (sh.xT_hi[:, k, tok], sh.xT_lo[:, k, tok]), k == 0, k == KD - 1)
                    mm.then_inc(gate_logit, 1)
                gate_up(1, 0, 1)
                pe.wait_ge(wr_in, 16)
                for t in range(NT):
                    pe.wait_ge(s.full, KD * (t // TPH + 1))
                    for k in range(KD):
                        mm = pe.matmul(bank(0)[:, t * experts:(t + 1) * experts], xT[:, k, t * P:(t + 1) * P],
                                       wr[:, k, 0:experts], start=(k == 0), stop=(k == KD - 1))
                mm.then_inc(logits, 1)

                def step(i, q):
                    half, slot = q % 2, (q // 2 + 1) % 2
                    j = i * HS + q
                    first = isinstance(i, int)
                    if half == 0:
                        pe.wait_ge(gu_lo_s, i * 2 + q // 2 + 2)
                    pe.wait_ge(silu_s, j + 1)
                    pe.wait_ge(su_s, j + 1)
                    if first and q == 3:
                        pe.wait_ge(cw_ready, 1)
                        pe.transpose(gate_bank(1)[0:NT * experts, 0:P], cw[:, :, :].rearrange("p t e -> p (t e)"),
                                     ident[:, :]).then_inc(cT_psum, 1)
                        pe.wait_ge(cT_ready, 1)
                    gate_up(None, slot, half)
                    pe.wait_ge(h_lo_s, j + 1)
                    pe.wait_ge(dn_lo_s, i * 2 + q // 2 + 1)
                    if first and q == 0:
                        pe.wait_ge(route, 1)
                    down(q // 2, q, half, first and q < 2)

                for q in range(HS):
                    step(0, q)
                with pe.Fori(1, (NU - 2) // HS) as i:
                    for q in range(HS):
                        step(i, q)
                for q in range(2):
                    j = NU - 2 + q
                    pe.wait_ge(h_lo_s, j + 1)
                    pe.wait_ge(dn_lo_s, NC)
                    down((NC - 1) % 2, j % HS, q)

            @block.scalar
            def _(act):
                act.wait_ge(raw_in[0], 16)
                act.activation(gu_hi[:, 0, :], raw[:, 0, 0:GU], ACT.Copy).then_inc(gu_hi_s, 1)
                norm_scalar(act, sh, s, xT)

                def shared_gate():
                    if gated:
                        act.wait_ge(gate_logit, 1)
                        for par in range(2):
                            act.activation(comb[:, par, :], sh.banks(2, 2), ACT.Sigmoid).then_inc(shared_ready, 1)

                def chunk(c, par, pair, first=False, last=False):
                    for half in range(2):
                        j = 2 * c + half
                        hs = 2 * par + half
                        act.wait_ge(gate_ps, j + 1)
                        if not first:
                            act.wait_ge(su_s, j - HS + 1)
                        if first and par == 0 and half == 1:
                            hi_part(0, 0, True)
                        act.activation(sg[:, hs, :], gate_bank(half), ACT.Silu).then_inc(silu_s, 1)
                        if first and par == 1 and half == 1:
                            hi_part(j - 1, hs - 1, True)
                        if half == 0:
                            if not last:
                                act.wait_ge(raw_in[(par + 1) % 2], (pair + (par + 1) // 2) * 16 + 16)
                                if not (first and par == 0):
                                    act.wait_ge(up_ps, 2 * c)
                                act.activation(gu_hi[:, (par + 1) % 2, :], raw[:, (par + 1) % 2, 0:GU],
                                               ACT.Copy).then_inc(gu_hi_s, 1)
                            if not first:
                                act.wait_ge(down_s, 2 * c - 2)
                            act.activation(dn_hi[:, par, :], raw[:, par, GU:WCH], ACT.Copy).then_inc(dn_hi_s, 1)
                        if first and par == 0 and half == 0:
                            shared_gate()
                        elif not (first and half == 0):
                            hi_part(j, hs, first)
                        if first and par == 0 and half == 1:
                            act.wait_ge(route, 3)
                            act.activation(ex[:, :, :], ex[:, :, :], ACT.Exp).then_inc(ex_ready, 1)
                        if first and par == 1 and half == 1:
                            act.wait_ge(cT_psum, 1)
                            act.activation(cT[:, :], gate_bank(1)[0:NT * experts, 0:P], ACT.Copy).then_inc(cT_ready, 1)

                def hi_part(j, hs, first):
                    act.wait_ge(hid_s, j + 1)
                    if not first:
                        act.wait_ge(down_s, j - HS + 1)
                    act.activation(h_hi[:, hs, :], hid[:, hs, :], ACT.Copy).then_inc(h_hi_s, 1)

                for par in range(2):
                    chunk(par, par, 0, first=True)
                with act.Fori(1, NC // 2) as i:
                    for par in range(2):
                        chunk(2 * i + par, par, i)
                chunk(NC - 1, 0, NC // 2, last=True)

            @block.gpsimd
            def _(pool):
                norm_deviation(pool, sh, s, 1)

                def lo_part(out, whole, hi):
                    return pool.tensor_tensor(out, whole, hi, ALU.subtract)

                pool.wait_ge(gu_hi_s, 1)
                lo_part(gu_lo[:, 0, :], raw[:, 0, 0:GU], gu_hi[:, 0, :]).then_inc(gu_lo_s, 1)
                if not gated:
                    pool.memset(comb[:, :, :], 1.0).then_inc(shared_ready, 1)

                def chunk(c, par, last=False):
                    if not last:
                        pool.wait_ge(gu_hi_s, c + 2)
                        lo_part(gu_lo[:, (par + 1) % 2, :], raw[:, (par + 1) % 2, 0:GU],
                                gu_hi[:, (par + 1) % 2, :]).then_inc(gu_lo_s, 1)
                    pool.wait_ge(dn_hi_s, c + 1)
                    lo_part(dn_lo[:, par, :], raw[:, par, GU:WCH], dn_hi[:, par, :]).then_inc(dn_lo_s, 1)
                    for half in range(2):
                        pool.wait_ge(h_hi_s, 2 * c + half + 1)
                        hs = 2 * par + half
                        lo_part(h_lo[:, hs, :], hid[:, hs, :], h_hi[:, hs, :]).then_inc(h_lo_s, 1)

                with pool.Fori(0, NC // 2) as i:
                    for par in range(2):
                        chunk(2 * i + par, par)
                chunk(NC - 1, 0, last=True)
                if after is not None:
                    norm_deviation(pool, sh, after, 0)

            @block.vector
            def _(dve):
                norm_vector(dve, sh, s)
                if gated:
                    dve.wait_ge(wr_in, 16)
                    gate_w = wr[:, :, experts:ER].to_broadcast([P, KD, P])
                    dve.tensor_copy(gw_hi[:, :, :], gate_w).then_inc(gw_ready, 1)
                    dve.wait_ge(gw_ready, 1)
                    dve.tensor_tensor(gw_lo[:, :, :], gate_w, gw_hi[:, :, :], ALU.subtract).then_inc(gw_ready, 1)
                norm_lo_vector(dve, sh, s, xT)

                steps = [0]

                def step(ins):
                    steps[0] += 1
                    ins.then_inc(route, 1)
                    dve.wait_ge(route, steps[0])

                def spread(v, n):
                    return v.unsqueeze(2).to_broadcast([P, NT, n])

                def route_logits():
                    dve.wait_ge(logits, 1)
                    step(dve.tensor_copy(lg[:, :, :], bank(0)[:, 0:NT * experts].rearrange("p (t e) -> p t e", t=NT)))
                    step(dve.tensor_reduce(neg[:, :], lg[:, :, :], AX_X, ALU.max))
                    step(dve.tensor_tensor(ex[:, :, :], lg[:, :, :], spread(neg[:, :], experts), ALU.subtract))

                def route_groups():
                    dve.wait_ge(ex_ready, 1)
                    step(dve.tensor_reduce(den[:, :], ex[:, :, :], AX_X, ALU.add))
                    step(dve.reciprocal(den[:, :], den[:, :]))
                    if experts < 16:
                        step(dve.memset(pr[:, :, experts:16], -1.0))
                    step(dve.tensor_tensor(pr[:, :, 0:experts], ex[:, :, :], spread(den[:, :], experts), ALU.mult))
                    if groups:
                        per = experts // groups
                        step(dve.memset(gs[:, :, groups:16], -1.0))
                        step(dve.tensor_reduce(gs[:, :, 0:groups], pr[:, :, :].rearrange("p t (g e) -> p (t g) e", g=groups),
                                               AX_X, ALU.max))
                        for t in range(NT):
                            ins = dve.max(gtop[:, t, :], gs[:, t, :])
                        step(ins)
                        step(dve.memset(gtop[:, :, 2:8], -1.0))
                        for t in range(NT):
                            ins = dve.match_replace(gleft[:, t, :], gtop[:, t, :], gs[:, t, :], -2.0)
                        step(ins)
                        step(dve.tensor_scalar(gmask[:, :, :], gleft[:, :, 0:groups], -2.0, None, ALU.is_equal))
                        step(dve.tensor_scalar(gminus[:, :, :], gmask[:, :, :], -1.0, None, ALU.add))
                        for dst, a, b, op in ((msk, pr, gmask, ALU.mult), (msk, msk, gminus, ALU.add)):
                            v = [y[:, :, :].rearrange("p t (g e) -> p (t g) e", g=groups) for y in (dst, a)]
                            m = b[:, :, :].rearrange("p t g -> p (t g)").unsqueeze(2).to_broadcast([P, NT * groups, per])
                            step(dve.tensor_tensor(v[0], v[1], m, op))

                def route_pick():
                    pick, k = (msk, 4) if groups else (pr, 2)
                    for t in range(NT):
                        ins = dve.max(top[:, t, :], pick[:, t, :])
                    step(ins)
                    step(dve.memset(top[:, :, k:8], -1.0))
                    for t in range(NT):
                        ins = dve.match_replace(left[:, t, :], top[:, t, :], pick[:, t, :], -2.0)
                    step(ins)
                    step(dve.tensor_scalar(left[:, :, :], left[:, :, :], -2.0, None, ALU.is_equal))
                    dve.scalar_tensor_tensor(cw[:, :, :], pick[:, :, 0:experts], 0.0, left[:, :, 0:experts],
                                             ALU.max, ALU.mult).then_inc(cw_ready, 1)

                def gated_up(j, hs, half):
                    dve.wait_ge(silu_s, j + 1)
                    dve.wait_ge(up_ps, j + 1)
                    dve.tensor_tensor(su[:, hs, :], sg[:, hs, :], up_bank(half), ALU.mult).then_inc(su_s, 1)

                def combined(j, par, pair, half, first=False):
                    dve.wait_ge(su_s, j + 1)
                    if isinstance(pair, int) and 2 * pair + par < SC:
                        dve.wait_ge(shared_ready, 2 if gated else 1)
                    else:
                        dve.wait_ge(comb_in[par], pair * 32 + (32 - 32 * ((SC - par + 1) // 2)))
                    if not first:
                        dve.wait_ge(h_lo_s, j - HS + 1)
                    dve.tensor_tensor(hid[:, 2 * par + half, :], su[:, 2 * par + half, :],
                                      comb[:, par, half * HALF:(half + 1) * HALF], ALU.mult).then_inc(hid_s, 1)

                def pair_of_chunks(i, chunks, first=False):
                    for par in range(chunks):
                        for half in range(2):
                            j = i * HS + 2 * par + half
                            gated_up(j, 2 * par + half, half)
                            combined(j, par, i, half, first)
                            if first and j == 1:
                                route_logits()
                                route_groups()
                            if first and j == 3:
                                route_pick()

                for i in range(SP):
                    pair_of_chunks(i, 2, first=(i == 0))
                with dve.Fori(SP, NC // 2) as i:
                    pair_of_chunks(i, 2)
                pair_of_chunks(NC // 2, 1)
                for q in range(NT // 2):
                    dve.wait_ge(down_s, NU - 1 + q // 2)
                    xs = x[:, 2 * q:2 * q + 2, :].rearrange("p t f -> p (t f)")
                    dve.tensor_tensor(xs, xs, bank(q), ALU.add).then_inc(x_back, 1)
                    if q == 1 and after is not None:
                        dve.wait_ge(x_back, 2)
                        norm_statistics(dve, sh, after, 0)


QKV = (KD + 2) * HP * HD
WPAIR = QKV + HP * DM
NUA = NPAIR * B
UW = HP * L


def attention_block(nc, sh, d, s, after):
    with ExitStack() as ctx:
        def sb(name, shape, dt=F32):
            return ctx.enter_context(nc.sbuf_tensor("a_" + name, shape, dt))

        def sem(name):
            return ctx.enter_context(nc.semaphore("a_" + name))

        bank, ident, x = sh.bank, sh.ident, sh.x
        raw = sb("raw", [P, 2, WPAIR])
        w_hi = sb("w_hi", [P, 2, QKV], F32R)
        w_lo = sb("w_lo", [P, 2, QKV], F32R)
        gq = sb("gq", [HD, 1])
        gk = sb("gk", [HD, 1])
        gg = sb("gg", [HD, 1])
        sq = sb("sq", [P, 2, 2 * UW])
        ss = sb("ss", [P, 2, 8])
        rr = sb("rr", [P, 2, 8])
        qkn = sb("qkn", [P, 2, 2 * UW])
        qT = sb("qT", [P, 2, UW])
        kT = sb("kT", [P, 2, UW])
        o_hi = sb("o_hi", [P, 2, HP * DM], F32R)
        o_lo = sb("o_lo", [P, 2, HP * DM], F32R)
        v = sb("v", [P, 2, UW])
        v_hi = sb("v_hi", [P, 4, UW], F32R)
        v_lo = sb("v_lo", [P, 4, UW], F32R)
        nmax = sb("nmax", [P, 2, 4])
        rsum = sb("rsum", [P, 2, 4])
        rinv = sb("rinv", [P, 2, 4])
        pe_ = sb("p_exp", [P, 2, 4, L])
        pn = sb("p_norm", [P, 2, 4, L])
        pT_hi = sb("pT_hi", [P, 2, HP, UW], F32R)
        pT_lo = sb("pT_lo", [P, 2, HP, UW], F32R)
        oT_hi = sb("oT_hi", [P, 2, UW], F32R)
        oT_lo = sb("oT_lo", [P, 2, UW], F32R)

        g_in, gg_ready = sem("g_in"), sem("gg_ready")
        raw_in = [sem(f"raw_in{i}") for i in range(2)]
        w_hi_s, w_lo_s, wo_hi_s, wo_lo_s = (sem(n) for n in ("w_hi_done", "w_lo_done", "wo_hi_done", "wo_lo_done"))
        qk_ps, v_ps, sq_s, v_s, ms, mse_s, rr_s, qkn_s = (
            sem(n) for n in ("qk_ps", "v_ps", "sq_done", "v_done", "ms_done", "mse_done", "rr_done", "qkn_done"))
        turn_ps, qT_s, kT_s, sc_ps, max_s, exp_s, rinv_s, pn_s = (
            sem(n) for n in ("turn_ps", "qT_done", "kT_done", "sc_ps", "max_done", "exp_done", "rinv_done", "pn_done"))
        pT_ps, pT_hi_s, pT_lo_s, v_lo_s, o_ps, oT_hi_s, oT_s, out_ps, out_s = (
            sem(n) for n in ("pT_ps", "pT_hi_done", "pT_lo_done", "v_lo_done", "o_ps", "oT_hi_done", "oT_done",
                             "out_ps", "out_done"))

        def steps(eng, body):
            for n in range(ATT_PEEL):
                body(0, n)
            with eng.Fori(0, ATT_LOOPS) as i:
                for n in range(ATT_PEEL, ATT_PEEL + ATT_BODY):
                    body(i, n)
            for n in range(ATT_PEEL, NUA + 1 - ATT_LOOPS * ATT_BODY):
                body(ATT_LOOPS, n)

        Q, K, V, QT, KT, OUT = (bank(n) for n in (2, 3, 4, 5, 6, 7))
        OT = V
        FIRST = (bank(0), bank(1), None)

        def qk_banks(t):
            return sh.banks(0 if isinstance(t, int) and t == 1 else 2, 2)

        with nc.Block() as block:
            @block.sync
            def _(sp):
                sp.dma_start(raw[:, 0, :], d["w_pair"][0]).then_inc(raw_in[0], 16)
                sp.dma_start(gq[:, :], d["gq"]).then_inc(g_in, 16)
                sp.dma_start(gk[:, :], d["gk"]).then_inc(g_in, 16)
                sp.dma_start(raw[:, 1, :], d["w_pair"][1]).then_inc(raw_in[1], 16)
                for p in range(2, NPAIR):
                    sp.wait_ge(w_lo_s, p - 1)
                    sp.wait_ge(wo_lo_s, p - 1)
                    sp.dma_start(raw[:, p % 2, :], d["w_pair"][p]).then_inc(raw_in[p % 2], 16)

            @block.tensor
            def _(pe):
                norm_tensor(pe, sh, s)

                def project(n, parts, banks=(Q, K, V)):
                    slot, b = (n // B) % 2, n % B
                    for which in parts:
                        dst = banks[which]
                        base, ks = ((0, KD), (KD, 1), (KD + 1, 1))[which]
                        for tile in range(2):
                            tok = slice(b * L + tile * P, b * L + (tile + 1) * P)
                            for k in range(ks):
                                a = (sh.xT_hi[:, k, tok], sh.xT_lo[:, k, tok]) if which == 0 else (sh.c_hi[:, tok], sh.c_lo[:, tok])
                                w = slice((base + k) * HP * HD, (base + k + 1) * HP * HD)
                                mm = product3(pe, dst[:, tile * HP * HD:(tile + 1) * HP * HD], a,
                                              (w_hi[:, slot, w], w_lo[:, slot, w]), k == 0, k == ks - 1)
                    return mm

                def heads_turned(n):
                    for which, dst in enumerate((QT, KT)):
                        for hh in range(HP):
                            for tile in range(2):
                                mm = pe.transpose(dst[:, hh * L + tile * P:hh * L + (tile + 1) * P],
                                                  qkn[:, n % 2, ((which * 2 + tile) * HP + hh) * HD:((which * 2 + tile) * HP + hh + 1) * HD],
                                                  ident[:, :])
                    mm.then_inc(turn_ps, 1)

                def scores(t, n):
                    for hh in range(HP):
                        if not (isinstance(t, int) and t == 0):
                            pe.wait_ge(pT_lo_s, HP * t + (hh + 1 - HP))
                        for tile in range(2):
                            mm = pe.matmul(bank(hh)[:, tile * L:(tile + 1) * L],
                                           qT[:, n % 2, hh * L + tile * P:hh * L + (tile + 1) * P],
                                           kT[:, n % 2, hh * L:(hh + 1) * L], start=True, stop=True)
                        mm.then_inc(sc_ps, 1)

                def probabilities_turned(t, n):
                    for hh in range(HP):
                        pe.wait_ge(pn_s, HP * t + hh + 1)
                        for kt in range(2):
                            for tile in range(2):
                                mm = pe.transpose(bank(hh)[:, kt * L + tile * P:kt * L + (tile + 1) * P],
                                                  pn[:, n % 2, 2 * hh + tile, kt * P:(kt + 1) * P], ident[:, :])
                        mm.then_inc(pT_ps, 1)

                def values(n):
                    for hh in range(HP):
                        for kt in range(2):
                            f = slice((kt * HP + hh) * HD, (kt * HP + hh + 1) * HD)
                            tok = slice(kt * L, (kt + 1) * L)
                            mm = product3(pe, OT[:, hh * L:(hh + 1) * L], (v_hi[:, n % 4, f], v_lo[:, n % 4, f]),
                                          (pT_hi[:, n % 2, hh, tok], pT_lo[:, n % 2, hh, tok]), kt == 0, kt == 1)
                    mm.then_inc(o_ps, 1)

                def output(n):
                    slot = (n // B) % 2
                    for tile in range(2):
                        for hh in range(HP):
                            tok = slice(hh * L + tile * P, hh * L + (tile + 1) * P)
                            w = slice(hh * DM, (hh + 1) * DM)
                            mm = product3(pe, OUT[:, tile * DM:(tile + 1) * DM], (oT_hi[:, n % 2, tok], oT_lo[:, n % 2, tok]),
                                          (o_hi[:, slot, w], o_lo[:, slot, w]), hh == 0, hh == HP - 1)
                    mm.then_inc(out_ps, 1)

                def step(i, n):
                    t = i * ATT_BODY + n
                    static = isinstance(i, int)
                    ahead = not (static and t > NUA - 3)
                    end = static and t == NUA
                    before = not (static and t == 0)
                    if not end:
                        pe.wait_ge(qT_s, t + 1)
                        pe.wait_ge(kT_s, t + 1)
                        scores(t, n)
                    if before:
                        pe.wait_ge(v_lo_s, t)
                        pe.wait_ge(pT_lo_s, HP * t)
                        if not (static and t > NUA - 2):
                            pe.wait_ge(v_s, t + 2)
                        values(n - 1)
                    if not (static and t >= NUA - 1):
                        pe.wait_ge(qkn_s, t + 2)
                    if ahead:
                        if n % B == 2:
                            pe.wait_ge(w_lo_s, i * 2 + ((n + 2) // B + 1))
                        project(n + 2, (0, 1)).then_inc(qk_ps, 1)
                    if not (static and t >= NUA - 1):
                        heads_turned(n + 1)
                    if ahead:
                        if before:
                            pe.wait_ge(oT_s, t)
                        else:
                            pe.wait_ge(v_s, 2)
                        project(n + 2, (2,)).then_inc(v_ps, 1)
                    if not end:
                        probabilities_turned(t, n)
                    if before:
                        pe.wait_ge(oT_s, t)
                        if (n - 1) % B == 0:
                            pe.wait_ge(wo_lo_s, i * 2 + ((n - 1) // B + 1))
                        if not (static and t == 1):
                            pe.wait_ge(out_s, t - 1)
                        output(n - 1)

                pe.wait_ge(w_lo_s, 1)
                project(0, (1,))
                project(1, (1,), FIRST)
                pe.wait_ge(s.lo, 2 * KD)
                project(0, (0,)).then_inc(qk_ps, 1)
                project(1, (0,), FIRST).then_inc(qk_ps, 1)
                project(0, (2,)).then_inc(v_ps, 1)
                pe.wait_ge(v_s, 1)
                project(1, (2,)).then_inc(v_ps, 1)
                pe.wait_ge(qkn_s, 1)
                heads_turned(0)
                pe.wait_ge(qkn_s, 2)
                steps(pe, step)

            @block.scalar
            def _(act):
                act.wait_ge(raw_in[0], 16)
                act.activation(w_hi[:, 0, :], raw[:, 0, 0:QKV], ACT.Copy).then_inc(w_hi_s, 1)
                act.activation(o_hi[:, 0, :], raw[:, 0, QKV:WPAIR], ACT.Copy).then_inc(wo_hi_s, 1)
                norm_scalar(act, sh, s)

                def squares(t, n):
                    act.wait_ge(qk_ps, t + 1)
                    if not (isinstance(t, int) and t < 2):
                        act.wait_ge(ms, t - 1)
                    act.activation(sq[:, n % 2, :], qk_banks(t), ACT.Square, scale=HD ** -0.5).then_inc(sq_s, 1)

                def values_hi(t, n):
                    act.wait_ge(v_ps, t + 1)
                    if not (isinstance(t, int) and t < 4):
                        act.wait_ge(o_ps, t - 3)
                    act.activation(v_hi[:, n % 4, :], V, ACT.Copy)
                    if not (isinstance(t, int) and t < 2):
                        act.wait_ge(v_lo_s, t - 1)
                    act.activation(v[:, n % 2, :], V, ACT.Copy).then_inc(v_s, 1)

                def queries_turned(t, n):
                    act.wait_ge(turn_ps, t + 1)
                    if not (isinstance(t, int) and t < 2):
                        act.wait_ge(sc_ps, HP * (t - 1))
                    act.activation(qT[:, n % 2, :], QT, ACT.Copy).then_inc(qT_s, 1)

                def keys_turned(t, n):
                    act.activation(kT[:, n % 2, :], KT, ACT.Copy, scale=gg[:, :]).then_inc(kT_s, 1)

                def softmax(t, n, hh):
                    act.wait_ge(max_s, HP * t + hh + 1)
                    if not (isinstance(t, int) and t < 2):
                        act.wait_ge(pn_s, HP * (t - 2) + hh + 1)
                    for tile in range(2):
                        m = 2 * hh + tile
                        ins = act.activation(pe_[:, n % 2, m, :], bank(hh)[:, tile * L:(tile + 1) * L], ACT.Exp,
                                             bias=nmax[:, n % 2, m:m + 1], accum_out=rsum[:, n % 2, m:m + 1])
                    ins.then_inc(exp_s, 1)

                def probabilities(t, n):
                    if not (isinstance(t, int) and t < 2):
                        act.wait_ge(o_ps, t - 1)
                    for hh in range(HP):
                        act.wait_ge(pT_ps, HP * t + hh + 1)
                        act.activation(pT_hi[:, n % 2, hh, :], bank(hh), ACT.Copy).then_inc(pT_hi_s, 1)

                def values_out(t, n):
                    act.wait_ge(o_ps, t + 1)
                    if not (isinstance(t, int) and t < 2):
                        act.wait_ge(out_ps, t - 1)
                    act.activation(oT_hi[:, n % 2, :], OT, ACT.Copy).then_inc(oT_hi_s, 1)

                for t in range(2):
                    squares(t, t)
                for t in range(2):
                    values_hi(t, t)
                act.wait_ge(gg_ready, 1)
                queries_turned(0, 0)
                keys_turned(0, 0)

                def step(i, n):
                    t = i * ATT_BODY + n
                    static = isinstance(i, int)
                    end = static and t == NUA
                    if not end:
                        softmax(t, n, 0)
                    if not (static and t == 0):
                        values_out(t - 1, n - 1)
                    if not end:
                        softmax(t, n, 1)
                    if not (static and t > NUA - 3):
                        squares(t + 2, n + 2)
                    if not (static and t >= NUA - 1):
                        queries_turned(t + 1, n + 1)
                        keys_turned(t + 1, n + 1)
                    if not end:
                        probabilities(t, n)
                    if not (static and t > NUA - 3):
                        values_hi(t + 2, n + 2)
                    slot = (n // B + 1) % 2
                    if static and t > NUA - B - 1:
                        return
                    if n % B == 0:
                        act.wait_ge(raw_in[slot], i * 16 + ((n // B + 1) // 2 * 16 + 16))
                        if not (static and t < B):
                            act.wait_ge(qk_ps, t)
                            act.wait_ge(v_ps, t)
                        act.activation(w_hi[:, slot, :], raw[:, slot, 0:QKV], ACT.Copy).then_inc(w_hi_s, 1)
                    if n % B == 1:
                        if not (static and t < B):
                            act.wait_ge(out_ps, t - 1)
                        act.activation(o_hi[:, slot, :], raw[:, slot, QKV:WPAIR], ACT.Copy).then_inc(wo_hi_s, 1)

                steps(act, step)

            @block.gpsimd
            def _(pool):
                norm_deviation(pool, sh, s, 1)
                pool.wait_ge(w_hi_s, 1)
                pool.tensor_tensor(w_lo[:, 0, :], raw[:, 0, 0:QKV], w_hi[:, 0, :], ALU.subtract).then_inc(w_lo_s, 1)

                def weights_lo(count, slot):
                    pool.wait_ge(w_hi_s, count)
                    pool.tensor_tensor(w_lo[:, slot, :], raw[:, slot, 0:QKV], w_hi[:, slot, :], ALU.subtract).then_inc(w_lo_s, 1)

                def output_weights_lo(count, slot):
                    pool.wait_ge(wo_hi_s, count)
                    pool.tensor_tensor(o_lo[:, slot, :], raw[:, slot, QKV:WPAIR], o_hi[:, slot, :], ALU.subtract)\
                        .then_inc(wo_lo_s, 1)

                def values_lo(t, n):
                    pool.wait_ge(v_s, t + 1)
                    pool.tensor_tensor(v_lo[:, n % 4, :], v[:, n % 2, :], v_hi[:, n % 4, :], ALU.subtract).then_inc(v_lo_s, 1)

                def rms(t, n):
                    pool.wait_ge(ms, t + 1)
                    if not (isinstance(t, int) and t < 2):
                        pool.wait_ge(qkn_s, t - 1)
                    pool.tensor_tensor(rr[:, n % 2, :], ss[:, n % 2, :], sh.eps[:, :], ALU.add).then_inc(mse_s, 1)
                    pool.wait_ge(mse_s, t + 1)
                    pool.tensor_tensor(rr[:, n % 2, :], rr[:, n % 2, :], sh.mhalf[:, 0:8], ALU.pow).then_inc(rr_s, 1)

                for t in range(2):
                    rms(t, t)
                for t in range(2):
                    values_lo(t, t)
                output_weights_lo(1, 0)

                def step(i, n):
                    t = i * ATT_BODY + n
                    static = isinstance(i, int)
                    if static and t > NUA - 3:
                        return
                    rms(t + 2, n + 2)
                    values_lo(t + 2, n + 2)
                    slot = (n // B + 1) % 2
                    if n % B < 2 and not (static and t > NUA - B - 1):
                        (weights_lo, output_weights_lo)[n % B](i * 2 + (n // B + 2), slot)

                steps(pool, step)
                norm_deviation(pool, sh, after, 0)

            @block.vector
            def _(dve):
                norm_vector(dve, sh, s)
                norm_lo_vector(dve, sh, s)
                dve.wait_ge(g_in, 32)
                dve.scalar_tensor_tensor(gg[:, :], gq[:, :], HD ** -0.5, gk[:, :], ALU.mult, ALU.mult).then_inc(gg_ready, 1)

                def mean_squares(t, n):
                    if not (isinstance(t, int) and t < 2):
                        dve.wait_ge(rr_s, t - 1)
                    dve.wait_ge(sq_s, t + 1)
                    dve.tensor_reduce(ss[:, n % 2, :], sq[:, n % 2, :].rearrange("p (a f) -> p a f", f=HD), AX_X,
                                      ALU.add).then_inc(ms, 1)

                def normed(t, n):
                    dve.wait_ge(rr_s, t + 1)
                    if not (isinstance(t, int) and t < 2):
                        dve.wait_ge(turn_ps, t - 1)
                    dve.tensor_tensor(qkn[:, n % 2, :].rearrange("p (a f) -> p a f", f=HD),
                                      qk_banks(t).rearrange("p (a f) -> p a f", f=HD),
                                      rr[:, n % 2, :].unsqueeze(2).to_broadcast([P, 8, HD]), ALU.mult).then_inc(qkn_s, 1)

                def maxima(t, n, hh):
                    dve.wait_ge(sc_ps, HP * t + hh + 1)
                    dve.tensor_reduce(nmax[:, n % 2, 2 * hh:2 * hh + 2], bank(hh).rearrange("p (a k) -> p a k", k=L),
                                      AX_X, ALU.max, negate=True).then_inc(max_s, 1)

                def normalised(t, n, hh):
                    dve.wait_ge(exp_s, HP * t + hh + 1)
                    dve.reciprocal(rinv[:, n % 2, 2 * hh:2 * hh + 2], rsum[:, n % 2, 2 * hh:2 * hh + 2]).then_inc(rinv_s, 1)
                    dve.wait_ge(rinv_s, HP * t + hh + 1)
                    for m in range(2 * hh, 2 * hh + 2):
                        ins = dve.tensor_scalar(pn[:, n % 2, m, :], pe_[:, n % 2, m, :], rinv[:, n % 2, m:m + 1], None, ALU.mult)
                    ins.then_inc(pn_s, 1)

                def probabilities_lo(t, n):
                    for hh in range(HP):
                        dve.wait_ge(pT_hi_s, HP * t + hh + 1)
                        dve.tensor_tensor(pT_lo[:, n % 2, hh, :], bank(hh), pT_hi[:, n % 2, hh, :], ALU.subtract)\
                            .then_inc(pT_lo_s, 1)

                def values_out(t, n):
                    dve.wait_ge(oT_hi_s, t + 1)
                    dve.tensor_tensor(oT_lo[:, n % 2, :], OT, oT_hi[:, n % 2, :], ALU.subtract).then_inc(oT_s, 1)

                def residual(t, n):
                    b = n % B
                    dve.wait_ge(out_ps, t + 1)
                    xs = x[:, 2 * b:2 * b + 2, :].rearrange("p t f -> p (t f)")
                    dve.tensor_tensor(xs, xs, OUT, ALU.add).then_inc(out_s, 1)

                for t in range(2):
                    mean_squares(t, t)
                for t in range(2):
                    normed(t, t)

                def step(i, n):
                    t = i * ATT_BODY + n
                    static = isinstance(i, int)
                    end = static and t == NUA
                    if not end:
                        maxima(t, n, 0)
                    if not (static and (t == 0 or t > NUA - 2)):
                        normed(t + 1, n + 1)
                    if not end:
                        maxima(t, n, 1)
                        normalised(t, n, 0)
                    if not (static and t == 0):
                        values_out(t - 1, n - 1)
                    if not end:
                        normalised(t, n, 1)
                    if not (static and t < 2):
                        residual(t - 2, n - 2)
                    if end:
                        dve.wait_ge(out_s, NUA - 1)
                        norm_statistics(dve, sh, after, 0)
                    if not (static and t > NUA - 3):
                        mean_squares(t + 2, n + 2)
                    if not end:
                        probabilities_lo(t, n)
                    else:
                        residual(t - 1, n - 1)

                steps(dve, step)


ATT_BODY = 2 * B
ATT_PEEL = 4
ATT_LOOPS = 3


def build(nc, d, out, stages=4):
    with ExitStack() as ctx:
        sh = Shared()

        def sb(name, shape, dt=F32):
            return ctx.enter_context(nc.sbuf_tensor(name, shape, dt))

        psum = ctx.enter_context(nc.psum_tensor("psum", [P, 8, 512], F32))
        sh.bank = lambda n: psum[:, n, :]
        sh.banks = lambda n, k: psum[:, n:n + k, :].rearrange("p b n -> p (b n)")
        sh.x = sb("x", [P, NT, DM])
        sh.xn = sb("xn", [P, NT, DM])
        sh.ident = sb("ident", [P, P])
        sh.ctxT = sb("ctxT", [P, T])
        sh.c_hi = sb("c_hi", [P, T], F32R)
        sh.c_lo = sb("c_lo", [P, T], F32R)
        sh.mhalf = sb("mhalf", [P, 8])
        sh.eps = sb("eps", [P, 8])
        sh.zeros = sb("zeros", [P, HALF], BF16)
        sh.st = sb("st", [P, NT, 6])
        sh.mv = sb("mv", [P, NT, 2])
        sh.vare = sb("vare", [P, NT])
        sh.rstd = sb("rstd", [P, NT])

        norms = [NormSems(lambda name, n=n: ctx.enter_context(nc.semaphore(f"n{n}_{name}")), routed=(n != 1))
                 for n in range(3)]
        mixer_block(nc, sh, d, norms[0])
        sh.xT_hi = sb("xT_hi", [P, KD, T], F32R)
        sh.xT_lo = sb("xT_lo", [P, KD, T], F32R)
        if stages >= 2:
            moe_block(nc, sh, "f0", norms[0], norms[1], d["moe0"], d["route0"], d["scratch0"], 8, 704, 0, True, out if stages == 2 else None)
        if stages >= 3:
            attention_block(nc, sh, d, norms[1], norms[2])
        if stages >= 4:
            moe_block(nc, sh, "f1", norms[2], None, d["moe1"], d["route1"], d["scratch1"], 16, 352, 4, False, out)
        if stages in (1, 3):
            stored = ctx.enter_context(nc.semaphore("stored"))
            with nc.Block() as block:
                @block.sync
                def _(sp):
                    sp.dma_start(out.rearrange("(t p) f -> p t f", p=P), sh.x[:, :, :]).then_inc(stored, 16)
                    sp.wait_ge(stored, 16)


def layout(a):
    import numpy as np

    c = np.ascontiguousarray
    a = {k: np.asarray(v) for k, v in a.items()}

    def channels(v):
        return v.reshape(G, P, -1).transpose(1, 0, 2)

    def moe(gate, up, down, n):
        gate, up = (w.reshape(KD, P, n, P).transpose(2, 1, 0, 3) for w in (gate, up))
        down = down.reshape(n, P, DM)
        return c(np.concatenate([gate.reshape(n, P, -1), up.reshape(n, P, -1), down], axis=2))

    def wide(w, shared):
        return np.concatenate([np.pad(shared, ((0, 0), (0, -shared.shape[1] % P))),
                               w.transpose(1, 0, 2).reshape(DM, -1)], axis=1)

    def tall(w, shared):
        return np.concatenate([np.pad(shared, ((0, -shared.shape[0] % P), (0, 0))), w.reshape(-1, DM)], axis=0)

    m = "L0_xattn_"
    f = "L0_ffn_"
    q = "L1_xattn_"
    e = "L1_ffn_"
    out = {
        "ctxT": c(a["ctx_1024"].reshape(T, CD).T),
        "x": c(a["x"].reshape(T, DM)),
        "w_in": c(a[m + "in_proj_w"].T),
        "w_dt": c(np.concatenate([a[m + "dt_proj_w"].T, a[m + "dt_proj_b"][None, :]], axis=0)),
        "chan": c(channels(np.concatenate([
            a[m + "conv_w"], a[m + "conv_b"][:, None], a[m + "dt_proj_b"][:, None], a[m + "D"][:, None],
            a[m + "A_log"], a[m + "x_proj_w"].T], axis=1))),
        "ident": np.eye(P, dtype=np.float32),
        "moe0": moe(wide(a[f + "Wg"], a[f + "Sg"]), wide(a[f + "Wu"], a[f + "Su"]),
                    tall(a[f + "Wd"], a[f + "Sd"]), chunks_of(8, 704)),
        "route0": c(np.concatenate([a[f + "Wr"], a[f + "Wsg"]], axis=1).reshape(KD, P, -1).transpose(1, 0, 2)),
        "moe1": moe(wide(a[e + "W1"].transpose(0, 2, 1), a[e + "Ws1"].T), wide(a[e + "W3"].transpose(0, 2, 1), a[e + "Ws3"].T),
                    tall(a[e + "W2"].transpose(0, 2, 1), a[e + "Ws2"].T), chunks_of(16, 352)),
        "route1": c(a[e + "Wg"].T.reshape(KD, P, -1).transpose(1, 0, 2)),
        "gq": a[q + "gq"].reshape(HD, 1),
        "gk": a[q + "gk"].reshape(HD, 1),
    }
    pair = [a[q + "Wq"].reshape(KD, P, NPAIR, HP * HD).transpose(2, 1, 0, 3).reshape(NPAIR, P, -1),
            a[q + "Wk"].reshape(P, NPAIR, HP * HD).transpose(1, 0, 2),
            a[q + "Wv"].reshape(P, NPAIR, HP * HD).transpose(1, 0, 2),
            a[q + "Wo"].reshape(NPAIR, HP, HD, DM).transpose(0, 2, 1, 3).reshape(NPAIR, HD, -1)]
    out["w_pair"] = c(np.concatenate(pair, axis=2))
    sel = np.zeros((3, NBC, NBC, P), np.uint16)
    for r in range(NBC):
        sel[:, r, r, :] = 0x3F80
    out["sel"] = c(sel.reshape(3 * NBC, NBC, P))
    return out


def program(nc, arrays, stages=4):
    d = {name: nc.dram_tensor(f"in_{name}", v.shape, mybir.dt.from_np(v.dtype), kind="ExternalInput").ap()
         for name, v in arrays.items()}
    d["scratch0"] = nc.dram_tensor("scratch0", (8, T), F32).ap()
    d["scratch1"] = nc.dram_tensor("scratch1", (16, T), F32).ap()
    out = nc.dram_tensor("out", (T, DM), F32, kind="ExternalOutput").ap()
    build(nc, d, out, stages)


def kernel(**inputs):
    import concourse.bacc as bacc
    from concourse.bass_utils import run_bass_kernel_spmd

    arrays = layout(inputs)
    nc = bacc.Bacc("TRN2", target_bir_lowering=False, num_devices=1)
    program(nc, arrays)
    r = run_bass_kernel_spmd(nc, [{f"in_{k}": v for k, v in arrays.items()}], core_ids=[0])
    return r.results[0]["out"].reshape(B, L, DM)
```
